# Optimizing a Trainium2 kernel written in Bass

```python
import numpy as np
import jax
import jax.numpy as jnp

def _softmax(x, axis=-1):
    return jax.nn.softmax(x, axis=axis)

def _gelu(x):
    return jax.nn.gelu(x, approximate=True)

def _silu(x):
    return jax.nn.silu(x)

def _sigmoid(x):
    return jax.nn.sigmoid(x)

def _layernorm(x, axis=-1, eps=1e-05):
    m = jnp.mean(x, axis=axis, keepdims=True)
    v = jnp.var(x, axis=axis, keepdims=True)
    return (x - m) / jnp.sqrt(v + eps)

def _scatter_add(tgt, idx, src, axis=0):
    return tgt.at[idx].add(src)

def _segment_sum(src, seg, n):
    return jax.ops.segment_sum(src, seg, n)
kernel_name = 'mk_conv_preact_d4_conv_nchw384_r4_a704d7'

def setup_inputs(seed: int=0):
    np.random.seed(seed)
    _w = jnp.asarray

    def _rec_inputs():
        import jax
        import jax.numpy as jnp
        _gk = jax.random.key(seed)
        x = -0.0002221 + 1 * jax.random.normal(jax.random.fold_in(_gk, 1), (16, 96, 16, 16), jnp.float32)
        return x
    x = _rec_inputs()

    def _L0_conv_setup():
        import jax, jax.numpy as jnp
        import numpy as np
        DIM = 96
        WH, WW = (8, 8)
        NUM_HEADS = 12

        def _relative_position_index(wh, ww):
            coords = np.stack(np.meshgrid(np.arange(wh), np.arange(ww), indexing='ij'))
            cf = coords.reshape(2, -1)
            rel = cf[:, :, None] - cf[:, None, :]
            rel = rel.transpose(1, 2, 0)
            rel[:, :, 0] += wh - 1
            rel[:, :, 1] += ww - 1
            rel[:, :, 0] *= 2 * ww - 1
            return rel.sum(-1).astype(np.int32)
        key = jax.random.key(seed)
        ks = jax.random.split(key, 6)
        C = DIM
        x = jax.random.normal(ks[0], (16, C, 16, 16), dtype=jnp.float32)
        qkv_w = jax.random.normal(ks[1], (3 * C, C), dtype=jnp.float32) * 0.02
        qkv_b = jnp.zeros((3 * C,), dtype=jnp.float32)
        proj_w = jax.random.normal(ks[2], (C, C), dtype=jnp.float32) * 0.02
        proj_b = jnp.zeros((C,), dtype=jnp.float32)
        rpb_table = jax.random.normal(ks[3], ((2 * WH - 1) * (2 * WW - 1), NUM_HEADS), dtype=jnp.float32) * 0.02
        rel_index = jnp.asarray(_relative_position_index(WH, WW))
        return {'x': x, 'qkv_w': qkv_w, 'qkv_b': qkv_b, 'proj_w': proj_w, 'proj_b': proj_b, 'rpb_table': rpb_table, 'rel_index': rel_index}
    _L0_conv_all = _L0_conv_setup()
    _L0_conv_in = {k: v for k, v in _L0_conv_all.items() if k in ('qkv_w', 'qkv_b', 'proj_w', 'proj_b', 'rpb_table', 'rel_index')}
    del _L0_conv_all

    def _L1_conv_setup():
        import jax, jax.numpy as jnp
        import numpy as np
        WS = 8
        HEADS = 12
        HD = 32
        DISP = WS // 2
        SCALE = HD ** (-0.5)
        NEG = np.float32(float('-inf'))
        _pos = np.stack(np.meshgrid(np.arange(WS), np.arange(WS), indexing='ij'), -1).reshape(-1, 2)
        REL = jnp.asarray(_pos[:, None, :] - _pos[None, :, :] + WS - 1)
        _ud = np.zeros((WS * WS, WS * WS), np.float32)
        _ud[-DISP * WS:, :-DISP * WS] = NEG
        _ud[:-DISP * WS, -DISP * WS:] = NEG
        UD_MASK = jnp.asarray(_ud)
        _lr = np.zeros((WS, WS, WS, WS), np.float32)
        _lr[:, -DISP:, :, :-DISP] = NEG
        _lr[:, :-DISP, :, -DISP:] = NEG
        LR_MASK = jnp.asarray(_lr.reshape(WS * WS, WS * WS))
        key = jax.random.key(seed)
        k1, k2, k3, k4, k5 = jax.random.split(key, 5)
        B, C, H, W = (16, 96, 16, 16)
        inner = HEADS * HD
        return {'x': jax.random.normal(k1, (B, C, H, W), jnp.float32), 'w_qkv': jax.random.normal(k2, (C, inner * 3), jnp.float32) * C ** (-0.5), 'w_out': jax.random.normal(k3, (inner, C), jnp.float32) * inner ** (-0.5), 'b_out': jax.random.normal(k4, (C,), jnp.float32) * 0.01, 'pos_emb': jax.random.normal(k5, (2 * WS - 1, 2 * WS - 1), jnp.float32) * 0.02}
    _L1_conv_all = _L1_conv_setup()
    _L1_conv_in = {k: v for k, v in _L1_conv_all.items() if k in ('w_qkv', 'w_out', 'b_out', 'pos_emb')}
    del _L1_conv_all

    def _L2_conv_setup():
        import jax, jax.numpy as jnp
        import numpy as np
        from jax import lax
        EPS = 1e-05
        DN = ('NCHW', 'OIHW', 'NCHW')

        def _quant_global(w):
            scale = 1.0 / jnp.maximum(jnp.mean(jnp.abs(w)), EPS)
            u = jnp.clip(jnp.round(w * scale), -1.0, 1.0)
            return (u, scale)

        def _quant_per_channel_dw(w):
            m = jnp.mean(jnp.abs(w).reshape(w.shape[0], w.shape[1], -1), axis=2, keepdims=True)
            scale = 1.0 / jnp.maximum(m, EPS)[..., None]
            u = jnp.clip(jnp.round(w * scale), -1.0, 1.0)
            scale_bcast = jnp.transpose(scale, (1, 0, 2, 3))
            return (u, scale_bcast)

        def _ste(w_real, u):
            return w_real + lax.stop_gradient(u - w_real)
        key = jax.random.key(seed)
        k1, k2, k3 = jax.random.split(key, 3)
        x = jax.random.normal(k1, (16, 96, 56, 56), dtype=jnp.float32)
        w_dw = jax.random.normal(k2, (96, 1, 3, 3), dtype=jnp.float32) * 0.1
        w_pw = jax.random.normal(k3, (96, 96, 1, 1), dtype=jnp.float32) * 0.05
        return {'x': x, 'w_dw': w_dw, 'w_pw': w_pw}
    _L2_conv_all = _L2_conv_setup()
    _L2_conv_in = {k: v for k, v in _L2_conv_all.items() if k in ('w_dw', 'w_pw')}
    del _L2_conv_all

    def _L3_conv_setup():
        import jax, jax.numpy as jnp
        import numpy as np
        MIN_V, MAX_V, NORM = (0.0, 4.0, 4.0)
        NUM_HEADS = 8
        BN_EPS = 1e-05

        @jax.custom_vjp
        def quant(x):
            return jnp.round(jnp.clip(x, MIN_V, MAX_V))

        def _quant_fwd(x):
            return (jnp.round(jnp.clip(x, MIN_V, MAX_V)), x)

        def _quant_bwd(x, g):
            return (jnp.where((x < MIN_V) | (x > MAX_V), 0.0, g),)
        quant.defvjp(_quant_fwd, _quant_bwd)

        def spike(x):
            return quant(x) / NORM

        def conv_bn(x, w, gamma, beta, mean, var):
            y = jnp.einsum('oc,bchw->bohw', w, x)
            s = gamma / jnp.sqrt(var + BN_EPS)
            return y * s[None, :, None, None] + (beta - mean * s)[None, :, None, None]
        key = jax.random.key(seed)
        B, C, H, W = (8, 96, 16, 16)
        ks = jax.random.split(key, 21)
        d = {'x': jax.random.normal(ks[0], (B, C, H, W), jnp.float32)}
        i = 1
        for p in ('q', 'k', 'v', 'p'):
            d[f'{p}_w'] = jax.random.normal(ks[i], (C, C), jnp.float32) * 0.05
            i += 1
            d[f'{p}_gamma'] = jax.random.uniform(ks[i], (C,), jnp.float32, 0.5, 1.5)
            i += 1
            d[f'{p}_beta'] = jax.random.normal(ks[i], (C,), jnp.float32) * 0.1
            i += 1
            d[f'{p}_mean'] = jax.random.normal(ks[i], (C,), jnp.float32) * 0.1
            i += 1
            d[f'{p}_var'] = jax.random.uniform(ks[i], (C,), jnp.float32, 0.5, 1.5)
            i += 1
        return d
    _L3_conv_all = _L3_conv_setup()
    _L3_conv_in = {k: v for k, v in _L3_conv_all.items() if k in ('q_w', 'q_gamma', 'q_beta', 'q_mean', 'q_var', 'k_w', 'k_gamma', 'k_beta', 'k_mean', 'k_var', 'v_w', 'v_gamma', 'v_beta', 'v_mean', 'v_var', 'p_w', 'p_gamma', 'p_beta', 'p_mean', 'p_var')}
    del _L3_conv_all
    return {'x': x, 'L0_conv_qkv_w': _L0_conv_in['qkv_w'], 'L0_conv_qkv_b': _L0_conv_in['qkv_b'], 'L0_conv_proj_w': _L0_conv_in['proj_w'], 'L0_conv_proj_b': _L0_conv_in['proj_b'], 'L0_conv_rpb_table': _L0_conv_in['rpb_table'], 'L0_conv_rel_index': _L0_conv_in['rel_index'], 'L1_conv_w_qkv': _L1_conv_in['w_qkv'], 'L1_conv_w_out': _L1_conv_in['w_out'], 'L1_conv_b_out': _L1_conv_in['b_out'], 'L1_conv_pos_emb': _L1_conv_in['pos_emb'], 'L2_conv_w_dw': _L2_conv_in['w_dw'], 'L2_conv_w_pw': _L2_conv_in['w_pw'], 'L3_conv_q_w': _L3_conv_in['q_w'], 'L3_conv_q_gamma': _L3_conv_in['q_gamma'], 'L3_conv_q_beta': _L3_conv_in['q_beta'], 'L3_conv_q_mean': _L3_conv_in['q_mean'], 'L3_conv_q_var': _L3_conv_in['q_var'], 'L3_conv_k_w': _L3_conv_in['k_w'], 'L3_conv_k_gamma': _L3_conv_in['k_gamma'], 'L3_conv_k_beta': _L3_conv_in['k_beta'], 'L3_conv_k_mean': _L3_conv_in['k_mean'], 'L3_conv_k_var': _L3_conv_in['k_var'], 'L3_conv_v_w': _L3_conv_in['v_w'], 'L3_conv_v_gamma': _L3_conv_in['v_gamma'], 'L3_conv_v_beta': _L3_conv_in['v_beta'], 'L3_conv_v_mean': _L3_conv_in['v_mean'], 'L3_conv_v_var': _L3_conv_in['v_var'], 'L3_conv_p_w': _L3_conv_in['p_w'], 'L3_conv_p_gamma': _L3_conv_in['p_gamma'], 'L3_conv_p_beta': _L3_conv_in['p_beta'], 'L3_conv_p_mean': _L3_conv_in['p_mean'], 'L3_conv_p_var': _L3_conv_in['p_var']}

def reference(x, L0_conv_qkv_w, L0_conv_qkv_b, L0_conv_proj_w, L0_conv_proj_b, L0_conv_rpb_table, L0_conv_rel_index, L1_conv_w_qkv, L1_conv_w_out, L1_conv_b_out, L1_conv_pos_emb, L2_conv_w_dw, L2_conv_w_pw, L3_conv_q_w, L3_conv_q_gamma, L3_conv_q_beta, L3_conv_q_mean, L3_conv_q_var, L3_conv_k_w, L3_conv_k_gamma, L3_conv_k_beta, L3_conv_k_mean, L3_conv_k_var, L3_conv_v_w, L3_conv_v_gamma, L3_conv_v_beta, L3_conv_v_mean, L3_conv_v_var, L3_conv_p_w, L3_conv_p_gamma, L3_conv_p_beta, L3_conv_p_mean, L3_conv_p_var):
    import jax
    import jax.numpy as jnp

    def _L0_conv_ref(x, qkv_w, qkv_b, proj_w, proj_b, rpb_table, rel_index):
        import jax, jax.numpy as jnp
        import numpy as np
        DIM = 96
        WH, WW = (8, 8)
        NUM_HEADS = 12

        def _relative_position_index(wh, ww):
            coords = np.stack(np.meshgrid(np.arange(wh), np.arange(ww), indexing='ij'))
            cf = coords.reshape(2, -1)
            rel = cf[:, :, None] - cf[:, None, :]
            rel = rel.transpose(1, 2, 0)
            rel[:, :, 0] += wh - 1
            rel[:, :, 1] += ww - 1
            rel[:, :, 0] *= 2 * ww - 1
            return rel.sum(-1).astype(np.int32)
        B, C, H, W = x.shape
        nh, hd = (NUM_HEADS, C // NUM_HEADS)
        N = WH * WW
        scale = hd ** (-0.5)
        xw = jnp.transpose(x, (0, 2, 3, 1))
        xw = xw.reshape(B, H // WH, WH, W // WW, WW, C)
        xw = jnp.transpose(xw, (0, 1, 3, 2, 4, 5)).reshape(-1, N, C)
        B_ = xw.shape[0]
        qkv = xw @ qkv_w.T + qkv_b
        qkv = qkv.reshape(B_, N, 3, nh, hd)
        qkv = jnp.transpose(qkv, (2, 0, 3, 1, 4))
        q, k, v = (qkv[0], qkv[1], qkv[2])
        attn = jnp.einsum('bhnd,bhmd->bhnm', q * scale, k)
        bias = rpb_table[rel_index.reshape(-1)].reshape(N, N, nh)
        bias = jnp.transpose(bias, (2, 0, 1))
        attn = jax.nn.softmax(attn + bias[None], axis=-1)
        out = jnp.einsum('bhnm,bhmd->bhnd', attn, v)
        out = jnp.transpose(out, (0, 2, 1, 3)).reshape(B_, N, C)
        out = out @ proj_w.T + proj_b
        out = out.reshape(B, H // WH, W // WW, WH, WW, C)
        out = jnp.transpose(out, (0, 1, 3, 2, 4, 5)).reshape(B, H, W, C)
        return jnp.transpose(out, (0, 3, 1, 2))

    def _L1_conv_ref(x, w_qkv, w_out, b_out, pos_emb):
        import jax, jax.numpy as jnp
        import numpy as np
        WS = 8
        HEADS = 12
        HD = 32
        DISP = WS // 2
        SCALE = HD ** (-0.5)
        NEG = np.float32(float('-inf'))
        _pos = np.stack(np.meshgrid(np.arange(WS), np.arange(WS), indexing='ij'), -1).reshape(-1, 2)
        REL = jnp.asarray(_pos[:, None, :] - _pos[None, :, :] + WS - 1)
        _ud = np.zeros((WS * WS, WS * WS), np.float32)
        _ud[-DISP * WS:, :-DISP * WS] = NEG
        _ud[:-DISP * WS, -DISP * WS:] = NEG
        UD_MASK = jnp.asarray(_ud)
        _lr = np.zeros((WS, WS, WS, WS), np.float32)
        _lr[:, -DISP:, :, :-DISP] = NEG
        _lr[:, :-DISP, :, -DISP:] = NEG
        LR_MASK = jnp.asarray(_lr.reshape(WS * WS, WS * WS))
        b, c, h, w = x.shape
        nw_h, nw_w = (h // WS, w // WS)
        xs = jnp.roll(x, shift=(-DISP, -DISP), axis=(2, 3))
        xs = jnp.transpose(xs, (0, 2, 3, 1))
        qkv = xs @ w_qkv
        q, k, v = jnp.split(qkv, 3, axis=-1)

        def to_windows(t):
            t = t.reshape(b, nw_h, WS, nw_w, WS, HEADS, HD)
            return jnp.transpose(t, (0, 5, 1, 3, 2, 4, 6)).reshape(b, HEADS, nw_h * nw_w, WS * WS, HD)
        q, k, v = map(to_windows, (q, k, v))
        dots = jnp.einsum('bhwid,bhwjd->bhwij', q, k) * SCALE
        dots = dots + pos_emb[REL[..., 0], REL[..., 1]]
        dots = dots.at[:, :, -nw_w:].add(UD_MASK)
        dots = dots.at[:, :, nw_w - 1::nw_w].add(LR_MASK)
        attn = jax.nn.softmax(dots, axis=-1)
        out = jnp.einsum('bhwij,bhwjd->bhwid', attn, v)
        out = out.reshape(b, HEADS, nw_h, nw_w, WS, WS, HD)
        out = jnp.transpose(out, (0, 2, 4, 3, 5, 1, 6)).reshape(b, h, w, HEADS * HD)
        out = out @ w_out + b_out
        out = jnp.transpose(out, (0, 3, 1, 2))
        return jnp.roll(out, shift=(DISP, DISP), axis=(2, 3))

    def _L2_conv_ref(x, w_dw, w_pw):
        import jax, jax.numpy as jnp
        import numpy as np
        from jax import lax
        EPS = 1e-05
        DN = ('NCHW', 'OIHW', 'NCHW')

        def _quant_global(w):
            scale = 1.0 / jnp.maximum(jnp.mean(jnp.abs(w)), EPS)
            u = jnp.clip(jnp.round(w * scale), -1.0, 1.0)
            return (u, scale)

        def _quant_per_channel_dw(w):
            m = jnp.mean(jnp.abs(w).reshape(w.shape[0], w.shape[1], -1), axis=2, keepdims=True)
            scale = 1.0 / jnp.maximum(m, EPS)[..., None]
            u = jnp.clip(jnp.round(w * scale), -1.0, 1.0)
            scale_bcast = jnp.transpose(scale, (1, 0, 2, 3))
            return (u, scale_bcast)

        def _ste(w_real, u):
            return w_real + lax.stop_gradient(u - w_real)
        C = x.shape[1]
        u_dw, s_dw = _quant_per_channel_dw(w_dw)
        y = lax.conv_general_dilated(x, _ste(w_dw, u_dw), window_strides=(1, 1), padding=((1, 1), (1, 1)), dimension_numbers=DN, feature_group_count=C)
        y = y / s_dw
        u_pw, s_pw = _quant_global(w_pw)
        y = lax.conv_general_dilated(y, _ste(w_pw, u_pw), window_strides=(1, 1), padding=((0, 0), (0, 0)), dimension_numbers=DN)
        y = y / s_pw
        return y

    def _L3_conv_ref(x, q_w, q_gamma, q_beta, q_mean, q_var, k_w, k_gamma, k_beta, k_mean, k_var, v_w, v_gamma, v_beta, v_mean, v_var, p_w, p_gamma, p_beta, p_mean, p_var):
        import jax, jax.numpy as jnp
        import numpy as np
        MIN_V, MAX_V, NORM = (0.0, 4.0, 4.0)
        NUM_HEADS = 8
        BN_EPS = 1e-05

        @jax.custom_vjp
        def quant(x):
            return jnp.round(jnp.clip(x, MIN_V, MAX_V))

        def _quant_fwd(x):
            return (jnp.round(jnp.clip(x, MIN_V, MAX_V)), x)

        def _quant_bwd(x, g):
            return (jnp.where((x < MIN_V) | (x > MAX_V), 0.0, g),)
        quant.defvjp(_quant_fwd, _quant_bwd)

        def spike(x):
            return quant(x) / NORM

        def conv_bn(x, w, gamma, beta, mean, var):
            y = jnp.einsum('oc,bchw->bohw', w, x)
            s = gamma / jnp.sqrt(var + BN_EPS)
            return y * s[None, :, None, None] + (beta - mean * s)[None, :, None, None]
        B, C, H, W = x.shape
        N = H * W
        hd = C // NUM_HEADS
        scale = hd ** (-0.5)
        xs = spike(x)
        q = spike(conv_bn(xs, q_w, q_gamma, q_beta, q_mean, q_var))
        k = spike(conv_bn(xs, k_w, k_gamma, k_beta, k_mean, k_var))
        v = spike(conv_bn(xs, v_w, v_gamma, v_beta, v_mean, v_var))

        def to_heads(t):
            return t.reshape(B, NUM_HEADS, hd, N).transpose(0, 1, 3, 2)
        q, k, v = (to_heads(q), to_heads(k), to_heads(v))
        kv = jnp.einsum('bhnd,bhne->bhde', k, v)
        attn = jnp.einsum('bhnd,bhde->bhne', q, kv) * (scale * 2)
        a = attn.transpose(0, 1, 3, 2).reshape(B, C, N)
        a = spike(a).reshape(B, C, H, W)
        out = conv_bn(a, p_w, p_gamma, p_beta, p_mean, p_var)
        return out

    def _gn(v, G=32, eps=1e-05):
        B_, C_, H_, W_ = v.shape
        g = v.reshape(B_, G, C_ // G, H_, W_)
        m = jnp.mean(g, axis=(2, 3, 4), keepdims=True)
        s = jnp.var(g, axis=(2, 3, 4), keepdims=True)
        return ((g - m) / jnp.sqrt(s + eps)).reshape(v.shape)

    def _ln_c(v, eps=1e-06):
        m = jnp.mean(v, axis=1, keepdims=True)
        s = jnp.var(v, axis=1, keepdims=True)
        return (v - m) / jnp.sqrt(s + eps)

    def _ln_t(v, eps=1e-05):
        m = jnp.mean(v, axis=-1, keepdims=True)
        s = jnp.var(v, axis=-1, keepdims=True)
        return (v - m) / jnp.sqrt(s + eps)

    def _to_tokens(v):
        B_, C_, H_, W_ = v.shape
        return v.reshape(B_, C_, H_ * W_).transpose(0, 2, 1)

    def _from_tokens(t, like):
        B_, C_, H_, W_ = like.shape
        return t.transpose(0, 2, 1).reshape(B_, C_, H_, W_)
    x = x + _L0_conv_ref(_gn(x), L0_conv_qkv_w, L0_conv_qkv_b, L0_conv_proj_w, L0_conv_proj_b, L0_conv_rpb_table, L0_conv_rel_index)
    x = x + _L1_conv_ref(_gn(x), L1_conv_w_qkv, L1_conv_w_out, L1_conv_b_out, L1_conv_pos_emb)
    x = x + _L2_conv_ref(_gn(x), L2_conv_w_dw, L2_conv_w_pw)
    x = x + _L3_conv_ref(_gn(x), L3_conv_q_w, L3_conv_q_gamma, L3_conv_q_beta, L3_conv_q_mean, L3_conv_q_var, L3_conv_k_w, L3_conv_k_gamma, L3_conv_k_beta, L3_conv_k_mean, L3_conv_k_var, L3_conv_v_w, L3_conv_v_gamma, L3_conv_v_beta, L3_conv_v_mean, L3_conv_v_var, L3_conv_p_w, L3_conv_p_gamma, L3_conv_p_beta, L3_conv_p_mean, L3_conv_p_var)
    return x

_drawn_inputs = setup_inputs


def setup_inputs(seed=0):
    import zlib

    import numpy as np

    out = dict(_drawn_inputs(seed))
    spreads = {'L0_conv_qkv_b': (0.0, 0.417), 'L0_conv_proj_b': (0.0, 0.1)}
    factors = {'L0_conv_qkv_w': 8.0,
     'L0_conv_rpb_table': 31.32,
     'L1_conv_b_out': 6.395,
     'L1_conv_pos_emb': 8.0,
     'L3_conv_p_var': 144.69,
     'L3_conv_p_gamma': 12.122}
    for name, (base, spread) in spreads.items():
        noise = np.random.default_rng([zlib.crc32(name.encode()), seed]).standard_normal(out[name].shape)
        drawn = base * np.exp(spread * noise) if base else spread * noise
        out[name] = jnp.asarray(drawn.astype(out[name].dtype))
    for name, factor in factors.items():
        out[name] = (out[name] * factor).astype(out[name].dtype)
    return out
```

```python
from contextlib import ExitStack

import numpy as np

import concourse.bass as bass
from concourse import mybir

F32 = mybir.dt.float32
BF16 = mybir.dt.bfloat16
I32 = mybir.dt.int32
ALU = mybir.AluOpType
ACT = mybir.ActivationFunctionType
AX = mybir.AxisListType

B, C, SIDE = 16, 96, 16
T = SIDE * SIDE
WIN, WT, NW = 8, 64, 4
HEADS, NP, NU, NH = 12, 3, 2, 2
GROUP = 3
EPS = 1e-5
NEG = -1e30
ROUND = 12582912.0
REL = (2 * WIN - 1) ** 2
BIAS_KEYS = 13
REL_LO = 113
HD0, HD1 = C // HEADS, 32
D0 = HD0 + 1
INNER = HEADS * HD1

CONSTS = {}
_at = 0
for _name, _n in (("ident", 128), ("qmask0", 4), ("qmask1", 2), ("group_mean", C), ("ones", 128),
                  ("head_blocks", C), ("masks", 4 * WT), ("rows", 2), ("minus_half", 1), ("perm", 4 * 128)):
    CONSTS[_name] = (_at, _at + _n)
    _at += _n
N_CONST = _at


def constants():
    c = np.zeros((128, N_CONST), np.float32)
    p = np.arange(128)

    def put(name, value, rows=128):
        a, b = CONSTS[name]
        c[:rows, a:b] = value

    put("ident", np.eye(128))
    put("qmask0", (p[:, None] % 32 // HD0 == np.arange(4)) * np.float32(HD0 ** -0.5))
    put("qmask1", (p[:, None] // HD1 % 2 == np.arange(2)) * np.float32(HD1 ** -0.5))
    ch = np.arange(C)
    put("group_mean", (ch[:, None] // GROUP == ch[None] // GROUP) / np.float32(GROUP * T), C)
    put("ones", 1.0)
    put("head_blocks", ch[:, None] // 12 == ch[None] // 12, C)
    tok = np.arange(WT)
    r, q = tok // WIN >= WIN // 2, tok % WIN >= WIN // 2
    ud, lr = r[:, None] != r[None], q[:, None] != q[None]
    m = np.zeros((2, WT, NW, WT), bool)
    for w in range(NW):
        m[:, :, w] |= (ud & (w // 2 == 1)) | (lr & (w % 2 == 1))
    put("masks", m.reshape(128, NW * WT) * np.float32(NEG))
    perm = np.zeros((WT, NW, NH, WT))
    for w in range(NW):
        src = (tok // WIN + w // 2 * 4) % WIN * WIN + (tok % WIN + w % 2 * 4) % WIN
        perm[WT - 1 - src, w, :, tok] = 1
    put("perm", perm.reshape(WT, NW * 128), WT)
    put("minus_half", -0.5)
    put("rows", np.stack([p, p + REL_LO], 1))
    return c


class Attention:

    def __init__(self, n, hd):
        self.n, self.hd = n, hd
        self.o_cols = NU * NH * (hd + 1)
        self.wide = hd == HD1
        self.ot_parts = 2 if self.wide else 1
        self.ot_rows = C if self.wide else NP * NU * hd
        self.row_groups = 2 if self.wide else 3
        self.qk_uses = 3 if self.wide else 2
        self.v_uses = NW if self.wide else 1
        self.pieces = 6 if self.wide else 4
        self.uses_at = [(0, 2), (2, 4), (4, 6), (6, 7)] if self.wide else [(0, 2), (2, 3), (3, 3), (3, 3)]


class AttentionSems:

    def __init__(self, sem, n):
        self.xn_ready = sem(f"l{n}_xn_ready")
        self.qk_ready = sem(f"l{n}_qk_ready")
        self.v_ready = sem(f"l{n}_v_ready")
        self.evac_a = sem(f"l{n}_evac_a")
        self.evac_b = sem(f"l{n}_evac_b")
        self.rows = sem(f"l{n}_rows")
        self.scores_ready = sem(f"l{n}_scores_ready")
        self.biased = sem(f"l{n}_biased")
        self.maxed = sem(f"l{n}_maxed")
        self.shifted = sem(f"l{n}_shifted")
        self.exped = sem(f"l{n}_exped")
        self.transposed = sem(f"l{n}_transposed")
        self.probsT_sb = sem(f"l{n}_probsT_sb")
        self.pv_done = sem(f"l{n}_pv_done")
        self.summed = sem(f"l{n}_summed")
        self.normed = sem(f"l{n}_normed")
        self.ot_done = sem(f"l{n}_ot_done")
        self.ot_sb = sem(f"l{n}_ot_sb")
        self.out_ready = sem(f"l{n}_out_ready")
        self.residual = sem(f"l{n}_residual")


def build(nc, a, out):
    ctx = ExitStack()
    with ctx:
        ctx.enter_context(nc.allow_non_contiguous_dma(reason="small weights and tables, loaded once"))

        def sb(name, shape, dt=F32):
            return ctx.enter_context(nc.sbuf_tensor(name, shape, dt))

        def sem(name):
            return ctx.enter_context(nc.semaphore(name))

        bank = [ctx.enter_context(nc.psum_tensor(f"bank{i}", [128, 512], F32)) for i in range(8)]
        ps_scores = bank[0:2]
        ps_probsT = bank[2:4]
        ps_heads = bank[4]
        ps_qkv = bank[5:7]
        ps_mix = bank[7]

        x = sb("x", [C, B * T])
        cst = sb("cst", [128, N_CONST])

        def const(name, rows=128):
            lo, hi = CONSTS[name]
            return cst[0:rows, lo:hi]

        ident = const("ident")
        ones = const("ones")
        w0_raw = sb("w0_raw", [C, 3, C])
        w0T = sb("w0T", [C, 3 * C])
        b0_qk = sb("b0_qk", [C, 2])
        b0_q4 = sb("b0_q4", [C, 4])
        b0_v = sb("b0_v", [128, NW * C // 2])
        p0_raw = sb("p0_raw", [C, C])
        p0T = sb("p0T", [NP * NU * HD0, NH, C])
        p0_b = sb("p0_b", [C, 1])
        rel_bc = sb("rel_bc", [REL_LO, WT * WT], I32)
        onehot = sb("onehot", [REL_LO, 2, WT * WT], BF16)
        table = sb("table", [REL_LO, 2, HEADS])
        table_rest = sb("table_rest", [REL_LO, 2, 2, HEADS])
        table_parts = sb("table_parts", [REL_LO, 2, 3, HEADS], BF16)
        bias0 = sb("bias0", [128, NP * NU, WT])
        w1 = sb("w1", [C, 3 * INNER])
        p1 = sb("p1", [C, NH, 2, C])
        p1_b = sb("p1_b", [C, 1])
        pos = sb("pos", [WT, WT])
        bias1 = sb("bias1", [128, NW, WT])
        dw = sb("dw", [C, 9])
        dw_u = sb("dw_u", [C, 9])
        pw_raw = sb("pw_raw", [C, C])
        pw_u = sb("pw_u", [C, C])
        pw_abs = sb("pw_abs", [C, 1])
        pwT = sb("pwT", [C, C])
        q_mean = sb("q_mean", [C, 4])
        w3_raw = sb("w3_raw", [C, 4, C])
        w3_rest = sb("w3_rest", [C, 2, 4 * C])
        w3_parts = sb("w3_parts", [C, 3, 4 * C], BF16)
        bn = sb("bn", [C, 4, 4])
        bn_r = sb("bn_r", [C, 4])
        bn_s = sb("bn_s", [C, 4])
        bn_s4 = sb("bn_s4", [C, 4])
        bn_t = sb("bn_t", [C, 4])
        bn_b = sb("bn_b", [C, 4])
        ident_b = sb("ident_b", [C, C], BF16)
        stats = sb("stats", [C, 6 * B])
        gn_sq = sb("gn_sq", [C, 2 * B])
        gn_sum = sb("gn_sum", [C, 2 * B])
        gn_shift = sb("gn_shift", [C, B])
        gn_in = sb("gn_in", [C, 2 * B])
        gn_m2 = sb("gn_m2", [C, B])
        gn_var = sb("gn_var", [C, B])
        gn_negmean = sb("gn_negmean", [C, B])
        gn_mean = sb("gn_mean", [C, B])
        gn_veps = sb("gn_veps", [C, B])
        gn_rstd = sb("gn_rstd", [C, B])

        xn = [sb(f"xn{i}", [C, NW, WT]) for i in range(2)]
        q0 = [sb(f"q0_{i}", [C, NW, 4, WT]) for i in range(2)]
        k0 = [sb(f"k0_{i}", [C, T]) for i in range(2)]
        v0 = [sb(f"v0_{i}", [128, NW * NP, NU, NH, D0]) for i in range(2)]
        q1 = [sb(f"q1_{i}", [128, 3, NW, 2, WT]) for i in range(2)]
        k1 = [sb(f"k1_{i}", [128, 3, T]) for i in range(2)]
        v1 = [sb(f"v1_{i}", [128, NW * NP, NU, NH, HD1 + 1]) for i in range(2)]
        probs = [sb(f"probs{i}", [128, NP * NU, WT]) for i in range(4)]
        row_max = [sb(f"row_max{i}", [128, NP * NU]) for i in range(4)]
        probsT = [sb(f"probsT{i}", [128, NP * 128]) for i in range(2)]
        inv_sum = [sb(f"inv_sum{i}", [128, HEADS]) for i in range(2)]
        heads = [sb(f"heads{i}", [128, NP * NU, HD1]) for i in range(2)]
        headsT = [sb(f"headsT{i}", [C, NW, 2, 128]) for i in range(2)]
        pad = [sb(f"pad{i}", [C, SIDE + 2, 2, SIDE + 2]) for i in range(2)]
        conv = [sb(f"conv{i}", [C, 2 * SIDE, SIDE]) for i in range(2)]
        xn3 = sb("xn3", [C, 2 * T])
        spike_in = [sb(f"spike_in{i}", [C, 2 * T], BF16) for i in range(2)]
        relu3 = [sb(f"relu3_{i}", [C, 3, 2 * T]) for i in range(2)]
        qkv3 = [sb(f"qkv3_{i}", [C, 3, 2 * T], BF16) for i in range(2)]
        relu_a = sb("relu_a", [C, 2 * T])
        rounded_a = sb("rounded_a", [C, 2 * T])
        rounded = sb("rounded", [C, 2 * T])
        kvT = sb("kvT", [128, 2, 4, C], BF16)
        kv = sb("kv", [C, 2, C])
        kv_lo = sb("kv_lo", [C, 2, C])
        kv_parts = sb("kv_parts", [C, 2, 2, C], BF16)
        spike_a = sb("spike_a", [C, 2 * T], BF16)
        y3 = sb("y3", [C, 2 * T])
        y_out = [sb(f"y_out{i}", [C, 2 * T]) for i in range(2)]

        x_in = sem("x_in")
        w_in = sem("w_in")
        bias_in = sem("bias_in")
        dve_prep = sem("dve_prep")
        pe_prep = sem("pe_prep")
        pool_prep = sem("pool_prep")
        stat = sem("stat")
        gn_pe = sem("gn_pe")
        gn_eps = sem("gn_eps")
        gn_done = sem("gn_done")

        L0, L1 = Attention(0, HD0), Attention(1, HD1)
        L0.s, L1.s = AttentionSems(sem, 0), AttentionSems(sem, 1)
        N_X = 4
        BIAS_IN = 16 * (1 + WIN)

        def wait(eng, s, v):
            if not (isinstance(v, int) and v <= 0):
                eng.wait_ge(s, v)

        def x_of(s, n=1):
            return x[:, bass.ds(s * T, n * T)]

        def image(ap):
            return ap.rearrange("c (y x) -> c y x", x=SIDE)

        def by_window(ap):
            return ap.rearrange("c (w t) -> c w t", w=NW)

        def window_pieces(L, w):
            wy, wx = w // 2, w % 2
            half = WIN // 2
            if not L.wide:
                y, xx = wy * WIN, wx * WIN
                return [(lambda i: i[:, y:y + WIN, xx:xx + WIN], lambda t: t)]

            def cols(i):
                return i.rearrange("c y (b x) -> c y b x", x=half)[:, :, 0:4:3] if wx else \
                    i[:, :, half:half + WIN].rearrange("c y (b x) -> c y b x", x=half)

            def tok(t):
                return t.rearrange("c y (b x) -> c y b x", x=half)

            if not wy:
                return [(lambda i: cols(i[:, half:half + WIN]), tok)]
            return [(lambda i, k=k: cols(i[:, k * 3 * half:(k * 3 + 1) * half]),
                     lambda t, k=k: tok(t[:, k * half:(k + 1) * half])) for k in range(2)]

        marks = {}

        block = ctx.enter_context(nc.Block())

        loads = []

        @block.sync
        def _(sp):
            n = B // N_X
            for i in range(N_X):
                sp.dma_start(x[:, i * n * T:(i + 1) * n * T].rearrange("c (b t) -> c b t", t=T),
                             a["x"][i * n:(i + 1) * n].rearrange("b c h w -> c b (h w)")).then_inc(x_in, 16)
            sp.dma_start(rel_bc[:, :], a["L0_conv_rel_index"].rearrange("q k -> (q k)").unsqueeze(0)
                         .broadcast_to([REL_LO, WT * WT])).then_inc(bias_in, 16)
            flipped = a["L1_conv_pos_emb"]
            for i in range(WIN):
                src = bass.AP(tensor=flipped.tensor, offset=flipped.offset + i * (2 * WIN - 1),
                              ap=[[1, WIN], [2 * WIN - 1, WIN], [1, WIN]])
                sp.dma_start(pos[i * WIN:(i + 1) * WIN, :].rearrange("q (y x) -> q y x", x=WIN), src).then_inc(bias_in, 16)

        def weight_loads():
            yield cst[:, :], a["consts"]
            yield w0_raw[:, :, :], a["L0_conv_qkv_w"].rearrange("(t o) i -> o t i", o=C)
            yield table[:, 0, :], a["L0_conv_rpb_table"][0:REL_LO]
            yield table[0:REL - REL_LO, 1, :], a["L0_conv_rpb_table"][REL_LO:REL]
            yield b0_qk[:, :], a["L0_conv_qkv_b"].rearrange("(t o) -> o t", o=C)[:, 0:2]
            bv = a["L0_conv_qkv_b"][2 * C:3 * C].rearrange("(p u e) -> u p e", p=NP, u=NU)
            for w in range(NW):
                for u in range(NU):
                    yield (b0_v[u * WT:(u + 1) * WT, w * C // 2:(w + 1) * C // 2].rearrange("k (p e) -> k p e", p=NP),
                           bv[u].unsqueeze(0).broadcast_to([WT, NP, NH * HD0]))
            for h in range(NH):
                yield (p0_raw[:, h * C // 2:(h + 1) * C // 2].rearrange("o (g d) -> o g d", d=HD0),
                       a["L0_conv_proj_w"].rearrange("o (g h d) -> o h g d", h=NH, d=HD0)[:, h])
            yield p0_b[:, :], a["L0_conv_proj_b"].unsqueeze(1)
            yield w1[:, :], a["L1_conv_w_qkv"]
            rows = a["L1_conv_w_out"].rearrange("(f g h d) c -> h f g d c", f=2, g=3, h=NH)
            for h in range(NH):
                for f in range(2):
                    for g in range(3):
                        yield p1[g * HD1:(g + 1) * HD1, h, f, :], rows[h, f, g]
            yield p1_b[:, :], a["L1_conv_b_out"].unsqueeze(1)
            yield dw[:, :], a["L2_conv_w_dw"].rearrange("c a y x -> c (a y x)")
            yield pw_raw[:, :], a["L2_conv_w_pw"].rearrange("o i y x -> o (i y x)")
            for j, name in enumerate("qkvp"):
                yield w3_raw[:, j, :], a[f"L3_conv_{name}_w"]
                for i, what in enumerate(("gamma", "beta", "mean", "var")):
                    yield bn[:, i, j:j + 1], a[f"L3_conv_{name}_{what}"].unsqueeze(1)

        loads = list(weight_loads())
        W_IN = 16 * len(loads)

        @block.scalar
        def _(act):
            for dst, src in loads:
                act.dma_start(dst, src).then_inc(w_in, 16)

        PE_W0, PE_P0, PE_BIAS, PE_POS, PE_PW_SUM, PE_PW, PE_W3 = range(1, 8)
        done = {}

        def dve_prepare(dve):
            count = [0]

            def step(ins):
                count[0] += 1
                ins.then_inc(dve_prep, 1)
                dve.wait_ge(dve_prep, count[0])

            dve.wait_ge(w_in, W_IN)
            for t, n in ((0, REL_LO), (1, REL - REL_LO)):
                step(nc.vector.tensor_copy(table_parts[0:n, t, 0, :], table[0:n, t, :]))
                step(nc.vector.tensor_tensor(table_rest[0:n, 0, t, :], table[0:n, t, :], table_parts[0:n, t, 0, :], ALU.subtract))
                step(nc.vector.tensor_copy(table_parts[0:n, t, 1, :], table_rest[0:n, 0, t, :]))
                step(nc.vector.tensor_tensor(table_rest[0:n, 1, t, :], table_rest[0:n, 0, t, :], table_parts[0:n, t, 1, :], ALU.subtract))
                step(nc.vector.tensor_copy(table_parts[0:n, t, 2, :], table_rest[0:n, 1, t, :]))
            dve.wait_ge(bias_in, BIAS_IN)
            lo = CONSTS["rows"][0]
            for t in range(2):
                step(nc.vector.tensor_scalar(onehot[:, t, :], rel_bc[:, :], cst[0:REL_LO, lo + t:lo + t + 1], None,
                                             ALU.is_equal))
            done["onehot"] = count[0]
            for v, hd in [(v, HD0) for v in v0] + [(v, HD1) for v in v1]:
                step(nc.vector.memset(v[:, :, :, :, :], 0.0))
                for u in range(NU):
                    step(nc.vector.memset(v[u * WT:(u + 1) * WT, :, u, :, hd:hd + 1], 1.0))
            for h in heads:
                step(nc.vector.memset(h[:, :, :], 0.0))
            dve.wait_ge(pe_prep, PE_W0)
            step(nc.vector.tensor_copy(w0T[:, :], bank[0][0:C, 0:3 * C]))
            dve.wait_ge(pe_prep, PE_P0)
            step(nc.vector.tensor_copy(p0T[:, :, :], bank[1][0:NP * NU * HD0, 0:NH * C].rearrange("p (h c) -> p h c", h=NH)))
            step(nc.vector.tensor_scalar(b0_q4[:, :], const("qmask0", C), b0_qk[:, 0:1], None, ALU.mult))
            dve.wait_ge(pe_prep, PE_BIAS)
            for k0_ in range(0, WT, BIAS_KEYS):
                n = min(BIAS_KEYS, WT - k0_)
                for h in range(NH):
                    src = bank[2 + k0_ // BIAS_KEYS][0:WT, 0:n * 3 * HEADS] \
                        .rearrange("q (k part g h) -> q h g k part", k=n, part=3, h=NH)[:, h]
                    step(nc.vector.tensor_reduce(bias0[h * WT:(h + 1) * WT, :, k0_:k0_ + n], src, AX.X, ALU.add))
            dve.wait_ge(pe_prep, PE_POS)
            step(nc.vector.tensor_tensor(bias1[:, :, :], ps_mix[:, 0:NW * WT].rearrange("p (w k) -> p w k", w=NW),
                                         const("masks").rearrange("p (w k) -> p w k", w=NW), ALU.add))
            done["layer0"] = count[0]

        def dve_prepare_late(dve):
            count = [done["layer0"]]

            def step(ins):
                count[0] += 1
                ins.then_inc(dve_prep, 1)
                dve.wait_ge(dve_prep, count[0])

            step(nc.vector.tensor_reduce(q_mean[:, 0:1], dw[:, :], AX.X, ALU.add, apply_absolute_value=True))
            step(nc.vector.tensor_scalar(q_mean[:, 0:1], q_mean[:, 0:1], 1.0 / 9, 1e-5, ALU.mult, ALU.max))
            step(nc.vector.reciprocal(q_mean[:, 1:2], q_mean[:, 0:1]))
            step(nc.vector.tensor_scalar(dw_u[:, :], dw[:, :], q_mean[:, 1:2], ROUND, ALU.mult, ALU.add))
            step(nc.vector.tensor_scalar(dw_u[:, :], dw_u[:, :], ROUND, 1.0, ALU.subtract, ALU.min))
            step(nc.vector.tensor_scalar(dw_u[:, :], dw_u[:, :], -1.0, None, ALU.max))
            step(nc.vector.tensor_tensor(dw_u[:, :], dw_u[:, :], dw[:, :], ALU.subtract))
            step(nc.vector.tensor_tensor(dw_u[:, :], dw_u[:, :], dw[:, :], ALU.add))
            step(nc.vector.tensor_scalar(dw_u[:, :], dw_u[:, :], q_mean[:, 0:1], None, ALU.mult))
            step(nc.vector.tensor_reduce(pw_abs[:, :], pw_raw[:, :], AX.X, ALU.add, apply_absolute_value=True))
            done["pw_abs"] = count[0]
            dve.wait_ge(pe_prep, PE_PW_SUM)
            step(nc.vector.tensor_scalar(q_mean[:, 2:3], bank[6][0:C, 0:1], 1.0 / (C * C), 1e-5, ALU.mult, ALU.max))
            step(nc.vector.reciprocal(q_mean[:, 3:4], q_mean[:, 2:3]))
            step(nc.vector.tensor_scalar(pw_u[:, :], pw_raw[:, :], q_mean[:, 3:4], ROUND, ALU.mult, ALU.add))
            step(nc.vector.tensor_scalar(pw_u[:, :], pw_u[:, :], ROUND, 1.0, ALU.subtract, ALU.min))
            step(nc.vector.tensor_scalar(pw_u[:, :], pw_u[:, :], -1.0, None, ALU.max))
            step(nc.vector.tensor_tensor(pw_u[:, :], pw_u[:, :], pw_raw[:, :], ALU.subtract))
            step(nc.vector.tensor_tensor(pw_u[:, :], pw_u[:, :], pw_raw[:, :], ALU.add))
            step(nc.vector.tensor_scalar(pw_u[:, :], pw_u[:, :], q_mean[:, 2:3], None, ALU.mult))
            done["pw_u"] = count[0]
            dve.wait_ge(pe_prep, PE_PW)
            step(nc.vector.tensor_copy(pwT[:, :], bank[6][0:C, 0:C]))
            dve.wait_ge(pe_prep, PE_W3)
            w3 = bank[7][0:C, 0:4 * C]
            step(nc.vector.tensor_copy(w3_parts[:, 0, :], w3))
            step(nc.vector.tensor_tensor(w3_rest[:, 0, :], w3, w3_parts[:, 0, :], ALU.subtract))
            step(nc.vector.tensor_copy(w3_parts[:, 1, :], w3_rest[:, 0, :]))
            step(nc.vector.tensor_tensor(w3_rest[:, 1, :], w3_rest[:, 0, :], w3_parts[:, 1, :], ALU.subtract))
            step(nc.vector.tensor_copy(w3_parts[:, 2, :], w3_rest[:, 1, :]))
            step(nc.vector.tensor_copy(ident_b[:, :], cst[0:C, 0:C]))
            dve.wait_ge(pool_prep, 2)
            step(nc.vector.tensor_tensor(bn_s[:, :], bn_r[:, :], bn[:, 0, :], ALU.mult))
            step(nc.vector.tensor_scalar(bn_s4[:, :], bn_s[:, :], 0.25, None, ALU.mult))
            step(nc.vector.tensor_tensor(bn_t[:, :], bn_s[:, :], bn[:, 2, :], ALU.mult))
            step(nc.vector.tensor_tensor(bn_b[:, :], bn[:, 1, :], bn_t[:, :], ALU.subtract))
            for i in range(2):
                step(nc.vector.memset(pad[i][:, :, :, :], 0.0))
            done["late"] = count[0]

        def pe_prepare(pe):
            pe.wait_ge(w_in, W_IN)
            for t in range(3):
                last = nc.tensor.transpose(bank[0][0:C, t * C:(t + 1) * C], w0_raw[:, t, :], ident[0:C, 0:C])
            last.then_inc(pe_prep, 1)
            for h in range(NH):
                cols = p0_raw[:, h * C // 2:(h + 1) * C // 2]
                last = nc.tensor.transpose(bank[1][0:NP * NU * HD0, h * C:(h + 1) * C], cols, ident[0:C, 0:C])
            last.then_inc(pe_prep, 1)
            pe.wait_ge(dve_prep, done["onehot"])
            for k in range(WT):
                for t, n in ((0, REL_LO), (1, REL - REL_LO)):
                    sel = onehot[0:n, t, :].rearrange("r (q k) -> r q k", k=WT)[:, :, k]
                    last = nc.tensor.matmul(
                        bank[2 + k // BIAS_KEYS][0:WT, k % BIAS_KEYS * 3 * HEADS:(k % BIAS_KEYS + 1) * 3 * HEADS],
                        sel, table_parts[0:n, t, :, :], start=(t == 0), stop=(t == 1))
            last.then_inc(pe_prep, 1)
            pe.wait_ge(bias_in, BIAS_IN)
            for w in range(NW):
                for yb in range(2):
                    for xb in range(2):
                        def block44(ap, i, j):
                            return ap.rearrange("q (yb y xb x) -> q yb y xb x", yb=2, xb=2, y=4)[:, i, :, j, :]
                        last = nc.tensor.matmul(block44(ps_mix[:, w * WT:(w + 1) * WT], yb, xb),
                                                const("perm", WT)[:, w * 128:(w + 1) * 128],
                                                block44(pos[:, :], yb ^ (w // 2), xb ^ (w % 2)), start=True, stop=True)
            last.then_inc(pe_prep, 1)

        def pe_prepare_late(pe):
            pe.wait_ge(dve_prep, done["pw_abs"])
            nc.tensor.matmul(bank[6][0:C, 0:1], ones[0:C, 0:C], pw_abs[:, :], start=True, stop=True).then_inc(pe_prep, 1)
            pe.wait_ge(dve_prep, done["pw_u"])
            nc.tensor.transpose(bank[6][0:C, 0:C], pw_u[:, :], ident[0:C, 0:C]).then_inc(pe_prep, 1)
            for j in range(4):
                last = nc.tensor.transpose(bank[7][0:C, j * C:(j + 1) * C], w3_raw[:, j, :], ident[0:C, 0:C])
            last.then_inc(pe_prep, 1)

        STEPS = 8
        HALF = T // 2

        def stat_base(layer):
            return layer * (B + STEPS)

        def dve_stats(dve, layer, s, n=1):
            for j in range(n):
                nc.vector.bn_stats(stats[:, bass.ds((s + j) * 6, 6)], x_of(s + j)).then_inc(stat, 1)

        def dve_group_norm(dve, layer):
            n = [stat_base(layer) + B]

            def step(ins):
                n[0] += 1
                ins.then_inc(stat, 1)
                dve.wait_ge(stat, n[0])

            dve.wait_ge(stat, n[0])
            mean, m2 = (stats[:, :].rearrange("c (n k) -> c k n", k=3)[:, k, :] for k in (1, 2))
            sides = stats[:, :].rearrange("c (b e k) -> c e k b", e=2, k=3)
            step(nc.vector.tensor_tensor(gn_in[:, 0:B], sides[:, 0, 1, :], sides[:, 1, 1, :], ALU.add))
            step(nc.vector.tensor_tensor(gn_sq[:, :], mean, mean, ALU.mult))
            step(nc.vector.scalar_tensor_tensor(gn_sum[:, :], gn_sq[:, :], float(HALF), m2, ALU.mult, ALU.add))
            both = gn_sum[:, :].rearrange("c (b e) -> c e b", e=2)
            step(nc.vector.tensor_tensor(gn_in[:, B:2 * B], both[:, 0, :], both[:, 1, :], ALU.add))
            dve.wait_ge(gn_pe, layer + 1)
            step(nc.vector.tensor_scalar(gn_mean[:, :], ps_mix[0:C, 0:B], float(HALF), None, ALU.mult))
            step(nc.vector.tensor_scalar(gn_negmean[:, :], gn_mean[:, :], -1.0, None, ALU.mult))
            step(nc.vector.tensor_tensor(gn_m2[:, :], gn_mean[:, :], gn_mean[:, :], ALU.mult))
            step(nc.vector.tensor_tensor(gn_var[:, :], ps_mix[0:C, B:2 * B], gn_m2[:, :], ALU.subtract))

        def pool_group_norm(pool, layer):
            pool.wait_ge(stat, stat_base(layer) + B + STEPS)
            nc.gpsimd.tensor_scalar(gn_veps[:, :], gn_var[:, :], EPS, None, ALU.add).then_inc(gn_eps, 1)
            pool.wait_ge(gn_eps, layer + 1)
            nc.gpsimd.tensor_tensor(gn_rstd[:, :], gn_veps[:, :], const("minus_half", C).broadcast_to([C, B]),
                                    ALU.pow).then_inc(gn_done, 1)
            pool.wait_ge(gn_done, 2 * layer + 1)
            nc.gpsimd.tensor_tensor(gn_shift[:, :], gn_negmean[:, :], gn_rstd[:, :], ALU.mult).then_inc(gn_done, 1)

        def pe_group_norm(pe, layer):
            pe.wait_ge(stat, stat_base(layer) + B + 4)
            nc.tensor.matmul(ps_mix[0:C, 0:2 * B], const("group_mean", C), gn_in[:, :], start=True, stop=True).then_inc(gn_pe, 1)

        def qkv_plan(L):
            if L.wide:
                return [("qk", 0, "act", 3), ("qk", 1, "dve", 3), ("qk", 2, "act", 3),
                        ("v", 0, "dve", 2), ("v", 1, "act", 2), ("v", 2, "dve", 2), ("v", 3, "act", 2)]
            return [("q", 0, "act", 4), ("k", 0, "dve", 1), ("v", 0, "dve", 2)]

        def bank_of(L, parity, i):
            plan = qkv_plan(L)
            b = (i + parity * len(plan)) % 2
            before = sum(plan[j][3] for j in range(i) if (j + parity * len(plan)) % 2 == b)
            return b, before

        def evacs(L, parity):
            plan = qkv_plan(L)
            tot = [0, 0]
            for i, use in enumerate(plan):
                tot[(i + parity * len(plan)) % 2] += use[3]
            return tot

        def evac_before(L, s, parity, b):
            both = evacs(L, 0)[b] + evacs(L, 1)[b]
            if isinstance(s, int):
                return s // 2 * both + (evacs(L, 0)[b] if s % 2 else 0)
            return s.pair * both + (evacs(L, 0)[b] if parity else 0)

        class Sample:

            def __init__(self, pair, parity):
                self.pair, self.parity = pair, parity

            def __add__(self, n):
                return self.pair * 2 + (self.parity + n)

            __radd__ = __add__

            def __mul__(self, n):
                return self.pair * (2 * n) + self.parity * n

            __rmul__ = __mul__

            def shift(self, n):
                return Sample(self.pair + (self.parity + n) // 2, (self.parity + n) % 2)

        def moved(s, n):
            return s + n if isinstance(s, int) else s.shift(n)

        def parity(s):
            return s % 2 if isinstance(s, int) else s.parity

        def win_count(s, w):
            return s * NW + (w + 1)

        def evac_sem(L, par, i):
            return (L.s.evac_a, L.s.evac_b)[bank_of(L, par, i)[0]]

        def evacuated(eng, L, s, i):
            par = parity(s)
            b, before = bank_of(L, par, i)
            eng.wait_ge(evac_sem(L, par, i), evac_before(L, s, par, b) + before + qkv_plan(L)[i][3])

        def pe_qkv(pe, L, s, i0, i1):
            par = parity(s)
            if i0 == 0:
                pe.wait_ge(L.s.xn_ready, s * L.pieces + L.pieces)
            for i in range(i0, i1):
                kind, j, _, _ = qkv_plan(L)[i]
                b, before = bank_of(L, par, i)
                wait(pe, evac_sem(L, par, i), evac_before(L, s, par, b) + before)
                o = ps_qkv[b]
                if kind != "v":
                    m = 128 if L.wide else C
                    w = w1 if L.wide else w0T
                    for half in {"q": (0,), "k": (1,), "qk": (0, 1)}[kind]:
                        col = half * (INNER if L.wide else C) + j * 128
                        last = nc.tensor.matmul(o[0:m, half * T:(half + 1) * T], w[:, col:col + m], xn[par][:, :, :],
                                                start=True, stop=True)
                    last.then_inc(L.s.qk_ready, 1)
                    continue
                for k in (range(NW) if not L.wide else (j,)):
                    for u in range(NU):
                        wv = (w1 if L.wide else w0T)[:, 2 * HEADS * L.hd:3 * HEADS * L.hd] \
                            .rearrange("c (p u e) -> c u p e", p=NP, u=NU)[:, u]
                        n = HEADS * L.hd // 2
                        at_ = 0 if L.wide else k * n
                        last = nc.tensor.matmul(o[u * WT:(u + 1) * WT, at_:at_ + n], xn[par][:, k, :], wv,
                                                start=True, stop=True)
                last.then_inc(L.s.v_ready, 1)

        def pe_scores(pe, L, s, w, r):
            if r == 0:
                if w == 0:
                    for i in range(L.qk_uses):
                        evacuated(pe, L, s, i)
                wait(pe, L.s.biased, win_count(s, w - 2))
            else:
                pe.wait_ge(L.s.rows, win_count(s, w - 1) * (L.row_groups - 1) + r)
            par = parity(s)
            for g in range(NP * NU):
                if (g % 2 if L.wide else g // 2) != r:
                    continue
                if L.wide:
                    rows = slice(g % 2 * 64, g % 2 * 64 + 64)
                    q = q1[par][rows, g // 2, w, :, :]
                    k = k1[par][rows, g // 2, w * WT:(w + 1) * WT]
                else:
                    rows = slice(g // 2 * 32, g // 2 * 32 + 32)
                    q = q0[par][rows, w, g % 2 * 2:g % 2 * 2 + 2, :]
                    k = k0[par][rows, w * WT:(w + 1) * WT]
                last = nc.tensor.matmul(ps_scores[w % 2][:, g * WT:(g + 1) * WT], q, k, start=True, stop=True)
            last.then_inc(L.s.scores_ready if r == L.row_groups - 1 else L.s.rows, 1)

        def pe_transpose(pe, L, s, w):
            pe.wait_ge(L.s.exped, win_count(s, w))
            wait(pe, L.s.probsT_sb, win_count(s, w - 2))
            for p in range(NP):
                last = nc.tensor.transpose(ps_probsT[w % 2][:, p * 128:(p + 1) * 128], probs[w][:, 2 * p:2 * p + 2, :], ident)
            last.then_inc(L.s.transposed, 1)

        def pe_values(pe, L, s, w):
            pe.wait_ge(L.s.probsT_sb, win_count(s, w))
            wait(pe, L.s.normed, 2 * win_count(s, w - 1))
            v = (v1 if L.wide else v0)[parity(s)]
            if L.wide or w == 0:
                evacuated(pe, L, s, L.qk_uses + w)
            for p in range(NP):
                last = nc.tensor.matmul(ps_heads[:, p * L.o_cols:(p + 1) * L.o_cols], probsT[w % 2][:, p * 128:(p + 1) * 128],
                                        v[:, w * NP + p, :, :, :], start=True, stop=True)
            last.then_inc(L.s.pv_done, 1)

        def pe_heads_transpose(pe, L, s, w, has_prev):
            pe.wait_ge(L.s.normed, 2 * win_count(s, w))
            wait(pe, L.s.ot_sb, win_count(s, w - 1))
            if w == 1 and has_prev:
                pe.wait_ge(L.s.residual, s * 1)
            for f in range(L.ot_parts):
                hv = heads[w % 2][:, :, :].rearrange("p g d -> p (g d)")[:, f * C:(f + 1) * C]
                last = nc.tensor.transpose(ps_mix[0:C, f * 128:(f + 1) * 128], hv, ident)
            last.then_inc(L.s.ot_done, 1)

        def pe_out(pe, L, s, last_sample=False):
            pe.wait_ge(L.s.ot_sb, win_count(s, NW - 1 if last_sample else NW))
            n = L.ot_rows
            o = image(ps_mix[0:C, 256:512])
            for w in range(NW):
                for of_image, of_tokens in window_pieces(L, w):
                    k = 0
                    for h in range(NH):
                        for f in range(L.ot_parts):
                            tokens = headsT[parity(s)][0:n, w, f, h * WT:(h + 1) * WT].rearrange("p (y x) -> p y x", x=WIN)
                            wt = p1[:, h, f, :] if L.wide else p0T[:, h, :]
                            last = nc.tensor.matmul(of_image(o), wt, of_tokens(tokens),
                                                    start=(k == 0), stop=(k == NH * L.ot_parts - 1))
                            k += 1
            last.then_inc(L.s.out_ready, 1)

        def act_exp(act, L, s, w):
            act.wait_ge(L.s.shifted, win_count(s, w))
            nc.scalar.activation(probs[w][:, :, :], probs[w][:, :, :], ACT.Exp).then_inc(L.s.exped, 1)

        def act_probsT(act, L, s, w):
            act.wait_ge(L.s.transposed, win_count(s, w))
            wait(act, L.s.pv_done, win_count(s, w - 2))
            nc.scalar.copy(probsT[w % 2][:, :], ps_probsT[w % 2][:, 0:NP * 128]).then_inc(L.s.probsT_sb, 1)

        def act_headsT(act, L, s, w):
            act.wait_ge(L.s.ot_done, win_count(s, w))
            if w == 0:
                wait(act, L.s.out_ready, s * 1 - 1)
            n, f = L.ot_rows, L.ot_parts
            nc.scalar.copy(headsT[parity(s)][0:n, w, 0:f, :],
                           ps_mix[0:n, 0:f * 128].rearrange("p (f t) -> p f t", f=f)).then_inc(L.s.ot_sb, 1)

        def evac_q(eng, L, s, i, j, slot):
            par = parity(s)
            b, _ = bank_of(L, par, i)
            if L.wide:
                src, dst = by_window(ps_qkv[b][:, 0:T]), q1[par][:, j, :, slot, :]
                lo = CONSTS["qmask1"][0] + slot
                scale = cst[:, lo:lo + 1]
                if eng == "act":
                    return nc.scalar.activation(dst, src, ACT.Copy, scale=scale)
                return nc.vector.tensor_scalar(dst, src, scale, None, ALU.mult)
            src, dst = by_window(ps_qkv[b][0:C, 0:T]), q0[par][:, :, slot, :]
            lo = CONSTS["qmask0"][0] + slot
            scale, bias = cst[0:C, lo:lo + 1], b0_q4[:, slot:slot + 1]
            if eng == "act":
                return nc.scalar.activation(dst, src, ACT.Identity, scale=scale, bias=bias)
            return nc.vector.tensor_scalar(dst, src, scale, bias, ALU.mult, ALU.add)

        def evac_k(eng, L, s, i, j):
            par = parity(s)
            b, _ = bank_of(L, par, i)
            if L.wide:
                src, dst = ps_qkv[b][:, T:2 * T], k1[par][:, j, :]
                return nc.scalar.copy(dst, src) if eng == "act" else nc.vector.tensor_copy(dst, src)
            src, dst = ps_qkv[b][0:C, T:2 * T], k0[par][:, :]
            if eng == "act":
                return nc.scalar.activation(dst, src, ACT.Identity, bias=b0_qk[:, 1:2])
            return nc.vector.tensor_scalar(dst, src, b0_qk[:, 1:2], None, ALU.add)

        def evac_v(eng, L, s, i, w, u):
            par = parity(s)
            b, _ = bank_of(L, par, i)
            rows = slice(u * WT, (u + 1) * WT)
            if L.wide:
                src = ps_qkv[b][rows, 0:INNER // 2].rearrange("k (p h d) -> k p h d", p=NP, h=NH)
                dst = v1[par][rows, w * NP:(w + 1) * NP, u, :, 0:HD1]
                return nc.scalar.copy(dst, src) if eng == "act" else nc.vector.tensor_copy(dst, src)
            src = ps_qkv[b][rows, 0:NW * C // 2].rearrange("k (w h d) -> k w h d", h=NH, d=HD0)
            bias = b0_v[rows, :].rearrange("k (w h d) -> k w h d", h=NH, d=HD0)
            return nc.vector.tensor_tensor(v0[par][rows, :, u, :, 0:HD0], src, bias, ALU.add)

        def evacuate(eng, who, L, s, i0, i1):
            for i in range(i0, i1):
                kind, j, engine, _ = qkv_plan(L)[i]
                if engine != who:
                    continue
                if kind == "v":
                    eng.wait_ge(L.s.v_ready, s * L.v_uses + (j + 1))
                    wait(eng, L.s.pv_done, s * NW - NW)
                    todo = [lambda u=u: evac_v(who, L, s, i, j, u) for u in range(NU)]
                else:
                    eng.wait_ge(L.s.qk_ready, s * L.qk_uses + (i + 1))
                    wait(eng, L.s.scores_ready, s * NW - NW)
                    todo = []
                    if kind != "k":
                        todo += [lambda h=h: evac_q(who, L, s, i, j, h) for h in range(2 if L.wide else 4)]
                    if kind != "q":
                        todo += [lambda: evac_k(who, L, s, i, j)]
                for one in todo:
                    one().then_inc(evac_sem(L, parity(s), i), 1)

        def dve_scores(dve, L, s, w):
            dve.wait_ge(L.s.scores_ready, win_count(s, w))
            wait(dve, L.s.transposed, win_count(s, w - 4))
            if L.wide:
                b = bias1[:, w, :].unsqueeze(1).broadcast_to([128, NP * NU, WT])
            else:
                b = bias0[:, :, :]
            nc.vector.tensor_tensor(probs[w][:, :, :], ps_scores[w % 2][:, 0:NP * NU * WT].rearrange("p (g k) -> p g k", k=WT),
                                    b, ALU.add).then_inc(L.s.biased, 1)
            dve.wait_ge(L.s.biased, win_count(s, w))
            nc.vector.tensor_reduce(row_max[w][:, :], probs[w][:, :, :], AX.X, ALU.max).then_inc(L.s.maxed, 1)

        def dve_normalise(dve, L, s, w):
            dve.wait_ge(L.s.pv_done, win_count(s, w))
            wait(dve, L.s.ot_done, win_count(s, w - 2))
            o = ps_heads[:, 0:NP * L.o_cols].rearrange("p (g e) -> p g e", e=L.hd + 1)
            nc.vector.reciprocal(inv_sum[w % 2][:, :], o[:, :, L.hd]).then_inc(L.s.summed, 1)
            dve.wait_ge(L.s.summed, win_count(s, w))
            hv = heads[w % 2][:, :, :].rearrange("p g d -> p (g d)")[:, 0:NP * NU * L.hd].rearrange("p (g d) -> p g d", d=L.hd)
            for h in range(NH):
                rows = slice(h * WT, (h + 1) * WT)
                oh = o[rows].rearrange("p (g h) e -> p h g e", h=NH)[:, h, :, 0:L.hd]
                r = inv_sum[w % 2][rows, :].rearrange("p (g h) -> p h g", h=NH)[:, h, :].unsqueeze(2) \
                    .broadcast_to([WT, NP * NU, L.hd])
                nc.vector.tensor_tensor(hv[rows], oh, r, ALU.mult).then_inc(L.s.normed, 1)

        def dve_residual(dve, L, s):
            dve.wait_ge(L.s.out_ready, s + 1)
            o = ps_mix[0:C, 256:512]
            b = p1_b if L.wide else p0_b
            nc.vector.scalar_tensor_tensor(x_of(s), o, b[:, 0:1], x_of(s), ALU.add, ALU.add).then_inc(L.s.residual, 1)
            dve.wait_ge(L.s.residual, s + 1)
            dve_stats(dve, L.n + 1, s)

        def dve_norm(dve, L, s):
            wait(dve, L.s.v_ready, s * L.v_uses - L.v_uses)
            for w in range(NW):
                for of_image, of_tokens in window_pieces(L, w):
                    tokens = xn[parity(s)][:, w, :].rearrange("c (y x) -> c y x", x=WIN)
                    nc.vector.tensor_scalar(of_tokens(tokens), of_image(image(x_of(s))), gn_mean[:, bass.ds(s * 1, 1)],
                                            gn_rstd[:, bass.ds(s * 1, 1)], ALU.subtract, ALU.mult).then_inc(L.s.xn_ready, 1)

        def pool_shift(pool, L, s, w):
            pool.wait_ge(L.s.maxed, win_count(s, w))
            nc.gpsimd.tensor_tensor(probs[w][:, :, :], probs[w][:, :, :],
                                    row_max[w][:, :].unsqueeze(2).broadcast_to([128, NP * NU, WT]),
                                    ALU.subtract).then_inc(L.s.shifted, 1)

        def at(s, w):
            return moved(s, w // NW), w % NW

        def pe_sample(pe, L, s, prev, nxt, nxt2):
            for w in range(NW):
                if nxt:
                    pe_qkv(pe, L, moved(s, 1), *L.uses_at[w])
                ahead = w < 2 or nxt
                if ahead:
                    pe_scores(pe, L, *at(s, w + 2), 0)
                pe_transpose(pe, L, s, w)
                if ahead:
                    pe_scores(pe, L, *at(s, w + 2), 1)
                if w >= 1 or prev:
                    pe_values(pe, L, *at(s, w - 1))
                if ahead and not L.wide:
                    pe_scores(pe, L, *at(s, w + 2), 2)
                if w >= 2 or prev:
                    pe_heads_transpose(pe, L, *at(s, w - 2), prev)
                if w == 2 and prev:
                    pe_out(pe, L, moved(s, -1))

        def act_sample(act, L, s, prev, nxt, nxt2):
            for w in range(NW):
                if w < 3 or nxt:
                    act_exp(act, L, *at(s, w + 1))
                act_probsT(act, L, s, w)
                if nxt:
                    evacuate(act, "act", L, moved(s, 1), *L.uses_at[w])
                if w >= 2 or prev:
                    act_headsT(act, L, *at(s, w - 2))

        def dve_sample(dve, L, s, prev, nxt, nxt2):
            for w in range(NW):
                if w < 3 or nxt:
                    dve_scores(dve, L, *at(s, w + 1))
                if w >= 1 or prev:
                    dve_normalise(dve, L, *at(s, w - 1))
                if nxt:
                    evacuate(dve, "dve", L, moved(s, 1), *L.uses_at[w])
                if w == 2 and prev:
                    dve_residual(dve, L, moved(s, -1))
                if w == 3 and nxt2:
                    dve_norm(dve, L, moved(s, 2))

        def pool_sample(pool, L, s, prev, nxt, nxt2):
            for w in range(NW):
                if w < 3 or nxt:
                    pool_shift(pool, L, *at(s, w + 1))

        def attention_loop(eng, L, body):
            body(eng, L, 0, False, True, True)
            with eng.Fori(0, B // 2 - 2) as i:
                body(eng, L, Sample(i, 1), True, True, True)
                body(eng, L, Sample(i + 1, 0), True, True, True)
            body(eng, L, B - 3, True, True, True)
            body(eng, L, B - 2, True, True, False)
            body(eng, L, B - 1, True, False, False)

        def pe_attention(pe, L):
            pe_group_norm(pe, L.n)
            for w in range(NW):
                pe_qkv(pe, L, 0, *L.uses_at[w])
            for w in range(2):
                for r in range(L.row_groups):
                    pe_scores(pe, L, 0, w, r)
            attention_loop(pe, L, pe_sample)
            pe_values(pe, L, B - 1, 3)
            pe_heads_transpose(pe, L, B - 1, 2, True)
            pe_heads_transpose(pe, L, B - 1, 3, True)
            pe_out(pe, L, B - 1, True)

        def act_attention(act, L):
            for w in range(NW):
                evacuate(act, "act", L, 0, *L.uses_at[w])
            act_exp(act, L, 0, 0)
            attention_loop(act, L, act_sample)
            act_headsT(act, L, B - 1, 2)
            act_headsT(act, L, B - 1, 3)

        def dve_attention(dve, L):
            dve_group_norm(dve, L.n)
            dve.wait_ge(gn_done, 2 * L.n + 1)
            dve_norm(dve, L, 0)
            dve_norm(dve, L, 1)
            for w in range(NW):
                evacuate(dve, "dve", L, 0, *L.uses_at[w])
            dve_scores(dve, L, 0, 0)
            attention_loop(dve, L, dve_sample)
            dve_normalise(dve, L, B - 1, 3)
            dve_residual(dve, L, B - 1)

        def pool_attention(pool, L):
            pool_group_norm(pool, L.n)
            pool_shift(pool, L, 0, 0)
            attention_loop(pool, L, pool_sample)

        PAIRS = B // 2
        N2 = 2 * T

        def pair_loop(eng, body):
            with eng.Fori(0, PAIRS // 2 - 1) as i:
                for par in range(2):
                    body(eng, i * 2 + par, par, True, True)
            body(eng, PAIRS - 2, 0, True, False)
            body(eng, PAIRS - 1, 1, False, False)

        def x_pair(j):
            return x[:, bass.ds(j * N2, N2)]

        l2_norm, l2_tap, l2_pw, l2_res = sem("l2_norm"), sem("l2_tap"), sem("l2_pw"), sem("l2_res")

        def act_pad(act, j, par):
            for k in range(2):
                s = j * 2 + k
                act.wait_ge(gn_done, 6)
                nc.scalar.activation(pad[par][:, 1:SIDE + 1, k, 1:SIDE + 1], image(x_of(s)), ACT.Identity,
                                     bias=gn_shift[:, bass.ds(s, 1)], scale=gn_rstd[:, bass.ds(s, 1)]).then_inc(l2_norm, 1)

        def dve_depthwise(dve, j, par):
            dve.wait_ge(l2_norm, j * 2 + 2)
            wait(dve, l2_pw, j - 1)
            rows = pad[par][:, :, :, :].rearrange("c y b x -> c (y b) x")
            y = conv[par][:, :, :]
            for t in range(9):
                src = rows[:, t // 3 * 2:t // 3 * 2 + 2 * SIDE, t % 3:t % 3 + SIDE]
                if t == 0:
                    ins = nc.vector.tensor_scalar(y, src, dw_u[:, 0:1], None, ALU.mult)
                else:
                    dve.wait_ge(l2_tap, j * 9 + t)
                    ins = nc.vector.scalar_tensor_tensor(y, src, dw_u[:, t:t + 1], y, ALU.mult, ALU.add)
                ins.then_inc(l2_tap, 1)

        def pe_pointwise(pe, j, par):
            pe.wait_ge(l2_tap, j * 9 + 9)
            wait(pe, l2_res, j - 1)
            nc.tensor.matmul(bank[par][0:C, :], pwT[:, :], conv[par][:, :, :].rearrange("c y x -> c (y x)"),
                             start=True, stop=True).then_inc(l2_pw, 1)

        def dve_l2_residual(dve, j, par):
            dve.wait_ge(l2_pw, j + 1)
            xs = x_pair(j).rearrange("c (b y x) -> c y b x", b=2, x=SIDE)
            nc.vector.tensor_tensor(xs, bank[par][0:C, :].rearrange("c (y b x) -> c y b x", b=2, x=SIDE), xs,
                                    ALU.add).then_inc(l2_res, 1)
            dve.wait_ge(l2_res, j + 1)
            dve_stats(dve, 3, j * 2, 2)

        def act_l2(act, j, par, nxt, nxt2):
            if nxt2:
                act.wait_ge(l2_tap, j * 9 + 9)
                act_pad(act, j + 2, par)

        def dve_l2(dve, j, par, nxt, nxt2):
            if nxt:
                dve_depthwise(dve, j + 1, 1 - par)
            dve_l2_residual(dve, j, par)

        def pe_l2(pe, j, par, nxt, nxt2):
            if nxt:
                pe_pointwise(pe, j + 1, 1 - par)

        l3 = {n: sem("l3_" + n) for n in ("norm", "spike_a0", "spike", "qkv", "relu", "round_a", "round",
                                          "turned", "turned_sb", "kv", "kv_step", "attn", "relu_a", "round_b",
                                          "spike_a", "proj", "y", "out")}
        stored = [sem(f"l3_stored{i}") for i in range(2)]
        ATTN_SCALE = float(np.float32(12 ** -0.5 * 2)) / 64

        def act_l3_norm(act, j, par):
            wait(act, l3["spike_a0"], j * 1)
            for k in range(2):
                s = j * 2 + k
                act.wait_ge(gn_done, 8)
                nc.scalar.activation(xn3[:, k * T:(k + 1) * T], x_of(s), ACT.Relu, bias=gn_shift[:, bass.ds(s, 1)],
                                     scale=gn_rstd[:, bass.ds(s, 1)]).then_inc(l3["norm"], 1)

        def dve_l3_spike(dve, j, par):
            dve.wait_ge(l3["norm"], j * 2 + 2)
            nc.vector.tensor_scalar(rounded[:, :], xn3[:, :], 4.0, ROUND, ALU.min, ALU.add).then_inc(l3["spike_a0"], 1)
            dve.wait_ge(l3["spike_a0"], j + 1)
            nc.vector.tensor_scalar(spike_in[par][:, :], rounded[:, :], ROUND, None, ALU.subtract).then_inc(l3["spike"], 1)

        def pe_l3_qkv(pe, j, par):
            pe.wait_ge(l3["spike"], j + 1)
            wait(pe, l3["relu"], j * 3)
            for i in range(3):
                for part in range(3):
                    last = nc.tensor.matmul(bank[i][0:C, :], w3_parts[:, part, i * C:(i + 1) * C], spike_in[par][:, :],
                                            start=(part == 0), stop=(part == 2))
                last.then_inc(l3["qkv"], 1)

        def act_l3_relu(act, j, par):
            for i in range(3):
                act.wait_ge(l3["qkv"], j * 3 + (i + 1))
                if i == 0:
                    wait(act, l3["round_a"], j - 1)
                nc.scalar.activation(relu3[par][:, i, :], bank[i][0:C, :], ACT.Relu, bias=bn_b[:, i:i + 1],
                                     scale=bn_s4[:, i:i + 1]).then_inc(l3["relu"], 1)

        def dve_l3_round(dve, j, par):
            dve.wait_ge(l3["relu"], j * 3 + 3)
            nc.vector.tensor_scalar(relu3[par][:, :, :], relu3[par][:, :, :], 4.0, ROUND, ALU.min, ALU.add).then_inc(l3["round_a"], 1)
            dve.wait_ge(l3["round_a"], j + 1)
            wait(dve, l3["attn"], j - 1)
            nc.vector.tensor_scalar(qkv3[par][:, :, :], relu3[par][:, :, :], ROUND, None, ALU.subtract).then_inc(l3["round"], 1)

        turned = bank[3][:, :].bitcast(BF16)[:, 0:8 * C].rearrange("t (k b c) -> t k b c", k=2, c=C)

        def pe_l3_turn(pe, j, par):
            pe.wait_ge(l3["round"], j + 1)
            wait(pe, l3["turned_sb"], j)
            for k in range(2):
                for b in range(4):
                    last = nc.tensor.transpose(turned[:, k, b, :], qkv3[par][:, 1 + k, b * 128:(b + 1) * 128], ident_b[:, :])
            last.then_inc(l3["turned"], 1)

        def act_l3_turn(act, j, par):
            act.wait_ge(l3["turned"], j + 1)
            wait(act, l3["kv"], j)
            nc.scalar.copy(kvT[:, :, :, :], turned).then_inc(l3["turned_sb"], 1)

        def pe_l3_kv(pe, j, par):
            pe.wait_ge(l3["turned_sb"], j + 1)
            wait(pe, l3["kv_step"], j * 4)
            for b in range(4):
                last = nc.tensor.matmul(bank[4][0:C, b // 2 * C:(b // 2 + 1) * C], kvT[:, 0, b, :], kvT[:, 1, b, :],
                                        start=(b % 2 == 0), stop=(b % 2 == 1))
            last.then_inc(l3["kv"], 1)

        def dve_l3_kv(dve, j, par):
            dve.wait_ge(l3["kv"], j + 1)
            n = [0]

            def step(ins):
                n[0] += 1
                ins.then_inc(l3["kv_step"], 1)
                dve.wait_ge(l3["kv_step"], j * 4 + n[0])

            step(nc.vector.tensor_tensor(kv[:, :, :], bank[4][0:C, 0:2 * C].rearrange("d (b e) -> d b e", b=2),
                                         const("head_blocks", C).unsqueeze(1).broadcast_to([C, 2, C]), ALU.mult))
            wait(dve, l3["attn"], j)
            step(nc.vector.tensor_copy(kv_parts[:, 0, :, :], kv[:, :, :]))
            step(nc.vector.tensor_tensor(kv_lo[:, :, :], kv[:, :, :], kv_parts[:, 0, :, :], ALU.subtract))
            nc.vector.tensor_copy(kv_parts[:, 1, :, :], kv_lo[:, :, :]).then_inc(l3["kv_step"], 1)

        def pe_l3_attn(pe, j, par):
            pe.wait_ge(l3["kv_step"], j * 4 + 4)
            wait(pe, l3["relu_a"], j)
            for b in range(2):
                for part in range(2):
                    last = nc.tensor.matmul(bank[5][0:C, b * T:(b + 1) * T], kv_parts[:, part, b, :],
                                            qkv3[par][:, 0, b * T:(b + 1) * T], start=(part == 0), stop=(part == 1))
            last.then_inc(l3["attn"], 1)

        def act_l3_attn(act, j, par):
            act.wait_ge(l3["attn"], j + 1)
            wait(act, l3["round_b"], j)
            nc.scalar.activation(relu_a[:, :], bank[5][0:C, :], ACT.Relu, scale=ATTN_SCALE).then_inc(l3["relu_a"], 1)

        def dve_l3_attn(dve, j, par):
            dve.wait_ge(l3["relu_a"], j + 1)
            wait(dve, l3["spike_a"], j)
            nc.vector.tensor_scalar(rounded_a[:, :], relu_a[:, :], 4.0, ROUND, ALU.min, ALU.add).then_inc(l3["round_b"], 1)
            dve.wait_ge(l3["round_b"], j + 1)
            wait(dve, l3["proj"], j)
            nc.vector.tensor_scalar(spike_a[:, :], rounded_a[:, :], ROUND, None, ALU.subtract).then_inc(l3["spike_a"], 1)

        def pe_l3_proj(pe, j, par):
            pe.wait_ge(l3["spike_a"], j + 1)
            wait(pe, l3["y"], j)
            for part in range(3):
                last = nc.tensor.matmul(bank[6][0:C, :], w3_parts[:, part, 3 * C:4 * C], spike_a[:, :],
                                        start=(part == 0), stop=(part == 2))
            last.then_inc(l3["proj"], 1)

        def act_l3_proj(act, j, par):
            act.wait_ge(l3["proj"], j + 1)
            wait(act, l3["out"], j)
            nc.scalar.activation(y3[:, :], bank[6][0:C, :], ACT.Identity, bias=bn_b[:, 3:4],
                                 scale=bn_s4[:, 3:4]).then_inc(l3["y"], 1)

        def dve_l3_out(dve, j, par):
            dve.wait_ge(l3["y"], j + 1)
            dve.wait_ge(stored[par], j * 8 - par * 8)
            nc.vector.tensor_tensor(y_out[par][:, :], y3[:, :], x_pair(j), ALU.add).then_inc(l3["out"], 1)

        def sp_l3(sp, j, par, nxt, nxt2):
            sp.wait_ge(l3["out"], j + 1)
            sp.dma_start(out[bass.ds(j * 2, 2)].rearrange("b c h w -> c b (h w)"),
                         y_out[par][:, :].rearrange("c (b t) -> c b t", b=2)).then_inc(stored[par], 16)

        def pe_l3(pe, j, par, nxt, nxt2):
            pe_l3_turn(pe, j, par)
            if nxt:
                pe_l3_qkv(pe, j + 1, 1 - par)
            pe_l3_kv(pe, j, par)
            pe_l3_attn(pe, j, par)
            pe_l3_proj(pe, j, par)

        def act_l3(act, j, par, nxt, nxt2):
            act_l3_turn(act, j, par)
            if nxt:
                act_l3_relu(act, j + 1, 1 - par)
            act_l3_attn(act, j, par)
            if nxt2:
                act_l3_norm(act, j + 2, par)
            act_l3_proj(act, j, par)

        def dve_l3(dve, j, par, nxt, nxt2):
            dve_l3_kv(dve, j, par)
            if nxt:
                dve_l3_round(dve, j + 1, 1 - par)
            dve_l3_attn(dve, j, par)
            if nxt2:
                dve_l3_spike(dve, j + 2, par)
            dve_l3_out(dve, j, par)

        @block.vector
        def _(dve):
            dve.wait_ge(x_in, 16 * N_X)
            with dve.Fori(0, B) as s:
                dve_stats(dve, 0, s)
            dve_prepare(dve)
            dve_attention(dve, L0)
            dve_attention(dve, L1)
            dve_group_norm(dve, 2)
            dve_prepare_late(dve)
            dve_depthwise(dve, 0, 0)
            pair_loop(dve, dve_l2)
            dve_group_norm(dve, 3)
            dve_l3_spike(dve, 0, 0)
            dve_l3_round(dve, 0, 0)
            dve_l3_spike(dve, 1, 1)
            pair_loop(dve, dve_l3)

        @block.tensor
        def _(pe):
            pe_prepare(pe)
            pe.wait_ge(dve_prep, done["layer0"])
            pe_attention(pe, L0)
            pe_attention(pe, L1)
            pe_group_norm(pe, 2)
            pe_prepare_late(pe)
            pe.wait_ge(dve_prep, done["late"])
            pe_pointwise(pe, 0, 0)
            pair_loop(pe, pe_l2)
            pe_group_norm(pe, 3)
            pe_l3_qkv(pe, 0, 0)
            pair_loop(pe, pe_l3)

        @block.scalar
        def _(act):
            act.wait_ge(dve_prep, done["layer0"])
            act.wait_ge(w_in, W_IN)
            act_attention(act, L0)
            act_attention(act, L1)
            act.wait_ge(dve_prep, done["late"])
            act_pad(act, 0, 0)
            act_pad(act, 1, 1)
            pair_loop(act, act_l2)
            act_l3_norm(act, 0, 0)
            act_l3_norm(act, 1, 1)
            act_l3_relu(act, 0, 0)
            pair_loop(act, act_l3)

        @block.gpsimd
        def _(pool):
            pool_attention(pool, L0)
            pool_attention(pool, L1)
            pool_group_norm(pool, 2)
            nc.gpsimd.tensor_scalar(bn_t[:, :], bn[:, 3, :], EPS, None, ALU.add).then_inc(pool_prep, 1)
            pool.wait_ge(pool_prep, 1)
            nc.gpsimd.tensor_tensor(bn_r[:, :], bn_t[:, :], const("minus_half", C).broadcast_to([C, 4]),
                                    ALU.pow).then_inc(pool_prep, 1)
            pool_group_norm(pool, 3)

        @block.sync
        def _(sp):
            pair_loop(sp, sp_l3)
            for one in stored:
                sp.wait_ge(one, 16 * PAIRS // 2)


def kernel(**inputs):
    import concourse.bacc as bacc
    from concourse.bass_utils import run_bass_kernel_spmd

    nc = bacc.Bacc("TRN2", target_bir_lowering=False, num_devices=1)
    arrays, aps = {}, {}
    for name, value in [*inputs.items(), ("consts", constants())]:
        if name == "L1_conv_pos_emb":
            value = np.asarray(value)[::-1, ::-1]
        value = np.ascontiguousarray(value)
        arrays[f"in_{name}"] = value
        aps[name] = nc.dram_tensor(f"in_{name}", value.shape, mybir.dt.from_np(value.dtype), kind="ExternalInput").ap()
    out = nc.dram_tensor("out_0_dram", (B, C, SIDE, SIDE), F32, kind="ExternalOutput").ap()
    build(nc, aps, out)
    return run_bass_kernel_spmd(nc, [arrays], core_ids=[0]).results[0]["out_0_dram"]
```

```python
from contextlib import ExitStack

import numpy as np

import concourse.bass as bass
from concourse import mybir

F32 = mybir.dt.float32
BF16 = mybir.dt.bfloat16
I32 = mybir.dt.int32
ALU = mybir.AluOpType
ACT = mybir.ActivationFunctionType
AX = mybir.AxisListType

B, C, SIDE = 16, 96, 16
T = SIDE * SIDE
WIN, WT, NW = 8, 64, 4
HEADS, NP, NU, NH = 12, 3, 2, 2
GROUP = 3
EPS = 1e-5
NEG = -1e30
ROUND = 12582912.0
REL = (2 * WIN - 1) ** 2
WARM = 8
BIAS_KEYS = 13
REL_LO = 113
HD0, HD1 = C // HEADS, 32
INNER = HEADS * HD1

CONSTS = {}
_at = 0
for _name, _n in (("ident", 128), ("qmask0", 6), ("qmask1", 2), ("group_mean", C), ("ones", 128),
                  ("head_blocks", C), ("masks", 4 * WT), ("rows", 2), ("minus_half", 1), ("perm", 4 * 128)):
    CONSTS[_name] = (_at, _at + _n)
    _at += _n
N_CONST = _at


def constants():
    c = np.zeros((128, N_CONST), np.float32)
    p = np.arange(128)

    def put(name, value, rows=128):
        a, b = CONSTS[name]
        c[:rows, a:b] = value

    put("ident", np.eye(128))
    put("qmask0", (p[:, None] % 64 // HD0 == np.arange(NP * NH)) * np.float32(HD0 ** -0.5))
    put("qmask1", (p[:, None] // HD1 % 2 == np.arange(2)) * np.float32(HD1 ** -0.5))
    ch = np.arange(C)
    put("group_mean", (ch[:, None] // GROUP == ch[None] // GROUP) / np.float32(GROUP * T), C)
    put("ones", 1.0)
    put("head_blocks", ch[:, None] // 12 == ch[None] // 12, C)
    tok = np.arange(WT)
    r, q = tok // WIN >= WIN // 2, tok % WIN >= WIN // 2
    ud, lr = r[:, None] != r[None], q[:, None] != q[None]
    m = np.zeros((2, WT, NW, WT), bool)
    for w in range(NW):
        m[:, :, w] |= (ud & (w // 2 == 1)) | (lr & (w % 2 == 1))
    put("masks", m.reshape(128, NW * WT) * np.float32(NEG))
    perm = np.zeros((WT, NW, NH, WT))
    for w in range(NW):
        src = (tok // WIN + w // 2 * 4) % WIN * WIN + (tok % WIN + w % 2 * 4) % WIN
        perm[WT - 1 - src, w, :, tok] = 1
    put("perm", perm.reshape(WT, NW * 128), WT)
    put("minus_half", -0.5)
    put("rows", np.stack([p, p + REL_LO], 1))
    return c


class Attention:

    def __init__(self, n, hd):
        self.n, self.hd = n, hd
        self.wide = hd == HD1
        self.slots = 2 if self.wide else NP * NH
        self.qk_uses = 3 if self.wide else 2
        self.v_uses = 2 if self.wide else 1
        self.pieces = 6 if self.wide else 4
        self.adds = self.pieces
        self.uses_at = [(1, 2, 3), (1, 3, 4), (1, 4, 5), (2, 0, 2)] if self.wide else \
            [(1, 1, 2), (1, 2, 3), (1, 0, 0), (2, 0, 1)]
        self.evacs_at = [[(1, 1, 0, 4), (1, 2, 0, 4)], [(1, 3, 0, 4)], [(1, 4, 0, 4)], [(2, 0, 0, 4)]] if self.wide else \
            [[(1, 0, 3, 6), (1, 1, 0, 2)], [(1, 2, 0, 4)], [], [(2, 0, 0, 3)]]


class AttentionSems:

    def __init__(self, sem, n):
        self.xn_ready = sem(f"l{n}_xn_ready")
        self.qk_ready = sem(f"l{n}_qk_ready")
        self.v_ready = sem(f"l{n}_v_ready")
        self.evac_a = sem(f"l{n}_evac_a")
        self.evac_b = sem(f"l{n}_evac_b")
        self.scores_ready = sem(f"l{n}_scores_ready")
        self.biased = sem(f"l{n}_biased")
        self.maxed = sem(f"l{n}_maxed")
        self.shifted = sem(f"l{n}_shifted")
        self.exped = sem(f"l{n}_exped")
        self.summed = sem(f"l{n}_summed")
        self.inverted = sem(f"l{n}_inverted")
        self.scaled = sem(f"l{n}_scaled")
        self.transposed = sem(f"l{n}_transposed")
        self.probsT_sb = sem(f"l{n}_probsT_sb")
        self.pv_done = sem(f"l{n}_pv_done")
        self.heads_sb = sem(f"l{n}_heads_sb")
        self.out_ready = sem(f"l{n}_out_ready")
        self.y_ready = sem(f"l{n}_y_ready")
        self.residual = sem(f"l{n}_residual")


def build(nc, a, out):
    ctx = ExitStack()
    with ctx:
        ctx.enter_context(nc.allow_non_contiguous_dma(reason="small weights and tables, loaded once"))

        def sb(name, shape, dt=F32):
            return ctx.enter_context(nc.sbuf_tensor(name, shape, dt))

        def sem(name):
            return ctx.enter_context(nc.semaphore(name))

        bank = [ctx.enter_context(nc.psum_tensor(f"bank{i}", [128, 512], F32)) for i in range(8)]
        ps_scores = bank[0:2]
        ps_probsT = bank[2:4]
        ps_heads = bank[4]
        ps_qkv = bank[5:7]
        ps_mix = bank[7]

        x = sb("x", [C, B * T])
        cst = sb("cst", [128, N_CONST])

        def const(name, rows=128):
            lo, hi = CONSTS[name]
            return cst[0:rows, lo:hi]

        ident = const("ident")
        ones = const("ones")
        w0_raw = sb("w0_raw", [C, 3, C])
        w0T = sb("w0T", [128, 2 * 128 + C])
        b0_qk = sb("b0_qk", [128, 2])
        b0_q = sb("b0_q", [128, NP * NH])
        b0_v = sb("b0_v", [128, 2 * C])
        p0_raw = sb("p0_raw", [C, C])
        p0T = sb("p0T", [128, C])
        p0_b = sb("p0_b", [C, 1])
        rel_bc = sb("rel_bc", [REL_LO, WT * WT], I32)
        onehot = sb("onehot", [REL_LO, 2, WT * WT], BF16)
        table = sb("table", [REL_LO, 2, HEADS])
        table_rest = sb("table_rest", [REL_LO, 2, 2, HEADS])
        table_parts = sb("table_parts", [REL_LO, 2, 3, HEADS], BF16)
        bias0 = sb("bias0", [128, NP * NU, WT])
        w1 = sb("w1", [128, 3 * INNER])
        p1 = sb("p1", [128, NP, C])
        p1_b = sb("p1_b", [C, 1])
        pos = sb("pos", [WT, WT])
        bias1 = sb("bias1", [128, NW, WT])
        dw = sb("dw", [C, 9])
        dw_u = sb("dw_u", [C, 9])
        pw_raw = sb("pw_raw", [C, C])
        pw_u = sb("pw_u", [C, C])
        pw_abs = sb("pw_abs", [C, 1])
        pwT = sb("pwT", [C, C])
        q_mean = sb("q_mean", [C, 4])
        w3_raw = sb("w3_raw", [C, 4, C])
        w3_rest = sb("w3_rest", [C, 2, 4 * C])
        w3_parts = sb("w3_parts", [C, 3, 4 * C], BF16)
        bn = sb("bn", [C, 4, 4])
        bn_r = sb("bn_r", [C, 4])
        bn_s = sb("bn_s", [C, 4])
        bn_s4 = sb("bn_s4", [C, 4])
        bn_t = sb("bn_t", [C, 4])
        bn_b = sb("bn_b", [C, 4])
        ident_b = sb("ident_b", [C, C], BF16)
        stats = sb("stats", [C, 6 * B])
        gn_sq = sb("gn_sq", [C, 2 * B])
        gn_sum = sb("gn_sum", [C, 2 * B])
        gn_shift = sb("gn_shift", [C, B])
        gn_in = sb("gn_in", [C, 2 * B])
        gn_m2 = sb("gn_m2", [C, B])
        gn_var = sb("gn_var", [C, B])
        gn_negmean = sb("gn_negmean", [C, B])
        gn_mean = sb("gn_mean", [C, B])
        gn_veps = sb("gn_veps", [C, B])
        gn_rstd = sb("gn_rstd", [C, B])

        xn = [sb(f"xn{i}", [128, NW, WT]) for i in range(2)]
        q0 = [sb(f"q0_{i}", [128, NW, NP * NH, WT]) for i in range(2)]
        k0 = [sb(f"k0_{i}", [128, NU, T + WT]) for i in range(2)]
        v0 = [sb(f"v0_{i}", [128, NW * NP, NH, NH * NU * HD0]) for i in range(2)]
        q1 = [sb(f"q1_{i}", [128, 3, NW, 2, WT]) for i in range(2)]
        k1 = [sb(f"k1_{i}", [128, NU, NP, T + WT]) for i in range(2)]
        v1 = [sb(f"v1_{i}", [128, NW * NP, NH, NU * HD1]) for i in range(2)]
        probs = [sb(f"probs{i}", [128, NP * NU, WT]) for i in range(4)]
        row_max = [sb(f"row_max{i}", [128, NP * NU]) for i in range(4)]
        probsT = [sb(f"probsT{i}", [128, NP * 128]) for i in range(2)]
        row_sum = [sb(f"row_sum{i}", [128, NP * NU]) for i in range(4)]
        inv_sum = [sb(f"inv_sum{i}", [128, NP * NU]) for i in range(4)]
        heads0 = [sb(f"heads0_{i}", [128, T]) for i in range(2)]
        heads1 = [sb(f"heads1_{i}", [128, NP, T]) for i in range(2)]
        y_attn = sb("y_attn", [C, T])
        pad = [sb(f"pad{i}", [C, SIDE + 2, 2, SIDE + 2]) for i in range(2)]
        conv = [sb(f"conv{i}", [C, 2 * SIDE, SIDE]) for i in range(2)]
        xn3 = sb("xn3", [C, 2 * T])
        spike_in = [sb(f"spike_in{i}", [C, 2 * T], BF16) for i in range(2)]
        relu3 = [sb(f"relu3_{i}", [C, 3, 2 * T]) for i in range(2)]
        qkv3 = [sb(f"qkv3_{i}", [C, 3, 2 * T], BF16) for i in range(2)]
        relu_a = sb("relu_a", [C, 2 * T])
        rounded_a = sb("rounded_a", [C, 2 * T])
        rounded = sb("rounded", [C, 2 * T])
        kvT = sb("kvT", [128, 2, 4, C], BF16)
        kv = sb("kv", [C, 2, C])
        kv_lo = sb("kv_lo", [C, 2, C])
        kv_parts = sb("kv_parts", [C, 2, 2, C], BF16)
        spike_a = sb("spike_a", [C, 2 * T], BF16)
        y3 = sb("y3", [C, 2 * T])
        y_out = [sb(f"y_out{i}", [C, 2 * T]) for i in range(2)]

        x_in = sem("x_in")
        w_in = sem("w_in")
        bias_in = sem("bias_in")
        dve_prep = sem("dve_prep")
        pe_prep = sem("pe_prep")
        pool_prep = sem("pool_prep")
        stat = sem("stat")
        gn_pe = sem("gn_pe")
        gn_eps = sem("gn_eps")
        gn_done = sem("gn_done")

        L0, L1 = Attention(0, HD0), Attention(1, HD1)
        L0.s, L1.s = AttentionSems(sem, 0), AttentionSems(sem, 1)
        N_X = 4
        BIAS_IN = 16 * (1 + WIN)

        def wait(eng, s, v):
            if not (isinstance(v, int) and v <= 0):
                eng.wait_ge(s, v)

        def x_of(s, n=1):
            return x[:, bass.ds(s * T, n * T)]

        def image(ap):
            return ap.rearrange("c (y x) -> c y x", x=SIDE)

        def by_window(ap):
            return ap.rearrange("c (w t) -> c w t", w=NW)

        def window_pieces(L, w):
            wy, wx = w // 2, w % 2
            half = WIN // 2
            if not L.wide:
                y, xx = wy * WIN, wx * WIN
                return [(lambda i: i[:, y:y + WIN, xx:xx + WIN], lambda t: t)]

            def cols(i):
                return i.rearrange("c y (b x) -> c y b x", x=half)[:, :, 0:4:3] if wx else \
                    i[:, :, half:half + WIN].rearrange("c y (b x) -> c y b x", x=half)

            def tok(t):
                return t.rearrange("c y (b x) -> c y b x", x=half)

            if not wy:
                return [(lambda i: cols(i[:, half:half + WIN]), tok)]
            return [(lambda i, k=k: cols(i[:, k * 3 * half:(k * 3 + 1) * half]),
                     lambda t, k=k: tok(t[:, k * half:(k + 1) * half])) for k in range(2)]

        marks = {}

        block = ctx.enter_context(nc.Block())

        loads = []

        @block.sync
        def _(sp):
            n = B // N_X
            for i in range(N_X):
                sp.dma_start(x[:, i * n * T:(i + 1) * n * T].rearrange("c (b t) -> c b t", t=T),
                             a["x"][i * n:(i + 1) * n].rearrange("b c h w -> c b (h w)")).then_inc(x_in, 16)
            sp.dma_start(rel_bc[:, :], a["L0_conv_rel_index"].rearrange("q k -> (q k)").unsqueeze(0)
                         .broadcast_to([REL_LO, WT * WT])).then_inc(bias_in, 16)
            flipped = a["L1_conv_pos_emb"]
            for i in range(WIN):
                src = bass.AP(tensor=flipped.tensor, offset=flipped.offset + i * (2 * WIN - 1),
                              ap=[[1, WIN], [2 * WIN - 1, WIN], [1, WIN]])
                sp.dma_start(pos[i * WIN:(i + 1) * WIN, :].rearrange("q (y x) -> q y x", x=WIN), src).then_inc(bias_in, 16)

        def weight_loads():
            yield cst[:, :], a["consts"]
            yield w0_raw[:, :, :], a["L0_conv_qkv_w"].rearrange("(t o) i -> o t i", o=C)
            yield table[:, 0, :], a["L0_conv_rpb_table"][0:REL_LO]
            yield table[0:REL - REL_LO, 1, :], a["L0_conv_rpb_table"][REL_LO:REL]
            bias_qk = a["L0_conv_qkv_b"].rearrange("(t p u e) -> u p e t", t=3, p=NP, u=NU)[:, :, :, 0:2]
            for u in range(NU):
                for p in range(NP + 1):
                    at_ = u * 64 + p * NH * HD0
                    yield b0_qk[at_:at_ + NH * HD0, :], bias_qk[u, p % NP]
            for k in range(2):
                yield b0_v[:, k * C:(k + 1) * C], a["L0_conv_qkv_b"][2 * C:3 * C].unsqueeze(0).broadcast_to([128, C])
            for h in range(NH):
                for u in range(NU):
                    yield (p0_raw[:, :].rearrange("o (p h u d) -> o h u p d", p=NP, h=NH, u=NU)[:, h, u],
                           a["L0_conv_proj_w"].rearrange("o (p u h d) -> o h u p d", p=NP, h=NH, u=NU)[:, h, u])
            yield p0_b[:, :], a["L0_conv_proj_b"].unsqueeze(1)
            yield w1[0:C, :], a["L1_conv_w_qkv"]
            for h in range(NH):
                for u in range(NU):
                    yield (p1[(h * NU + u) * HD1:(h * NU + u + 1) * HD1, :, :],
                           a["L1_conv_w_out"].rearrange("(p u h d) c -> h u d p c", p=NP, u=NU, h=NH)[h, u])
            yield p1_b[:, :], a["L1_conv_b_out"].unsqueeze(1)
            yield dw[:, :], a["L2_conv_w_dw"].rearrange("c a y x -> c (a y x)")
            yield pw_raw[:, :], a["L2_conv_w_pw"].rearrange("o i y x -> o (i y x)")
            for j, name in enumerate("qkvp"):
                yield w3_raw[:, j, :], a[f"L3_conv_{name}_w"]
                for i, what in enumerate(("gamma", "beta", "mean", "var")):
                    yield bn[:, i, j:j + 1], a[f"L3_conv_{name}_{what}"].unsqueeze(1)

        loads = list(weight_loads())
        W_IN = 16 * len(loads)

        @block.scalar
        def _(act):
            for dst, src in loads:
                act.dma_start(dst, src).then_inc(w_in, 16)

        PE_W0, PE_P0, PE_BIAS, PE_POS, PE_PW_SUM, PE_PW, PE_W3 = range(1, 8)
        done = {}

        def dve_prepare(dve):
            count = [0]

            def step(ins):
                count[0] += 1
                ins.then_inc(dve_prep, 1)
                dve.wait_ge(dve_prep, count[0])

            dve.wait_ge(w_in, W_IN)
            for t, n in ((0, REL_LO), (1, REL - REL_LO)):
                step(nc.vector.tensor_copy(table_parts[0:n, t, 0, :], table[0:n, t, :]))
                step(nc.vector.tensor_tensor(table_rest[0:n, 0, t, :], table[0:n, t, :], table_parts[0:n, t, 0, :], ALU.subtract))
                step(nc.vector.tensor_copy(table_parts[0:n, t, 1, :], table_rest[0:n, 0, t, :]))
                step(nc.vector.tensor_tensor(table_rest[0:n, 1, t, :], table_rest[0:n, 0, t, :], table_parts[0:n, t, 1, :], ALU.subtract))
                step(nc.vector.tensor_copy(table_parts[0:n, t, 2, :], table_rest[0:n, 1, t, :]))
            dve.wait_ge(bias_in, BIAS_IN)
            lo = CONSTS["rows"][0]
            for t in range(2):
                step(nc.vector.tensor_scalar(onehot[:, t, :], rel_bc[:, :], cst[0:REL_LO, lo + t:lo + t + 1], None,
                                             ALU.is_equal))
            done["onehot"] = count[0]
            for v in v0 + v1:
                step(nc.vector.memset(v[:, :, :, :], 0.0))
            dve.wait_ge(pe_prep, PE_W0)
            step(nc.vector.memset(w0T[:, :], 0.0))
            for u in range(NU):
                step(nc.vector.tensor_copy(
                    w0T[0:C, 0:256].rearrange("c (t u r) -> c u t r", t=2, u=NU)[:, u, :, 0:48].rearrange("c t (p e) -> c t p e", p=NP),
                    bank[0][0:C, 0:2 * C].rearrange("c (t p u e) -> c u t p e", t=2, p=NP, u=NU)[:, u]))
            step(nc.vector.tensor_copy(w0T[0:C, 256:], bank[0][0:C, 2 * C:3 * C]))
            for t in (w1[C:, :], p0T[C:, :]):
                step(nc.vector.memset(t, 0.0))
            for t in xn:
                step(nc.vector.memset(t[C:, :, :], 0.0))
            for t in heads0:
                step(nc.vector.memset(t[C:, :], 0.0))
            for k in k0:
                step(nc.vector.memset(k[:, :, :], 0.0))
            for k in k1:
                step(nc.vector.memset(k[:, :, :, :], 0.0))
            dve.wait_ge(pe_prep, PE_P0)
            step(nc.vector.tensor_copy(p0T[0:C, :], bank[1][0:C, 0:C]))
            step(nc.vector.tensor_scalar(b0_q[:, :], const("qmask0"), b0_qk[:, 0:1], None, ALU.mult))
            dve.wait_ge(pe_prep, PE_BIAS)
            for k0_ in range(0, WT, BIAS_KEYS):
                n = min(BIAS_KEYS, WT - k0_)
                for h in range(NH):
                    src = bank[2 + k0_ // BIAS_KEYS][0:WT, 0:n * 3 * HEADS] \
                        .rearrange("q (k part g h) -> q h g k part", k=n, part=3, h=NH)[:, h]
                    step(nc.vector.tensor_reduce(bias0[h * WT:(h + 1) * WT, :, k0_:k0_ + n], src, AX.X, ALU.add))
            dve.wait_ge(pe_prep, PE_POS)
            step(nc.vector.tensor_tensor(bias1[:, :, :], ps_mix[:, 0:NW * WT].rearrange("p (w k) -> p w k", w=NW),
                                         const("masks").rearrange("p (w k) -> p w k", w=NW), ALU.add))
            done["layer0"] = count[0]

        def dve_prepare_late(dve):
            count = [done["layer0"]]

            def step(ins):
                count[0] += 1
                ins.then_inc(dve_prep, 1)
                dve.wait_ge(dve_prep, count[0])

            step(nc.vector.tensor_reduce(q_mean[:, 0:1], dw[:, :], AX.X, ALU.add, apply_absolute_value=True))
            step(nc.vector.tensor_scalar(q_mean[:, 0:1], q_mean[:, 0:1], 1.0 / 9, 1e-5, ALU.mult, ALU.max))
            step(nc.vector.reciprocal(q_mean[:, 1:2], q_mean[:, 0:1]))
            step(nc.vector.tensor_scalar(dw_u[:, :], dw[:, :], q_mean[:, 1:2], ROUND, ALU.mult, ALU.add))
            step(nc.vector.tensor_scalar(dw_u[:, :], dw_u[:, :], ROUND, 1.0, ALU.subtract, ALU.min))
            step(nc.vector.tensor_scalar(dw_u[:, :], dw_u[:, :], -1.0, None, ALU.max))
            step(nc.vector.tensor_tensor(dw_u[:, :], dw_u[:, :], dw[:, :], ALU.subtract))
            step(nc.vector.tensor_tensor(dw_u[:, :], dw_u[:, :], dw[:, :], ALU.add))
            step(nc.vector.tensor_scalar(dw_u[:, :], dw_u[:, :], q_mean[:, 0:1], None, ALU.mult))
            step(nc.vector.tensor_reduce(pw_abs[:, :], pw_raw[:, :], AX.X, ALU.add, apply_absolute_value=True))
            done["pw_abs"] = count[0]
            dve.wait_ge(pe_prep, PE_PW_SUM)
            step(nc.vector.tensor_scalar(q_mean[:, 2:3], bank[6][0:C, 0:1], 1.0 / (C * C), 1e-5, ALU.mult, ALU.max))
            step(nc.vector.reciprocal(q_mean[:, 3:4], q_mean[:, 2:3]))
            step(nc.vector.tensor_scalar(pw_u[:, :], pw_raw[:, :], q_mean[:, 3:4], ROUND, ALU.mult, ALU.add))
            step(nc.vector.tensor_scalar(pw_u[:, :], pw_u[:, :], ROUND, 1.0, ALU.subtract, ALU.min))
            step(nc.vector.tensor_scalar(pw_u[:, :], pw_u[:, :], -1.0, None, ALU.max))
            step(nc.vector.tensor_tensor(pw_u[:, :], pw_u[:, :], pw_raw[:, :], ALU.subtract))
            step(nc.vector.tensor_tensor(pw_u[:, :], pw_u[:, :], pw_raw[:, :], ALU.add))
            step(nc.vector.tensor_scalar(pw_u[:, :], pw_u[:, :], q_mean[:, 2:3], None, ALU.mult))
            done["pw_u"] = count[0]
            dve.wait_ge(pe_prep, PE_PW)
            step(nc.vector.tensor_copy(pwT[:, :], bank[6][0:C, 0:C]))
            dve.wait_ge(pe_prep, PE_W3)
            w3 = bank[7][0:C, 0:4 * C]
            step(nc.vector.tensor_copy(w3_parts[:, 0, :], w3))
            step(nc.vector.tensor_tensor(w3_rest[:, 0, :], w3, w3_parts[:, 0, :], ALU.subtract))
            step(nc.vector.tensor_copy(w3_parts[:, 1, :], w3_rest[:, 0, :]))
            step(nc.vector.tensor_tensor(w3_rest[:, 1, :], w3_rest[:, 0, :], w3_parts[:, 1, :], ALU.subtract))
            step(nc.vector.tensor_copy(w3_parts[:, 2, :], w3_rest[:, 1, :]))
            step(nc.vector.tensor_copy(ident_b[:, :], cst[0:C, 0:C]))
            dve.wait_ge(pool_prep, 2)
            step(nc.vector.tensor_tensor(bn_s[:, :], bn_r[:, :], bn[:, 0, :], ALU.mult))
            step(nc.vector.tensor_scalar(bn_s4[:, :], bn_s[:, :], 0.25, None, ALU.mult))
            step(nc.vector.tensor_tensor(bn_t[:, :], bn_s[:, :], bn[:, 2, :], ALU.mult))
            step(nc.vector.tensor_tensor(bn_b[:, :], bn[:, 1, :], bn_t[:, :], ALU.subtract))
            for i in range(2):
                step(nc.vector.memset(pad[i][:, :, :, :], 0.0))
            done["late"] = count[0]

        def pe_prepare(pe):
            pe.wait_ge(w_in, W_IN)
            for t in range(3):
                last = nc.tensor.transpose(bank[0][0:C, t * C:(t + 1) * C], w0_raw[:, t, :], ident[0:C, 0:C])
            last.then_inc(pe_prep, 1)
            nc.tensor.transpose(bank[1][0:C, 0:C], p0_raw[:, :], ident[0:C, 0:C]).then_inc(pe_prep, 1)
            pe.wait_ge(dve_prep, done["onehot"])
            for k in range(WT):
                for t, n in ((0, REL_LO), (1, REL - REL_LO)):
                    sel = onehot[0:n, t, :].rearrange("r (q k) -> r q k", k=WT)[:, :, k]
                    last = nc.tensor.matmul(
                        bank[2 + k // BIAS_KEYS][0:WT, k % BIAS_KEYS * 3 * HEADS:(k % BIAS_KEYS + 1) * 3 * HEADS],
                        sel, table_parts[0:n, t, :, :], start=(t == 0), stop=(t == 1))
            last.then_inc(pe_prep, 1)
            pe.wait_ge(bias_in, BIAS_IN)
            for w in range(NW):
                for yb in range(2):
                    for xb in range(2):
                        def block44(ap, i, j):
                            return ap.rearrange("q (yb y xb x) -> q yb y xb x", yb=2, xb=2, y=4)[:, i, :, j, :]
                        last = nc.tensor.matmul(block44(ps_mix[:, w * WT:(w + 1) * WT], yb, xb),
                                                const("perm", WT)[:, w * 128:(w + 1) * 128],
                                                block44(pos[:, :], yb ^ (w // 2), xb ^ (w % 2)), start=True, stop=True)
            last.then_inc(pe_prep, 1)

        def pe_prepare_late(pe):
            pe.wait_ge(dve_prep, done["pw_abs"])
            nc.tensor.matmul(bank[6][0:C, 0:1], ones[0:C, 0:C], pw_abs[:, :], start=True, stop=True).then_inc(pe_prep, 1)
            pe.wait_ge(dve_prep, done["pw_u"])
            nc.tensor.transpose(bank[6][0:C, 0:C], pw_u[:, :], ident[0:C, 0:C]).then_inc(pe_prep, 1)
            for j in range(4):
                last = nc.tensor.transpose(bank[7][0:C, j * C:(j + 1) * C], w3_raw[:, j, :], ident[0:C, 0:C])
            last.then_inc(pe_prep, 1)

        STEPS = 8
        HALF = T // 2

        def stat_base(layer):
            return layer * (B + STEPS)

        def dve_stats(dve, layer, s, n=1):
            for j in range(n):
                nc.vector.bn_stats(stats[:, bass.ds((s + j) * 6, 6)], x_of(s + j)).then_inc(stat, 1)

        def dve_group_norm(dve, layer):
            n = [stat_base(layer) + B]

            def step(ins):
                n[0] += 1
                ins.then_inc(stat, 1)
                dve.wait_ge(stat, n[0])

            dve.wait_ge(stat, n[0])
            mean, m2 = (stats[:, :].rearrange("c (n k) -> c k n", k=3)[:, k, :] for k in (1, 2))
            sides = stats[:, :].rearrange("c (b e k) -> c e k b", e=2, k=3)
            step(nc.vector.tensor_tensor(gn_in[:, 0:B], sides[:, 0, 1, :], sides[:, 1, 1, :], ALU.add))
            step(nc.vector.tensor_tensor(gn_sq[:, :], mean, mean, ALU.mult))
            step(nc.vector.scalar_tensor_tensor(gn_sum[:, :], gn_sq[:, :], float(HALF), m2, ALU.mult, ALU.add))
            both = gn_sum[:, :].rearrange("c (b e) -> c e b", e=2)
            step(nc.vector.tensor_tensor(gn_in[:, B:2 * B], both[:, 0, :], both[:, 1, :], ALU.add))
            dve.wait_ge(gn_pe, layer + 1)
            step(nc.vector.tensor_scalar(gn_mean[:, :], ps_mix[0:C, 0:B], float(HALF), None, ALU.mult))
            step(nc.vector.tensor_scalar(gn_negmean[:, :], gn_mean[:, :], -1.0, None, ALU.mult))
            step(nc.vector.tensor_tensor(gn_m2[:, :], gn_mean[:, :], gn_mean[:, :], ALU.mult))
            step(nc.vector.tensor_tensor(gn_var[:, :], ps_mix[0:C, B:2 * B], gn_m2[:, :], ALU.subtract))

        def pool_group_norm(pool, layer):
            pool.wait_ge(stat, stat_base(layer) + B + STEPS)
            nc.gpsimd.tensor_scalar(gn_veps[:, :], gn_var[:, :], EPS, None, ALU.add).then_inc(gn_eps, 1)
            pool.wait_ge(gn_eps, layer + 1)
            nc.gpsimd.tensor_tensor(gn_rstd[:, :], gn_veps[:, :], const("minus_half", C).broadcast_to([C, B]),
                                    ALU.pow).then_inc(gn_done, 1)
            pool.wait_ge(gn_done, 2 * layer + 1)
            nc.gpsimd.tensor_tensor(gn_shift[:, :], gn_negmean[:, :], gn_rstd[:, :], ALU.mult).then_inc(gn_done, 1)

        def pe_group_norm(pe, layer):
            pe.wait_ge(stat, stat_base(layer) + B + 4)
            nc.tensor.matmul(ps_mix[0:C, 0:2 * B], const("group_mean", C), gn_in[:, :], start=True, stop=True).then_inc(gn_pe, 1)

        def qkv_plan(L):
            if L.wide:
                return [("qk", 0, "act", 4), ("qk", 1, "dve", 4), ("qk", 2, "act", 4),
                        ("v", 0, "dve", 4), ("v", 1, "act", 4)]
            return [("q", 0, "act", L.slots), ("k", 0, "dve", 2), ("v", 0, "dve", 4)]

        def bank_of(L, parity, i):
            plan = qkv_plan(L)
            b = (i + parity * len(plan)) % 2
            before = sum(plan[j][3] for j in range(i) if (j + parity * len(plan)) % 2 == b)
            return b, before

        def evacs(L, parity):
            plan = qkv_plan(L)
            tot = [0, 0]
            for i, use in enumerate(plan):
                tot[(i + parity * len(plan)) % 2] += use[3]
            return tot

        def evac_before(L, s, parity, b):
            both = evacs(L, 0)[b] + evacs(L, 1)[b]
            if isinstance(s, int):
                return s // 2 * both + (evacs(L, 0)[b] if s % 2 else 0)
            return s.pair * both + (evacs(L, 0)[b] if parity else 0)

        class Sample:

            def __init__(self, pair, parity):
                self.pair, self.parity = pair, parity

            def __add__(self, n):
                return self.pair * 2 + (self.parity + n)

            __radd__ = __add__

            def __mul__(self, n):
                return self.pair * (2 * n) + self.parity * n

            __rmul__ = __mul__

            def shift(self, n):
                return Sample(self.pair + (self.parity + n) // 2, (self.parity + n) % 2)

        def moved(s, n):
            return s + n if isinstance(s, int) else s.shift(n)

        def parity(s):
            return s % 2 if isinstance(s, int) else s.parity

        def win_count(s, w):
            return s * NW + (w + 1)

        def evac_sem(L, par, i):
            return (L.s.evac_a, L.s.evac_b)[bank_of(L, par, i)[0]]

        def evacuated(eng, L, s, i):
            par = parity(s)
            b, before = bank_of(L, par, i)
            eng.wait_ge(evac_sem(L, par, i), evac_before(L, s, par, b) + before + qkv_plan(L)[i][3])

        def pe_qkv(pe, L, s, i0, i1):
            par = parity(s)
            if i0 == 0:
                pe.wait_ge(L.s.xn_ready, s * L.pieces + L.pieces)
            for i in range(i0, i1):
                kind, j, _, _ = qkv_plan(L)[i]
                b, before = bank_of(L, par, i)
                wait(pe, evac_sem(L, par, i), evac_before(L, s, par, b) + before)
                o = ps_qkv[b]
                if kind != "v":
                    w = w1 if L.wide else w0T
                    for half in {"q": (0,), "k": (1,), "qk": (0, 1)}[kind]:
                        col = half * (INNER if L.wide else 128) + j * 128
                        last = nc.tensor.matmul(o[:, half * T:(half + 1) * T], w[:, col:col + 128], xn[par][:, :, :],
                                                start=True, stop=True)
                    last.then_inc(L.s.qk_ready, 1)
                    continue
                n = HEADS * L.hd
                for k in (range(NW // 2) if not L.wide else (j,)):
                    at_ = 0 if L.wide else k * n
                    last = nc.tensor.matmul(o[:, at_:at_ + n], xn[par][:, 2 * k:2 * k + 2, :].rearrange("c w t -> c (w t)"),
                                            w1[:, 2 * n:3 * n] if L.wide else w0T[:, 256:], start=True, stop=True)
                last.then_inc(L.s.v_ready, 1)

        def pe_scores(pe, L, s, w, half):
            if half == 0:
                if w == 0:
                    for i in range(L.qk_uses):
                        evacuated(pe, L, s, i)
                wait(pe, L.s.biased, win_count(s, w - 2))
            par = parity(s)
            keys = slice(w * WT, (w + 2) * WT)
            for g in range(half * NP, (half + 1) * NP):
                p, u = g // NU, g % NU
                if L.wide:
                    q, k = q1[par][:, p, w, :, :], k1[par][:, u, p, keys]
                else:
                    q, k = q0[par][:, w, p * NH:(p + 1) * NH, :], k0[par][:, u, keys]
                last = nc.tensor.matmul(ps_scores[w % 2][:, g * WT:(g + 2) * WT], q, k, start=True, stop=True)
            if half:
                last.then_inc(L.s.scores_ready, 1)

        def pe_transpose(pe, L, s, w):
            pe.wait_ge(L.s.scaled, win_count(s, w))
            wait(pe, L.s.probsT_sb, win_count(s, w - 2))
            for p in range(NP):
                last = nc.tensor.transpose(ps_probsT[w % 2][:, p * 128:(p + 1) * 128], probs[w][:, 2 * p:2 * p + 2, :], ident)
            last.then_inc(L.s.transposed, 1)

        def pe_values(pe, L, s, w):
            pe.wait_ge(L.s.probsT_sb, win_count(s, w))
            pT = probsT[w % 2]
            if L.wide:
                if w % 2 == 0:
                    evacuated(pe, L, s, L.qk_uses + w // 2)
                wait(pe, L.s.heads_sb, win_count(s, w - 1))
                for p in range(NP):
                    for h in range(NH):
                        last = nc.tensor.matmul(ps_heads[h * WT:(h + 1) * WT, p * WT:(p + 1) * WT],
                                                v1[parity(s)][:, w * NP + p, h, :], pT[:, p * 128 + h * WT:p * 128 + (h + 1) * WT],
                                                start=True, stop=True)
            else:
                if w == 0:
                    evacuated(pe, L, s, L.qk_uses)
                    wait(pe, L.s.heads_sb, s * 1)
                v = v0[parity(s)]
                for p in range(NP):
                    for h in range(NH):
                        last = nc.tensor.matmul(ps_heads[p * 32:(p + 1) * 32, w * WT:(w + 1) * WT],
                                                v[:, (w % 2 * 2 + w // 2) * NP + p, h, :],
                                                pT[:, p * 128 + h * WT:p * 128 + (h + 1) * WT],
                                                start=(h == 0), stop=(h == NH - 1))
            last.then_inc(L.s.pv_done, 1)

        def pe_out(pe, L, s):
            pe.wait_ge(L.s.heads_sb, win_count(s, 3) if L.wide else s + 1)
            wait(pe, L.s.y_ready, s * 1)
            o = ps_mix[0:C, 0:T]
            if L.wide:
                for p in range(NP):
                    last = nc.tensor.matmul(o, p1[:, p, :], heads1[parity(s)][:, p, :], start=(p == 0), stop=(p == NP - 1))
            else:
                last = nc.tensor.matmul(o, p0T[:, :], heads0[parity(s)][:, :], start=True, stop=True)
            last.then_inc(L.s.out_ready, 1)

        def act_exp(act, L, s, w):
            act.wait_ge(L.s.shifted, win_count(s, w))
            nc.scalar.activation(probs[w][:, :, :], probs[w][:, :, :], ACT.Exp).then_inc(L.s.exped, 1)

        def act_probsT(act, L, s, w):
            act.wait_ge(L.s.transposed, win_count(s, w))
            wait(act, L.s.pv_done, win_count(s, w - 2))
            nc.scalar.copy(probsT[w % 2][:, :], ps_probsT[w % 2][:, 0:NP * 128]).then_inc(L.s.probsT_sb, 1)

        def act_heads(act, L, s, w):
            act.wait_ge(L.s.pv_done, win_count(s, w))
            if L.wide:
                nc.scalar.copy(heads1[parity(s)][:, :, w * WT:(w + 1) * WT],
                               ps_heads[:, 0:NP * WT].rearrange("r (p q) -> r p q", p=NP)).then_inc(L.s.heads_sb, 1)
            else:
                nc.scalar.copy(heads0[parity(s)][0:C, :], ps_heads[0:C, 0:T]).then_inc(L.s.heads_sb, 1)

        def act_out(act, L, s):
            act.wait_ge(L.s.out_ready, s + 1)
            wait(act, L.s.residual, s * L.adds)
            nc.scalar.activation(y_attn[:, :], ps_mix[0:C, 0:T], ACT.Identity,
                                 bias=(p1_b if L.wide else p0_b)[:, 0:1]).then_inc(L.s.y_ready, 1)

        def evac_q(eng, L, s, i, j, slot):
            par = parity(s)
            b, _ = bank_of(L, par, i)
            if L.wide:
                src, dst = by_window(ps_qkv[b][:, 0:T]), q1[par][:, j, :, slot, :]
                lo = CONSTS["qmask1"][0] + slot
                scale = cst[:, lo:lo + 1]
                if eng == "act":
                    return nc.scalar.activation(dst, src, ACT.Copy, scale=scale)
                return nc.vector.tensor_scalar(dst, src, scale, None, ALU.mult)
            src, dst = by_window(ps_qkv[b][:, 0:T]), q0[par][:, :, slot, :]
            lo = CONSTS["qmask0"][0] + slot
            scale, bias = cst[:, lo:lo + 1], b0_q[:, slot:slot + 1]
            if eng == "act":
                return nc.scalar.activation(dst, src, ACT.Identity, scale=scale, bias=bias)
            return nc.vector.tensor_scalar(dst, src, scale, bias, ALU.mult, ALU.add)

        def evac_k(eng, L, s, i, j, u):
            par = parity(s)
            b, _ = bank_of(L, par, i)
            rows = slice(u * 64, u * 64 + 64)
            src = ps_qkv[b][rows, T:2 * T]
            if L.wide:
                dst = k1[par][rows, u, j, 0:T]
                return nc.scalar.copy(dst, src) if eng == "act" else nc.vector.tensor_copy(dst, src)
            return nc.vector.tensor_scalar(k0[par][rows, u, 0:T], src, b0_qk[rows, 1:2], None, ALU.add)

        def evac_v(eng, L, s, i, j, odd, u):
            par = parity(s)
            b, _ = bank_of(L, par, i)
            src_rows, rows = slice(odd * WT, (odd + 1) * WT), slice(u * WT, (u + 1) * WT)
            if L.wide:
                src = ps_qkv[b][src_rows, 0:INNER].rearrange("k (p u h d) -> k u p h d", p=NP, u=NU, h=NH)[:, u]
                w = 2 * j + odd
                dst = v1[par][rows, w * NP:(w + 1) * NP, :, u * HD1:(u + 1) * HD1]
                return nc.scalar.copy(dst, src) if eng == "act" else nc.vector.tensor_copy(dst, src)
            def heads_of_u(ap):
                return ap.rearrange("k (g u h d) -> k u g h d", u=NU, h=NH, d=HD0)[:, u]
            n = 2 * NP
            dst = v0[par][rows, odd * n:(odd + 1) * n, :, :].rearrange("k g h e -> k g (h e)")[:, :, u * HD0:u * HD0 + 56] \
                .rearrange("k g (a d) -> k g a d", d=HD0)[:, :, 0:7:6, :]
            return nc.vector.tensor_tensor(dst, heads_of_u(ps_qkv[b][src_rows, 0:2 * C]), heads_of_u(b0_v[src_rows, :]), ALU.add)

        def evacuate(eng, who, L, s, i, first=0, end=99):
            kind, j, engine, _ = qkv_plan(L)[i]
            if engine != who:
                return
            if kind == "v":
                todo = [lambda o=o, u=u: evac_v(who, L, s, i, j, o, u) for o in range(2) for u in range(NU)]
            else:
                todo = []
                if kind != "k":
                    todo += [lambda h=h: evac_q(who, L, s, i, j, h) for h in range(L.slots)]
                if kind != "q":
                    todo += [lambda u=u: evac_k(who, L, s, i, j, u) for u in range(NU)]
            if first == 0 and kind == "v":
                eng.wait_ge(L.s.v_ready, s * L.v_uses + (j + 1))
                wait(eng, L.s.pv_done, s * NW - NW)
            elif first == 0:
                eng.wait_ge(L.s.qk_ready, s * L.qk_uses + (i + 1))
                wait(eng, L.s.scores_ready, s * NW - NW)
            for one in todo[first:end]:
                one().then_inc(evac_sem(L, parity(s), i), 1)

        def evacuate_step(eng, who, L, s, w, nxt, nxt2):
            for ahead, i, first, end in L.evacs_at[w]:
                if nxt2 if ahead == 2 else nxt:
                    evacuate(eng, who, L, moved(s, ahead), i, first, end)

        def dve_scores(dve, L, s, w):
            dve.wait_ge(L.s.scores_ready, win_count(s, w))
            wait(dve, L.s.transposed, win_count(s, w - 4))
            if L.wide:
                b = bias1[:, w, :].unsqueeze(1).broadcast_to([128, NP * NU, WT])
            else:
                b = bias0[:, :, :]
            nc.vector.tensor_tensor(probs[w][:, :, :], ps_scores[w % 2][:, 0:NP * NU * WT].rearrange("p (g k) -> p g k", k=WT),
                                    b, ALU.add).then_inc(L.s.biased, 1)
            dve.wait_ge(L.s.biased, win_count(s, w))
            nc.vector.tensor_reduce(row_max[w][:, :], probs[w][:, :, :], AX.X, ALU.max).then_inc(L.s.maxed, 1)

        def dve_sum(dve, L, s, w):
            dve.wait_ge(L.s.exped, win_count(s, w))
            nc.vector.tensor_reduce(row_sum[w][:, :], probs[w][:, :, :], AX.X, ALU.add).then_inc(L.s.summed, 1)
            dve.wait_ge(L.s.summed, win_count(s, w))
            nc.vector.reciprocal(inv_sum[w][:, :], row_sum[w][:, :]).then_inc(L.s.inverted, 1)

        def dve_new_x(dve, L, s):
            dve.wait_ge(L.s.residual, s * L.adds + L.adds)
            dve_stats(dve, L.n + 1, s)

        def dve_norm(dve, L, s):
            wait(dve, L.s.v_ready, s * L.v_uses - L.v_uses)
            for w in range(NW):
                for of_image, of_tokens in window_pieces(L, w):
                    tokens = xn[parity(s)][0:C, w, :].rearrange("c (y x) -> c y x", x=WIN)
                    nc.vector.tensor_scalar(of_tokens(tokens), of_image(image(x_of(s))), gn_mean[:, bass.ds(s * 1, 1)],
                                            gn_rstd[:, bass.ds(s * 1, 1)], ALU.subtract, ALU.mult).then_inc(L.s.xn_ready, 1)

        def by_row(r):
            return r[:, :].unsqueeze(2).broadcast_to([128, NP * NU, WT])

        def pool_shift(pool, L, s, w):
            pool.wait_ge(L.s.maxed, win_count(s, w))
            nc.gpsimd.tensor_tensor(probs[w][:, :, :], probs[w][:, :, :], by_row(row_max[w]),
                                    ALU.subtract).then_inc(L.s.shifted, 1)

        def pool_scale(pool, L, s, w):
            pool.wait_ge(L.s.inverted, win_count(s, w))
            nc.gpsimd.tensor_tensor(probs[w][:, :, :], probs[w][:, :, :], by_row(inv_sum[w]),
                                    ALU.mult).then_inc(L.s.scaled, 1)

        def pool_residual(pool, L, s, half):
            parts = [(w, *part) for w in range(NW) for part in window_pieces(L, w)]
            n = len(parts) // 2
            if half == 0:
                pool.wait_ge(L.s.y_ready, s + 1)
            for w, of_image, of_tokens in parts[half * n:(half + 1) * n]:
                pool.wait_ge(gn_done, 2 * L.n + 2)
                part = of_image(image(x_of(s)))
                nc.gpsimd.tensor_tensor(part, of_tokens(y_attn[:, w * WT:(w + 1) * WT].rearrange("c (y x) -> c y x", x=WIN)),
                                        part, ALU.add).then_inc(L.s.residual, 1)

        def at(s, w):
            return moved(s, w // NW), w % NW

        def uses(L, s, w, nxt, nxt2):
            ahead, i0, i1 = L.uses_at[w]
            return (moved(s, ahead), i0, i1) if (nxt2 if ahead == 2 else nxt) else (s, 0, 0)

        def pe_sample(pe, L, s, prev, nxt, nxt2):
            for w in range(NW):
                q = uses(L, s, w, nxt, nxt2)
                if q[2]:
                    pe_qkv(pe, L, *q)
                ahead = w < 1 or nxt
                if ahead:
                    pe_scores(pe, L, *at(s, w + 3), 0)
                pe_transpose(pe, L, s, w)
                if ahead:
                    pe_scores(pe, L, *at(s, w + 3), 1)
                if w >= 1 or prev:
                    pe_values(pe, L, *at(s, w - 1))
                if w == 1 and prev:
                    pe_out(pe, L, moved(s, -1))

        def act_sample(act, L, s, prev, nxt, nxt2):
            for w in range(NW):
                if w < 2 or nxt:
                    act_exp(act, L, *at(s, w + 2))
                act_probsT(act, L, s, w)
                evacuate_step(act, "act", L, s, w, nxt, nxt2)
                if (w >= 1 or prev) and (L.wide or w == 0):
                    act_heads(act, L, *at(s, w - 1))
                if w == 1 and prev:
                    act_out(act, L, moved(s, -1))

        def dve_sample(dve, L, s, prev, nxt, nxt2):
            for w in range(NW):
                if w < 2 or nxt:
                    dve_scores(dve, L, *at(s, w + 2))
                if w < 3 or nxt:
                    dve_sum(dve, L, *at(s, w + 1))
                evacuate_step(dve, "dve", L, s, w, nxt, nxt2)
                if w == 2 and nxt2:
                    dve_norm(dve, L, moved(s, 2))
                if w == 1 and prev == 2:
                    dve_new_x(dve, L, moved(s, -2))

        def pool_sample(pool, L, s, prev, nxt, nxt2):
            for w in range(NW):
                if w < 2 or nxt:
                    pool_shift(pool, L, *at(s, w + 2))
                if w < 3 or nxt:
                    pool_scale(pool, L, *at(s, w + 1))
                if w >= 2 and prev:
                    pool_residual(pool, L, moved(s, -1), w - 2)

        def attention_loop(eng, L, body):
            body(eng, L, 0, 0, True, True)
            body(eng, L, 1, 1, True, True)
            with eng.Fori(0, B // 2 - 2) as i:
                for par in range(2):
                    body(eng, L, Sample(i + 1, par), 2, True, True)
            body(eng, L, B - 2, 2, True, False)
            body(eng, L, B - 1, 2, False, False)

        def first_uses(L):
            return [(0, 0, L.qk_uses + L.v_uses), (1, 0, L.uses_at[3][2])]

        def pe_stay_warm(pe, n):
            for _ in range(n):
                nc.tensor.matmul(ps_heads[:, :], ident, cst[:, 0:512], start=True, stop=True)

        def pe_attention(pe, L):
            pe_group_norm(pe, L.n)
            (_, _, n), second = first_uses(L)
            pe_qkv(pe, L, 0, 0, L.qk_uses)
            for half in range(2):
                pe_scores(pe, L, 0, 0, half)
            for half in range(2):
                pe_scores(pe, L, 0, 1, half)
            pe_qkv(pe, L, 0, L.qk_uses, n)
            pe_qkv(pe, L, *second)
            for half in range(2):
                pe_scores(pe, L, 0, 2, half)
            pe_stay_warm(pe, WARM)
            attention_loop(pe, L, pe_sample)
            pe_values(pe, L, B - 1, 3)
            pe_out(pe, L, B - 1)

        def evacuate_first(eng, who, L, s, i0, i1):
            for i in range(i0, i1):
                later = [first for ahead, use, first, _ in L.evacs_at[0] if use == i]
                evacuate(eng, who, L, s, i, 0, later[0] if s == 1 and later else 99)

        def act_attention(act, L):
            evacuate_first(act, "act", L, 0, 0, L.qk_uses)
            act_exp(act, L, 0, 0)
            evacuate_first(act, "act", L, 0, L.qk_uses, L.qk_uses + L.v_uses)
            act_exp(act, L, 0, 1)
            evacuate_first(act, "act", L, *first_uses(L)[1])
            attention_loop(act, L, act_sample)
            act_heads(act, L, B - 1, 3)
            act_out(act, L, B - 1)

        def dve_attention(dve, L):
            dve_group_norm(dve, L.n)
            dve.wait_ge(gn_done, 2 * L.n + 1)
            dve_norm(dve, L, 0)
            evacuate_first(dve, "dve", L, 0, 0, L.qk_uses)
            dve_scores(dve, L, 0, 0)
            dve_norm(dve, L, 1)
            dve_scores(dve, L, 0, 1)
            evacuate_first(dve, "dve", L, 0, L.qk_uses, L.qk_uses + L.v_uses)
            dve_sum(dve, L, 0, 0)
            evacuate_first(dve, "dve", L, *first_uses(L)[1])
            attention_loop(dve, L, dve_sample)
            dve_new_x(dve, L, B - 2)
            dve_new_x(dve, L, B - 1)

        def pool_attention(pool, L):
            pool_group_norm(pool, L.n)
            pool_shift(pool, L, 0, 0)
            pool_shift(pool, L, 0, 1)
            pool_scale(pool, L, 0, 0)
            attention_loop(pool, L, pool_sample)
            for half in range(2):
                pool_residual(pool, L, B - 1, half)

        PAIRS = B // 2
        N2 = 2 * T

        def pair_loop(eng, body):
            body(eng, 0, 0, True, True)
            body(eng, 1, 1, True, True)
            with eng.Fori(0, PAIRS // 2 - 2) as i:
                for par in range(2):
                    body(eng, i * 2 + (2 + par), par, True, True)
            body(eng, PAIRS - 2, 0, True, False)
            body(eng, PAIRS - 1, 1, False, False)

        def x_pair(j):
            return x[:, bass.ds(j * N2, N2)]

        l2_norm, l2_tap, l2_pw, l2_res = sem("l2_norm"), sem("l2_tap"), sem("l2_pw"), sem("l2_res")

        def act_pad(act, j, par):
            for k in range(2):
                s = j * 2 + k
                act.wait_ge(gn_done, 6)
                nc.scalar.activation(pad[par][:, 1:SIDE + 1, k, 1:SIDE + 1], image(x_of(s)), ACT.Identity,
                                     bias=gn_shift[:, bass.ds(s, 1)], scale=gn_rstd[:, bass.ds(s, 1)]).then_inc(l2_norm, 1)

        def dve_depthwise(dve, j, par):
            dve.wait_ge(l2_norm, j * 2 + 2)
            wait(dve, l2_pw, j - 1)
            rows = pad[par][:, :, :, :].rearrange("c y b x -> c (y b) x")
            y = conv[par][:, :, :]
            for t in range(9):
                src = rows[:, t // 3 * 2:t // 3 * 2 + 2 * SIDE, t % 3:t % 3 + SIDE]
                if t == 0:
                    ins = nc.vector.tensor_scalar(y, src, dw_u[:, 0:1], None, ALU.mult)
                else:
                    dve.wait_ge(l2_tap, j * 9 + t)
                    ins = nc.vector.scalar_tensor_tensor(y, src, dw_u[:, t:t + 1], y, ALU.mult, ALU.add)
                ins.then_inc(l2_tap, 1)

        def pe_pointwise(pe, j, par):
            pe.wait_ge(l2_tap, j * 9 + 9)
            wait(pe, l2_res, j - 1)
            nc.tensor.matmul(bank[par][0:C, :], pwT[:, :], conv[par][:, :, :].rearrange("c y x -> c (y x)"),
                             start=True, stop=True).then_inc(l2_pw, 1)

        def dve_l2_residual(dve, j, par):
            dve.wait_ge(l2_pw, j + 1)
            xs = x_pair(j).rearrange("c (b y x) -> c y b x", b=2, x=SIDE)
            nc.vector.tensor_tensor(xs, bank[par][0:C, :].rearrange("c (y b x) -> c y b x", b=2, x=SIDE), xs,
                                    ALU.add).then_inc(l2_res, 1)
            dve.wait_ge(l2_res, j + 1)
            dve_stats(dve, 3, j * 2, 2)

        def act_l2(act, j, par, nxt, nxt2):
            if nxt2:
                act.wait_ge(l2_tap, j * 9 + 9)
                act_pad(act, j + 2, par)

        def dve_l2(dve, j, par, nxt, nxt2):
            if nxt:
                dve_depthwise(dve, j + 1, 1 - par)
            dve_l2_residual(dve, j, par)

        def pe_l2(pe, j, par, nxt, nxt2):
            if nxt:
                pe_pointwise(pe, j + 1, 1 - par)

        l3 = {n: sem("l3_" + n) for n in ("norm", "spike_a0", "spike", "qkv", "relu", "round_a", "round",
                                          "turned", "turned_sb", "kv", "kv_step", "attn", "relu_a", "round_b",
                                          "spike_a", "proj", "y", "out")}
        stored = [sem(f"l3_stored{i}") for i in range(2)]
        ATTN_SCALE = float(np.float32(12 ** -0.5 * 2)) / 64

        def act_l3_norm(act, j, par):
            wait(act, l3["spike_a0"], j * 1)
            for k in range(2):
                s = j * 2 + k
                act.wait_ge(gn_done, 8)
                nc.scalar.activation(xn3[:, k * T:(k + 1) * T], x_of(s), ACT.Relu, bias=gn_shift[:, bass.ds(s, 1)],
                                     scale=gn_rstd[:, bass.ds(s, 1)]).then_inc(l3["norm"], 1)

        def dve_l3_spike(dve, j, par):
            dve.wait_ge(l3["norm"], j * 2 + 2)
            nc.vector.tensor_scalar(rounded[:, :], xn3[:, :], 4.0, ROUND, ALU.min, ALU.add).then_inc(l3["spike_a0"], 1)
            dve.wait_ge(l3["spike_a0"], j + 1)
            nc.vector.tensor_scalar(spike_in[par][:, :], rounded[:, :], ROUND, None, ALU.subtract).then_inc(l3["spike"], 1)

        def pe_l3_qkv(pe, j, par):
            pe.wait_ge(l3["spike"], j + 1)
            wait(pe, l3["relu"], j * 3)
            for i in range(3):
                for part in range(3):
                    last = nc.tensor.matmul(bank[i][0:C, :], w3_parts[:, part, i * C:(i + 1) * C], spike_in[par][:, :],
                                            start=(part == 0), stop=(part == 2))
                last.then_inc(l3["qkv"], 1)

        def act_l3_relu(act, j, par):
            for i in range(3):
                act.wait_ge(l3["qkv"], j * 3 + (i + 1))
                if i == 0:
                    wait(act, l3["round_a"], j - 1)
                nc.scalar.activation(relu3[par][:, i, :], bank[i][0:C, :], ACT.Relu, bias=bn_b[:, i:i + 1],
                                     scale=bn_s4[:, i:i + 1]).then_inc(l3["relu"], 1)

        def dve_l3_round(dve, j, par):
            dve.wait_ge(l3["relu"], j * 3 + 3)
            nc.vector.tensor_scalar(relu3[par][:, :, :], relu3[par][:, :, :], 4.0, ROUND, ALU.min, ALU.add).then_inc(l3["round_a"], 1)
            dve.wait_ge(l3["round_a"], j + 1)
            wait(dve, l3["attn"], j - 1)
            nc.vector.tensor_scalar(qkv3[par][:, :, :], relu3[par][:, :, :], ROUND, None, ALU.subtract).then_inc(l3["round"], 1)

        turned = bank[3][:, :].bitcast(BF16)[:, 0:8 * C].rearrange("t (k b c) -> t k b c", k=2, c=C)

        def pe_l3_turn(pe, j, par):
            pe.wait_ge(l3["round"], j + 1)
            wait(pe, l3["turned_sb"], j)
            for k in range(2):
                for b in range(4):
                    last = nc.tensor.transpose(turned[:, k, b, :], qkv3[par][:, 1 + k, b * 128:(b + 1) * 128], ident_b[:, :])
            last.then_inc(l3["turned"], 1)

        def act_l3_turn(act, j, par):
            act.wait_ge(l3["turned"], j + 1)
            wait(act, l3["kv"], j)
            nc.scalar.copy(kvT[:, :, :, :], turned).then_inc(l3["turned_sb"], 1)

        def pe_l3_kv(pe, j, par):
            pe.wait_ge(l3["turned_sb"], j + 1)
            wait(pe, l3["kv_step"], j * 4)
            for b in range(4):
                last = nc.tensor.matmul(bank[4][0:C, b // 2 * C:(b // 2 + 1) * C], kvT[:, 0, b, :], kvT[:, 1, b, :],
                                        start=(b % 2 == 0), stop=(b % 2 == 1))
            last.then_inc(l3["kv"], 1)

        def dve_l3_kv(dve, j, par):
            dve.wait_ge(l3["kv"], j + 1)
            n = [0]

            def step(ins):
                n[0] += 1
                ins.then_inc(l3["kv_step"], 1)
                dve.wait_ge(l3["kv_step"], j * 4 + n[0])

            step(nc.vector.tensor_tensor(kv[:, :, :], bank[4][0:C, 0:2 * C].rearrange("d (b e) -> d b e", b=2),
                                         const("head_blocks", C).unsqueeze(1).broadcast_to([C, 2, C]), ALU.mult))
            wait(dve, l3["attn"], j)
            step(nc.vector.tensor_copy(kv_parts[:, 0, :, :], kv[:, :, :]))
            step(nc.vector.tensor_tensor(kv_lo[:, :, :], kv[:, :, :], kv_parts[:, 0, :, :], ALU.subtract))
            nc.vector.tensor_copy(kv_parts[:, 1, :, :], kv_lo[:, :, :]).then_inc(l3["kv_step"], 1)

        def pe_l3_attn(pe, j, par):
            pe.wait_ge(l3["kv_step"], j * 4 + 4)
            wait(pe, l3["relu_a"], j)
            for b in range(2):
                for part in range(2):
                    last = nc.tensor.matmul(bank[5][0:C, b * T:(b + 1) * T], kv_parts[:, part, b, :],
                                            qkv3[par][:, 0, b * T:(b + 1) * T], start=(part == 0), stop=(part == 1))
            last.then_inc(l3["attn"], 1)

        def act_l3_attn(act, j, par):
            act.wait_ge(l3["attn"], j + 1)
            wait(act, l3["round_b"], j)
            nc.scalar.activation(relu_a[:, :], bank[5][0:C, :], ACT.Relu, scale=ATTN_SCALE).then_inc(l3["relu_a"], 1)

        def dve_l3_attn(dve, j, par):
            dve.wait_ge(l3["relu_a"], j + 1)
            wait(dve, l3["spike_a"], j)
            nc.vector.tensor_scalar(rounded_a[:, :], relu_a[:, :], 4.0, ROUND, ALU.min, ALU.add).then_inc(l3["round_b"], 1)
            dve.wait_ge(l3["round_b"], j + 1)
            wait(dve, l3["proj"], j)
            nc.vector.tensor_scalar(spike_a[:, :], rounded_a[:, :], ROUND, None, ALU.subtract).then_inc(l3["spike_a"], 1)

        def pe_l3_proj(pe, j, par):
            pe.wait_ge(l3["spike_a"], j + 1)
            wait(pe, l3["y"], j)
            for part in range(3):
                last = nc.tensor.matmul(bank[6][0:C, :], w3_parts[:, part, 3 * C:4 * C], spike_a[:, :],
                                        start=(part == 0), stop=(part == 2))
            last.then_inc(l3["proj"], 1)

        def act_l3_proj(act, j, par):
            act.wait_ge(l3["proj"], j + 1)
            wait(act, l3["out"], j)
            nc.scalar.activation(y3[:, :], bank[6][0:C, :], ACT.Identity, bias=bn_b[:, 3:4],
                                 scale=bn_s4[:, 3:4]).then_inc(l3["y"], 1)

        def dve_l3_out(dve, j, par):
            dve.wait_ge(l3["y"], j + 1)
            wait(dve, stored[par], j * 8 - par * 8)
            nc.vector.tensor_tensor(y_out[par][:, :], y3[:, :], x_pair(j), ALU.add).then_inc(l3["out"], 1)

        def sp_l3(sp, j, par, nxt, nxt2):
            sp.wait_ge(l3["out"], j + 1)
            sp.dma_start(out[bass.ds(j * 2, 2)].rearrange("b c h w -> c b (h w)"),
                         y_out[par][:, :].rearrange("c (b t) -> c b t", b=2)).then_inc(stored[par], 16)

        def pe_l3(pe, j, par, nxt, nxt2):
            pe_l3_turn(pe, j, par)
            if nxt:
                pe_l3_qkv(pe, j + 1, 1 - par)
            pe_l3_kv(pe, j, par)
            pe_l3_attn(pe, j, par)
            pe_l3_proj(pe, j, par)

        def act_l3(act, j, par, nxt, nxt2):
            act_l3_turn(act, j, par)
            if nxt:
                act_l3_relu(act, j + 1, 1 - par)
            act_l3_attn(act, j, par)
            if nxt2:
                act_l3_norm(act, j + 2, par)
            act_l3_proj(act, j, par)

        def dve_l3(dve, j, par, nxt, nxt2):
            dve_l3_kv(dve, j, par)
            if nxt:
                dve_l3_round(dve, j + 1, 1 - par)
            dve_l3_attn(dve, j, par)
            if nxt2:
                dve_l3_spike(dve, j + 2, par)
            dve_l3_out(dve, j, par)

        @block.vector
        def _(dve):
            dve.wait_ge(x_in, 16 * N_X)
            with dve.Fori(0, B) as s:
                dve_stats(dve, 0, s)
            dve_prepare(dve)
            dve_attention(dve, L0)
            dve_attention(dve, L1)
            dve_group_norm(dve, 2)
            dve_prepare_late(dve)
            dve_depthwise(dve, 0, 0)
            pair_loop(dve, dve_l2)
            dve_group_norm(dve, 3)
            dve_l3_spike(dve, 0, 0)
            dve_l3_round(dve, 0, 0)
            dve_l3_spike(dve, 1, 1)
            pair_loop(dve, dve_l3)

        @block.tensor
        def _(pe):
            pe_prepare(pe)
            pe.wait_ge(dve_prep, done["layer0"])
            pe_attention(pe, L0)
            pe_attention(pe, L1)
            pe_group_norm(pe, 2)
            pe_prepare_late(pe)
            pe.wait_ge(dve_prep, done["late"])
            pe_pointwise(pe, 0, 0)
            pair_loop(pe, pe_l2)
            pe_group_norm(pe, 3)
            pe_l3_qkv(pe, 0, 0)
            pair_loop(pe, pe_l3)

        @block.scalar
        def _(act):
            act.wait_ge(dve_prep, done["layer0"])
            act.wait_ge(w_in, W_IN)
            act_attention(act, L0)
            act_attention(act, L1)
            act.wait_ge(dve_prep, done["late"])
            act_pad(act, 0, 0)
            act_pad(act, 1, 1)
            pair_loop(act, act_l2)
            act_l3_norm(act, 0, 0)
            act_l3_norm(act, 1, 1)
            act_l3_relu(act, 0, 0)
            pair_loop(act, act_l3)

        @block.gpsimd
        def _(pool):
            pool_attention(pool, L0)
            pool_attention(pool, L1)
            pool_group_norm(pool, 2)
            nc.gpsimd.tensor_scalar(bn_t[:, :], bn[:, 3, :], EPS, None, ALU.add).then_inc(pool_prep, 1)
            pool.wait_ge(pool_prep, 1)
            nc.gpsimd.tensor_tensor(bn_r[:, :], bn_t[:, :], const("minus_half", C).broadcast_to([C, 4]),
                                    ALU.pow).then_inc(pool_prep, 1)
            pool_group_norm(pool, 3)

        @block.sync
        def _(sp):
            pair_loop(sp, sp_l3)
            for one in stored:
                sp.wait_ge(one, 16 * PAIRS // 2)


def kernel(**inputs):
    import concourse.bacc as bacc
    from concourse.bass_utils import run_bass_kernel_spmd

    nc = bacc.Bacc("TRN2", target_bir_lowering=False, num_devices=1)
    arrays, aps = {}, {}
    for name, value in [*inputs.items(), ("consts", constants())]:
        if name == "L1_conv_pos_emb":
            value = np.asarray(value)[::-1, ::-1]
        value = np.ascontiguousarray(value)
        arrays[f"in_{name}"] = value
        aps[name] = nc.dram_tensor(f"in_{name}", value.shape, mybir.dt.from_np(value.dtype), kind="ExternalInput").ap()
    out = nc.dram_tensor("out_0_dram", (B, C, SIDE, SIDE), F32, kind="ExternalOutput").ap()
    build(nc, aps, out)
    return run_bass_kernel_spmd(nc, [arrays], core_ids=[0]).results[0]["out_0_dram"]
```

```python
from contextlib import ExitStack

import numpy as np

import concourse.bass as bass
from concourse import mybir

F32 = mybir.dt.float32
BF16 = mybir.dt.bfloat16
I32 = mybir.dt.int32
ALU = mybir.AluOpType
ACT = mybir.ActivationFunctionType
AX = mybir.AxisListType

B, C, SIDE = 16, 96, 16
T = SIDE * SIDE
WIN, WT, NW = 8, 64, 4
HEADS, NP, NU, NH = 12, 3, 2, 2
GROUP = 3
EPS = 1e-5
NEG = -1e30
ROUND = 12582912.0
REL = (2 * WIN - 1) ** 2
PE_TAPS = 4
BIAS_KEYS = 13
REL_LO = 113
HD0, HD1 = C // HEADS, 32
INNER = HEADS * HD1

CONSTS = {}
_at = 0
for _name, _n in (("ident", 128), ("qmask0", 6), ("qmask1", 2), ("group_mean", C), ("ones", 128),
                  ("head_blocks", C), ("masks", 4 * WT), ("rows", 2), ("minus_half", 1), ("perm", 4 * 128)):
    CONSTS[_name] = (_at, _at + _n)
    _at += _n
N_CONST = _at


def constants():
    c = np.zeros((128, N_CONST), np.float32)
    p = np.arange(128)

    def put(name, value, rows=128):
        a, b = CONSTS[name]
        c[:rows, a:b] = value

    put("ident", np.eye(128))
    put("qmask0", (p[:, None] % 64 // HD0 == np.arange(NP * NH)) * np.float32(HD0 ** -0.5))
    put("qmask1", (p[:, None] // HD1 % 2 == np.arange(2)) * np.float32(HD1 ** -0.5))
    ch = np.arange(C)
    put("group_mean", (ch[:, None] // GROUP == ch[None] // GROUP) / np.float32(GROUP * T), C)
    put("ones", 1.0)
    put("head_blocks", ch[:, None] // 12 == ch[None] // 12, C)
    tok = np.arange(WT)
    r, q = tok // WIN >= WIN // 2, tok % WIN >= WIN // 2
    ud, lr = r[:, None] != r[None], q[:, None] != q[None]
    m = np.zeros((2, WT, NW, WT), bool)
    for w in range(NW):
        m[:, :, w] |= (ud & (w // 2 == 1)) | (lr & (w % 2 == 1))
    put("masks", m.reshape(128, NW * WT) * np.float32(NEG))
    perm = np.zeros((WT, NW, NH, WT))
    for w in range(NW):
        src = (tok // WIN + w // 2 * 4) % WIN * WIN + (tok % WIN + w % 2 * 4) % WIN
        perm[WT - 1 - src, w, :, tok] = 1
    put("perm", perm.reshape(WT, NW * 128), WT)
    put("minus_half", -0.5)
    put("rows", np.stack([p, p + REL_LO], 1))
    return c


class Attention:

    def __init__(self, n, hd):
        self.n, self.hd = n, hd
        self.wide = hd == HD1
        self.slots = 2 if self.wide else NP * NH
        self.qk_uses = 3 if self.wide else 2
        self.v_uses = 2 if self.wide else 1
        self.pieces = 6 if self.wide else 4
        self.adds = self.pieces
        self.uses_at = [(1, 3, 4), (1, 4, 5), (2, 0, 2), (2, 2, 3)] if self.wide else \
            [(1, 0, 0), (1, 2, 3), (2, 0, 1), (2, 1, 2)]
        self.evacs_at = [[(1, 2, 0, 4)], [(1, 3, 0, 4)], [(1, 4, 0, 4)], [(2, 0, 0, 4), (2, 1, 0, 4)]] if self.wide else \
            [[(1, 0, 3, 6), (1, 1, 0, 2)], [], [(1, 2, 0, 4)], [(2, 0, 0, 3)]]


class AttentionSems:

    def __init__(self, sem, n):
        self.xn_ready = sem(f"l{n}_xn_ready")
        self.qk_ready = sem(f"l{n}_qk_ready")
        self.v_ready = sem(f"l{n}_v_ready")
        self.evac_a = sem(f"l{n}_evac_a")
        self.evac_b = sem(f"l{n}_evac_b")
        self.scores_ready = sem(f"l{n}_scores_ready")
        self.biased = sem(f"l{n}_biased")
        self.maxed = sem(f"l{n}_maxed")
        self.shifted = sem(f"l{n}_shifted")
        self.exped = sem(f"l{n}_exped")
        self.summed = sem(f"l{n}_summed")
        self.inverted = sem(f"l{n}_inverted")
        self.scaled = sem(f"l{n}_scaled")
        self.transposed = sem(f"l{n}_transposed")
        self.probsT_sb = sem(f"l{n}_probsT_sb")
        self.pv_done = sem(f"l{n}_pv_done")
        self.heads_sb = sem(f"l{n}_heads_sb")
        self.out_ready = sem(f"l{n}_out_ready")
        self.y_ready = sem(f"l{n}_y_ready")
        self.residual = sem(f"l{n}_residual")


def build(nc, a, out):
    ctx = ExitStack()
    with ctx:
        ctx.enter_context(nc.allow_non_contiguous_dma(reason="small weights and tables, loaded once"))

        def sb(name, shape, dt=F32):
            return ctx.enter_context(nc.sbuf_tensor(name, shape, dt))

        def sem(name):
            return ctx.enter_context(nc.semaphore(name))

        bank = [ctx.enter_context(nc.psum_tensor(f"bank{i}", [128, 512], F32)) for i in range(8)]
        ps_scores = bank[0:2]
        ps_probsT = bank[2:4]
        ps_heads = bank[4]
        ps_qkv = bank[5:7]
        ps_mix = bank[7]

        x = sb("x", [C, B * T])
        cst = sb("cst", [128, N_CONST])

        def const(name, rows=128):
            lo, hi = CONSTS[name]
            return cst[0:rows, lo:hi]

        ident = const("ident")
        ones = const("ones")
        w0_raw = sb("w0_raw", [C, 3, C])
        w0T = sb("w0T", [128, 2 * 128 + C])
        b0_qk = sb("b0_qk", [128, 2])
        b0_q = sb("b0_q", [128, NP * NH])
        b0_v = sb("b0_v", [128, 2 * C])
        p0_raw = sb("p0_raw", [C, C])
        p0T = sb("p0T", [128, C])
        p0_b = sb("p0_b", [C, 1])
        rel_bc = sb("rel_bc", [REL_LO, WT * WT], I32)
        onehot = sb("onehot", [REL_LO, 2, WT * WT], BF16)
        table = sb("table", [REL_LO, 2, HEADS])
        table_rest = sb("table_rest", [REL_LO, 2, 2, HEADS])
        table_parts = sb("table_parts", [REL_LO, 2, 3, HEADS], BF16)
        bias0 = sb("bias0", [128, NP * NU, WT])
        w1 = sb("w1", [128, 3 * INNER])
        p1 = sb("p1", [128, NP, C])
        p1_b = sb("p1_b", [C, 1])
        pos = sb("pos", [WT, WT])
        bias1 = sb("bias1", [128, NW, WT])
        dw = sb("dw", [C, 9])
        dw_u = sb("dw_u", [C, 9])
        pw_raw = sb("pw_raw", [C, C])
        pw_u = sb("pw_u", [C, C])
        pw_abs = sb("pw_abs", [C, 1])
        pwT = sb("pwT", [C, C])
        tapT = sb("tapT", [C, PE_TAPS, C])
        q_mean = sb("q_mean", [C, 4])
        w3_raw = sb("w3_raw", [C, 4, C])
        w3_rest = sb("w3_rest", [C, 2, 4 * C])
        w3_parts = sb("w3_parts", [128, 3, 4 * C], BF16)
        bn = sb("bn", [C, 4, 4])
        bn_r = sb("bn_r", [C, 4])
        bn_s = sb("bn_s", [C, 4])
        bn_s4 = sb("bn_s4", [C, 4])
        bn_t = sb("bn_t", [C, 4])
        bn_m = sb("bn_m", [C, 4])
        bn_b = sb("bn_b", [C, 4])
        ident_b = sb("ident_b", [C, C], BF16)
        stats = sb("stats", [C, 6 * B])
        gn_sq = sb("gn_sq", [C, B])
        gn_sum = sb("gn_sum", [C, B])
        gn_shift = sb("gn_shift", [C, B])
        gn_in = sb("gn_in", [C, B])
        gn_m2 = sb("gn_m2", [C, B // 2])
        gn_var = sb("gn_var", [C, B // 2])
        gn_negmean = sb("gn_negmean", [C, B])
        gn_mean = sb("gn_mean", [C, B])
        gn_veps = sb("gn_veps", [C, B // 2])
        gn_rstd = sb("gn_rstd", [C, B])

        xn = [sb(f"xn{i}", [128, NW, WT]) for i in range(2)]
        q0 = [sb(f"q0_{i}", [128, NW, NP * NH, WT]) for i in range(2)]
        k0 = [sb(f"k0_{i}", [128, NU, T + WT]) for i in range(2)]
        v0 = [sb(f"v0_{i}", [128, NW * NP, NH, NH * NU * HD0]) for i in range(2)]
        q1 = [sb(f"q1_{i}", [128, 3, NW, 2, WT]) for i in range(2)]
        k1 = [sb(f"k1_{i}", [128, NU, NP, T + WT]) for i in range(2)]
        v1 = [sb(f"v1_{i}", [128, NW * NP, NH, NU * HD1]) for i in range(2)]
        probs = [sb(f"probs{i}", [128, NP * NU, WT]) for i in range(4)]
        row_max = [sb(f"row_max{i}", [128, NP * NU]) for i in range(4)]
        probsT = [sb(f"probsT{i}", [128, NP * 128]) for i in range(2)]
        row_sum = [sb(f"row_sum{i}", [128, NP * NU]) for i in range(4)]
        inv_sum = [sb(f"inv_sum{i}", [128, NP * NU]) for i in range(4)]
        heads0 = [sb(f"heads0_{i}", [128, T]) for i in range(2)]
        heads1 = [sb(f"heads1_{i}", [128, NP, T]) for i in range(2)]
        act_first_exp = sb("act_first_exp", [128, 1])
        y_attn = sb("y_attn", [C, T])
        pad = [sb(f"pad{i}", [C, SIDE + 2, 2, SIDE + 2]) for i in range(2)]
        conv = [sb(f"conv{i}", [C, 2 * SIDE, SIDE]) for i in range(2)]
        xn3 = sb("xn3", [C, 2 * T])
        spike_in = sb("spike_in", [128, 2 * T], BF16)
        relu3 = [sb(f"relu3_{i}", [C, 3, 2 * T]) for i in range(2)]
        qkv3 = [sb(f"qkv3_{i}", [C, 3, 2 * T], BF16) for i in range(2)]
        relu_a = sb("relu_a", [C, 2 * T])
        rounded_a = sb("rounded_a", [C, 2 * T])
        rounded = sb("rounded", [C, 2 * T])
        kvT = sb("kvT", [128, 2, 4, C], BF16)
        kv = sb("kv", [C, 2, C])
        kv_lo = sb("kv_lo", [C, 2, C])
        kv_parts = sb("kv_parts", [C, 2, 2, C], BF16)
        spike_a = sb("spike_a", [128, 2 * T], BF16)
        y3 = sb("y3", [C, 2 * T])
        y_out = [sb(f"y_out{i}", [C, 2 * T]) for i in range(2)]

        x_in = sem("x_in")
        rel_in = sem("rel_in")
        pos_in = sem("pos_in")
        table_in = sem("table_in")
        w_in = sem("w_in")
        late_in = sem("late_in")
        first_exp = sem("first_exp")
        zeroed = sem("zeroed")
        dve_prep = sem("dve_prep")
        pe_prep = sem("pe_prep")
        pool_prep = sem("pool_prep")
        stat = sem("stat")
        gn_step = sem("gn_step")
        gn_pe = sem("gn_pe")
        gn_eps = sem("gn_eps")
        gn_done = sem("gn_done")

        L0, L1 = Attention(0, HD0), Attention(1, HD1)
        L0.s, L1.s = AttentionSems(sem, 0), AttentionSems(sem, 1)
        N_X = 4

        def wait(eng, s, v):
            if not (isinstance(v, int) and v <= 0):
                eng.wait_ge(s, v)

        def x_of(s, n=1):
            return x[:, bass.ds(s * T, n * T)]

        def image(ap):
            return ap.rearrange("c (y x) -> c y x", x=SIDE)

        def by_window(ap):
            return ap.rearrange("c (w t) -> c w t", w=NW)

        def window_pieces(L, w):
            wy, wx = w // 2, w % 2
            half = WIN // 2
            if not L.wide:
                y, xx = wy * WIN, wx * WIN
                return [(lambda i: i[:, y:y + WIN, xx:xx + WIN], lambda t: t)]

            def cols(i):
                return i.rearrange("c y (b x) -> c y b x", x=half)[:, :, 0:4:3] if wx else \
                    i[:, :, half:half + WIN].rearrange("c y (b x) -> c y b x", x=half)

            def tok(t):
                return t.rearrange("c y (b x) -> c y b x", x=half)

            if not wy:
                return [(lambda i: cols(i[:, half:half + WIN]), tok)]
            return [(lambda i, k=k: cols(i[:, k * 3 * half:(k * 3 + 1) * half]),
                     lambda t, k=k: tok(t[:, k * half:(k + 1) * half])) for k in range(2)]

        block = ctx.enter_context(nc.Block())

        @block.sync
        def _(sp):
            sp.dma_start(rel_bc[:, :], a["L0_conv_rel_index"].rearrange("q k -> (q k)").unsqueeze(0)
                         .broadcast_to([REL_LO, WT * WT])).then_inc(rel_in, 16)
            n = B // N_X
            for i in range(N_X):
                sp.dma_start(x[:, i * n * T:(i + 1) * n * T].rearrange("c (b t) -> c b t", t=T),
                             a["x"][i * n:(i + 1) * n].rearrange("b c h w -> c b (h w)")).then_inc(x_in, 16)
            flipped = a["L1_conv_pos_emb"]
            for i in range(WIN):
                src = bass.AP(tensor=flipped.tensor, offset=flipped.offset + i * (2 * WIN - 1),
                              ap=[[1, WIN], [2 * WIN - 1, WIN], [1, WIN]])
                sp.dma_start(pos[i * WIN:(i + 1) * WIN, :].rearrange("q (y x) -> q y x", x=WIN), src).then_inc(pos_in, 16)

        def table_loads():
            yield cst[:, :], a["consts"]
            yield table[:, 0, :], a["L0_conv_rpb_table"][0:REL_LO]
            yield table[0:REL - REL_LO, 1, :], a["L0_conv_rpb_table"][REL_LO:REL]

        def first_loads():
            yield w0_raw[:, :, :], a["L0_conv_qkv_w"].rearrange("(t o) i -> o t i", o=C)
            bias_qk = a["L0_conv_qkv_b"].rearrange("(t p u e) -> u p e t", t=3, p=NP, u=NU)[:, :, :, 0:2]
            for u in range(NU):
                for p in range(NP + 1):
                    at_ = u * 64 + p * NH * HD0
                    yield b0_qk[at_:at_ + NH * HD0, :], bias_qk[u, p % NP]
            for k in range(2):
                yield b0_v[:, k * C:(k + 1) * C], a["L0_conv_qkv_b"][2 * C:3 * C].unsqueeze(0).broadcast_to([128, C])
            for h in range(NH):
                for u in range(NU):
                    yield (p0_raw[:, :].rearrange("o (p h u d) -> o h u p d", p=NP, h=NH, u=NU)[:, h, u],
                           a["L0_conv_proj_w"].rearrange("o (p u h d) -> o h u p d", p=NP, h=NH, u=NU)[:, h, u])
            yield p0_b[:, :], a["L0_conv_proj_b"].unsqueeze(1)

        def late_loads():
            yield w1[0:C, :], a["L1_conv_w_qkv"]
            for h in range(NH):
                for u in range(NU):
                    yield (p1[(h * NU + u) * HD1:(h * NU + u + 1) * HD1, :, :],
                           a["L1_conv_w_out"].rearrange("(p u h d) c -> h u d p c", p=NP, u=NU, h=NH)[h, u])
            yield p1_b[:, :], a["L1_conv_b_out"].unsqueeze(1)
            yield dw[:, :], a["L2_conv_w_dw"].rearrange("c a y x -> c (a y x)")
            yield pw_raw[:, :], a["L2_conv_w_pw"].rearrange("o i y x -> o (i y x)")
            for j, name in enumerate("qkvp"):
                yield w3_raw[:, j, :], a[f"L3_conv_{name}_w"]
                for i, what in enumerate(("gamma", "beta", "mean", "var")):
                    yield bn[:, i, j:j + 1], a[f"L3_conv_{name}_{what}"].unsqueeze(1)

        TABLE_IN, W_IN, LATE_IN = (16 * len(list(each())) for each in (table_loads, first_loads, late_loads))

        @block.scalar
        def _(act):
            for dst, src in table_loads():
                act.dma_start(dst, src).then_inc(table_in, 16)
            for dst, src in first_loads():
                act.dma_start(dst, src).then_inc(w_in, 16)
            for dst, src in late_loads():
                act.dma_start(dst, src).then_inc(late_in, 16)

        PE_POS, PE_W0, PE_P0, PE_W3, PE_PW_SUM, PE_BIAS, PE_PW = 1, 2, 3, 6, 7, 4, 11
        BIAS_COUNTS = [PE_BIAS, PE_BIAS + 1, PE_PW_SUM + 1, PE_PW_SUM + 2, PE_PW_SUM + 3]
        done = {}
        zero_buffers = [w0T[:, :], p0T[C:, :], *(t[C:, :, :] for t in xn), *(t[C:, :] for t in heads0),
                        *(t[:, :, :] for t in k0),
                        *(t[:, :, :, :] for t in v0), *(t[:, :, :, :] for t in v1),
                        *(t[:, :, :, :] for t in k1), w1[C:, :],
                        w3_parts[C:, :, :], spike_in[C:, :], spike_a[C:, :],
                        *(t[:, :, :, :] for t in pad)]

        def pool_prepare(pool):
            for i, t in enumerate(zero_buffers):
                nc.gpsimd.memset(t, 0.0).then_inc(zeroed, 1)
                pool.wait_ge(zeroed, i + 1)

        def pool_prepare_late(pool):
            pool.wait_ge(late_in, LATE_IN)
            nc.gpsimd.tensor_scalar(bn_t[:, :], bn[:, 3, :], EPS, None, ALU.add).then_inc(pool_prep, 1)
            pool.wait_ge(pool_prep, 1)
            nc.gpsimd.tensor_tensor(bn_r[:, :], bn_t[:, :], const("minus_half", C).broadcast_to([C, 4]),
                                    ALU.pow).then_inc(pool_prep, 1)

        def dve_prepare(dve):
            count = [0]

            def step(ins):
                count[0] += 1
                ins.then_inc(dve_prep, 1)
                dve.wait_ge(dve_prep, count[0])

            dve.wait_ge(table_in, TABLE_IN)
            for t, n in ((0, REL_LO), (1, REL - REL_LO)):
                step(nc.vector.tensor_copy(table_parts[0:n, t, 0, :], table[0:n, t, :]))
                step(nc.vector.tensor_tensor(table_rest[0:n, 0, t, :], table[0:n, t, :], table_parts[0:n, t, 0, :], ALU.subtract))
                step(nc.vector.tensor_copy(table_parts[0:n, t, 1, :], table_rest[0:n, 0, t, :]))
                step(nc.vector.tensor_tensor(table_rest[0:n, 1, t, :], table_rest[0:n, 0, t, :], table_parts[0:n, t, 1, :], ALU.subtract))
                step(nc.vector.tensor_copy(table_parts[0:n, t, 2, :], table_rest[0:n, 1, t, :]))
            dve.wait_ge(rel_in, 16)
            lo = CONSTS["rows"][0]
            for t in range(2):
                step(nc.vector.tensor_scalar(onehot[:, t, :], rel_bc[:, :], cst[0:REL_LO, lo + t:lo + t + 1], None,
                                             ALU.is_equal))
            done["onehot"] = count[0]
            dve.wait_ge(x_in, 16 * N_X)
            with dve.Fori(0, B // 4) as i:
                dve_stats(dve, 0, i * 4, 4)
            dve.wait_ge(pe_prep, PE_POS)
            step(nc.vector.tensor_tensor(bias1[:, :, :], ps_mix[:, 0:NW * WT].rearrange("p (w k) -> p w k", w=NW),
                                         const("masks").rearrange("p (w k) -> p w k", w=NW), ALU.add))
            dve.wait_ge(zeroed, len(zero_buffers))
            dve.wait_ge(pe_prep, PE_W0)
            for u in range(NU):
                step(nc.vector.tensor_copy(
                    w0T[0:C, 0:256].rearrange("c (t u r) -> c u t r", t=2, u=NU)[:, u, :, 0:48].rearrange("c t (p e) -> c t p e", p=NP),
                    bank[0][0:C, 0:2 * C].rearrange("c (t p u e) -> c u t p e", t=2, p=NP, u=NU)[:, u]))
            step(nc.vector.tensor_copy(w0T[0:C, 256:], bank[0][0:C, 2 * C:3 * C]))
            dve.wait_ge(pe_prep, PE_P0)
            step(nc.vector.tensor_copy(p0T[0:C, :], bank[1][0:C, 0:C]))
            dve.wait_ge(w_in, W_IN)
            step(nc.vector.tensor_scalar(b0_q[:, :], const("qmask0"), b0_qk[:, 0:1], None, ALU.mult))
            dve_group_norm(dve, 0, 0)

            def bias_banks(first, end):
                for i in range(first, end):
                    dve.wait_ge(pe_prep, BIAS_COUNTS[i])
                    k0_ = i * BIAS_KEYS
                    n = min(BIAS_KEYS, WT - k0_)
                    for h in range(NH):
                        src = bank[2 + i][0:WT, 0:n * 3 * HEADS] \
                            .rearrange("q (k part g h) -> q h g k part", k=n, part=3, h=NH)[:, h]
                        step(nc.vector.tensor_reduce(bias0[h * WT:(h + 1) * WT, :, k0_:k0_ + n], src, AX.X, ALU.add))

            bias_banks(0, 2)

            dve.wait_ge(late_in, LATE_IN)
            step(nc.vector.tensor_reduce(pw_abs[:, :], pw_raw[:, :], AX.X, ALU.add, apply_absolute_value=True))
            done["pw_abs"] = count[0]
            step(nc.vector.tensor_reduce(q_mean[:, 0:1], dw[:, :], AX.X, ALU.add, apply_absolute_value=True))
            step(nc.vector.tensor_scalar(q_mean[:, 0:1], q_mean[:, 0:1], 1.0 / 9, 1e-5, ALU.mult, ALU.max))
            step(nc.vector.reciprocal(q_mean[:, 1:2], q_mean[:, 0:1]))
            step(nc.vector.tensor_scalar(dw_u[:, :], dw[:, :], q_mean[:, 1:2], ROUND, ALU.mult, ALU.add))
            step(nc.vector.tensor_scalar(dw_u[:, :], dw_u[:, :], ROUND, 1.0, ALU.subtract, ALU.min))
            step(nc.vector.tensor_scalar(dw_u[:, :], dw_u[:, :], -1.0, None, ALU.max))
            step(nc.vector.tensor_tensor(dw_u[:, :], dw_u[:, :], dw[:, :], ALU.subtract))
            step(nc.vector.tensor_tensor(dw_u[:, :], dw_u[:, :], dw[:, :], ALU.add))
            step(nc.vector.tensor_scalar(dw_u[:, :], dw_u[:, :], q_mean[:, 0:1], None, ALU.mult))
            dve.wait_ge(pool_prep, 2)
            step(nc.vector.tensor_tensor(bn_s[:, :], bn_r[:, :], bn[:, 0, :], ALU.mult))
            step(nc.vector.tensor_scalar(bn_s4[:, :], bn_s[:, :], 0.25, None, ALU.mult))
            step(nc.vector.tensor_tensor(bn_m[:, :], bn_s[:, :], bn[:, 2, :], ALU.mult))
            step(nc.vector.tensor_tensor(bn_b[:, :], bn[:, 1, :], bn_m[:, :], ALU.subtract))
            step(nc.vector.tensor_copy(ident_b[:, :], cst[0:C, 0:C]))
            dve.wait_ge(pe_prep, PE_W3)
            w3 = bank[1][0:C, C:5 * C]
            step(nc.vector.tensor_copy(w3_parts[0:C, 0, :], w3))
            step(nc.vector.tensor_tensor(w3_rest[:, 0, :], w3, w3_parts[0:C, 0, :], ALU.subtract))
            step(nc.vector.tensor_copy(w3_parts[0:C, 1, :], w3_rest[:, 0, :]))
            step(nc.vector.tensor_tensor(w3_rest[:, 1, :], w3_rest[:, 0, :], w3_parts[0:C, 1, :], ALU.subtract))
            step(nc.vector.tensor_copy(w3_parts[0:C, 2, :], w3_rest[:, 1, :]))
            dve.wait_ge(pe_prep, PE_PW_SUM)
            step(nc.vector.tensor_scalar(q_mean[:, 2:3], bank[0][0:C, 0:1], 1.0 / (C * C), 1e-5, ALU.mult, ALU.max))
            step(nc.vector.reciprocal(q_mean[:, 3:4], q_mean[:, 2:3]))
            step(nc.vector.tensor_scalar(pw_u[:, :], pw_raw[:, :], q_mean[:, 3:4], ROUND, ALU.mult, ALU.add))
            step(nc.vector.tensor_scalar(pw_u[:, :], pw_u[:, :], ROUND, 1.0, ALU.subtract, ALU.min))
            step(nc.vector.tensor_scalar(pw_u[:, :], pw_u[:, :], -1.0, None, ALU.max))
            step(nc.vector.tensor_tensor(pw_u[:, :], pw_u[:, :], pw_raw[:, :], ALU.subtract))
            step(nc.vector.tensor_tensor(pw_u[:, :], pw_u[:, :], pw_raw[:, :], ALU.add))
            step(nc.vector.tensor_scalar(pw_u[:, :], pw_u[:, :], q_mean[:, 2:3], None, ALU.mult))
            done["pw_u"] = count[0]
            bias_banks(2, 5)
            dve.wait_ge(pe_prep, PE_PW)
            step(nc.vector.tensor_copy(pwT[:, :], bank[0][0:C, C:2 * C]))
            for t in range(PE_TAPS):
                tap = 9 - PE_TAPS + t
                step(nc.vector.tensor_scalar(tapT[:, t, :], pwT[:, :], dw_u[:, tap:tap + 1], None, ALU.mult))
            done["all"] = count[0]

        def pe_prepare(pe):
            pe.wait_ge(table_in, TABLE_IN)
            pe.wait_ge(pos_in, 16 * WIN)
            for w in range(NW):
                for yb in range(2):
                    for xb in range(2):
                        def block44(ap, i, j):
                            return ap.rearrange("q (yb y xb x) -> q yb y xb x", yb=2, xb=2, y=4)[:, i, :, j, :]
                        last = nc.tensor.matmul(block44(ps_mix[:, w * WT:(w + 1) * WT], yb, xb),
                                                const("perm", WT)[:, w * 128:(w + 1) * 128],
                                                block44(pos[:, :], yb ^ (w // 2), xb ^ (w % 2)), start=True, stop=True)
            last.then_inc(pe_prep, 1)
            pe.wait_ge(w_in, W_IN)
            for t in range(3):
                last = nc.tensor.transpose(bank[0][0:C, t * C:(t + 1) * C], w0_raw[:, t, :], ident[0:C, 0:C])
            last.then_inc(pe_prep, 1)
            nc.tensor.transpose(bank[1][0:C, 0:C], p0_raw[:, :], ident[0:C, 0:C]).then_inc(pe_prep, 1)
            pe.wait_ge(dve_prep, done["onehot"])
            for i, k0_ in enumerate(range(0, WT, BIAS_KEYS)):
                if i == 2:
                    pe_group_norm(pe, 0, 0)
                    pe_late_weights(pe)
                for k in range(k0_, min(k0_ + BIAS_KEYS, WT)):
                    for t, n in ((0, REL_LO), (1, REL - REL_LO)):
                        sel = onehot[0:n, t, :].rearrange("r (q k) -> r q k", k=WT)[:, :, k]
                        last = nc.tensor.matmul(bank[2 + i][0:WT, (k - k0_) * 3 * HEADS:(k - k0_ + 1) * 3 * HEADS],
                                                sel, table_parts[0:n, t, :, :], start=(t == 0), stop=(t == 1))
                last.then_inc(pe_prep, 1)
            pe.wait_ge(dve_prep, done["pw_u"])
            nc.tensor.transpose(bank[0][0:C, C:2 * C], pw_u[:, :], ident[0:C, 0:C]).then_inc(pe_prep, 1)

        def pe_late_weights(pe):
            pe.wait_ge(dve_prep, done["pw_abs"])
            for j in range(4):
                last = nc.tensor.transpose(bank[1][0:C, (1 + j) * C:(2 + j) * C], w3_raw[:, j, :], ident[0:C, 0:C])
            last.then_inc(pe_prep, 1)
            nc.tensor.matmul(bank[0][0:C, 0:1], ones[0:C, 0:C], pw_abs[:, :], start=True, stop=True).then_inc(pe_prep, 1)

        STEPS = 8
        SPAN = T // 2
        HB = B // 2

        def gn_count(layer, half):
            return layer * 2 + half + 1

        def dve_stats(dve, layer, s, n=1):
            for j in range(n):
                nc.vector.bn_stats(stats[:, bass.ds((s + j) * 6, 6)], x_of(s + j)).then_inc(stat, 1)

        def dve_group_norm(dve, layer, half):
            n = [(gn_count(layer, half) - 1) * STEPS]

            def step(ins):
                n[0] += 1
                ins.then_inc(gn_step, 1)
                dve.wait_ge(gn_step, n[0])

            dve.wait_ge(stat, layer * B + (half + 1) * HB)
            of = slice(half * HB, (half + 1) * HB)
            pairs = slice(half * B, (half + 1) * B)
            mean, m2 = (stats[:, :].rearrange("c (n k) -> c k n", k=3)[:, k, pairs] for k in (1, 2))
            sides = stats[:, :].rearrange("c (b e k) -> c e k b", e=2, k=3)
            step(nc.vector.tensor_tensor(gn_in[:, 0:HB], sides[:, 0, 1, of], sides[:, 1, 1, of], ALU.add))
            step(nc.vector.tensor_tensor(gn_sq[:, :], mean, mean, ALU.mult))
            step(nc.vector.scalar_tensor_tensor(gn_sum[:, :], gn_sq[:, :], float(SPAN), m2, ALU.mult, ALU.add))
            both = gn_sum[:, :].rearrange("c (b e) -> c e b", e=2)
            step(nc.vector.tensor_tensor(gn_in[:, HB:2 * HB], both[:, 0, :], both[:, 1, :], ALU.add))
            dve.wait_ge(gn_pe, gn_count(layer, half))
            step(nc.vector.tensor_scalar(gn_mean[:, of], ps_mix[0:C, 0:HB], float(SPAN), None, ALU.mult))
            step(nc.vector.tensor_scalar(gn_negmean[:, of], gn_mean[:, of], -1.0, None, ALU.mult))
            step(nc.vector.tensor_tensor(gn_m2[:, :], gn_mean[:, of], gn_mean[:, of], ALU.mult))
            step(nc.vector.tensor_tensor(gn_var[:, :], ps_mix[0:C, HB:2 * HB], gn_m2[:, :], ALU.subtract))

        def pool_group_norm(pool, layer, half):
            n = gn_count(layer, half)
            of = slice(half * HB, (half + 1) * HB)
            pool.wait_ge(gn_step, n * STEPS)
            nc.gpsimd.tensor_scalar(gn_veps[:, :], gn_var[:, :], EPS, None, ALU.add).then_inc(gn_eps, 1)
            pool.wait_ge(gn_eps, n)
            nc.gpsimd.tensor_tensor(gn_rstd[:, of], gn_veps[:, :], const("minus_half", C).broadcast_to([C, HB]),
                                    ALU.pow).then_inc(gn_done, 1)
            pool.wait_ge(gn_done, 2 * n - 1)
            nc.gpsimd.tensor_tensor(gn_shift[:, of], gn_negmean[:, of], gn_rstd[:, of], ALU.mult).then_inc(gn_done, 1)

        def gn_ready(eng, layer, half):
            eng.wait_ge(gn_done, 2 * gn_count(layer, half))

        def pe_group_norm(pe, layer, half):
            pe.wait_ge(gn_step, (gn_count(layer, half) - 1) * STEPS + 4)
            nc.tensor.matmul(ps_mix[0:C, 0:2 * HB], const("group_mean", C), gn_in[:, :], start=True, stop=True).then_inc(gn_pe, 1)

        def qkv_plan(L):
            if L.wide:
                return [("qk", 0, "act", 4), ("qk", 1, "dve", 4), ("qk", 2, "act", 4),
                        ("v", 0, "dve", 4), ("v", 1, "act", 4)]
            return [("q", 0, "act", L.slots), ("k", 0, "dve", 2), ("v", 0, "dve", 4)]

        def bank_of(L, parity, i):
            plan = qkv_plan(L)
            b = (i + parity * len(plan)) % 2
            before = sum(plan[j][3] for j in range(i) if (j + parity * len(plan)) % 2 == b)
            return b, before

        def evacs(L, parity):
            plan = qkv_plan(L)
            tot = [0, 0]
            for i, use in enumerate(plan):
                tot[(i + parity * len(plan)) % 2] += use[3]
            return tot

        def evac_before(L, s, parity, b):
            both = evacs(L, 0)[b] + evacs(L, 1)[b]
            if isinstance(s, int):
                return s // 2 * both + (evacs(L, 0)[b] if s % 2 else 0)
            return s.pair * both + (evacs(L, 0)[b] if parity else 0)

        class Sample:

            def __init__(self, pair, parity):
                self.pair, self.parity = pair, parity

            def __add__(self, n):
                return self.pair * 2 + (self.parity + n)

            __radd__ = __add__

            def __mul__(self, n):
                return self.pair * (2 * n) + self.parity * n

            __rmul__ = __mul__

            def shift(self, n):
                return Sample(self.pair + (self.parity + n) // 2, (self.parity + n) % 2)

        def moved(s, n):
            return s + n if isinstance(s, int) else s.shift(n)

        def parity(s):
            return s % 2 if isinstance(s, int) else s.parity

        def win_count(s, w):
            return s * NW + (w + 1)

        def evac_sem(L, par, i):
            return (L.s.evac_a, L.s.evac_b)[bank_of(L, par, i)[0]]

        def evacuated(eng, L, s, i):
            par = parity(s)
            b, before = bank_of(L, par, i)
            eng.wait_ge(evac_sem(L, par, i), evac_before(L, s, par, b) + before + qkv_plan(L)[i][3])

        def pe_qkv(pe, L, s, i0, i1):
            par = parity(s)
            if i0 == 0:
                pe.wait_ge(L.s.xn_ready, s * L.pieces + L.pieces)
            for i in range(i0, i1):
                kind, j, _, _ = qkv_plan(L)[i]
                b, before = bank_of(L, par, i)
                wait(pe, evac_sem(L, par, i), evac_before(L, s, par, b) + before)
                o = ps_qkv[b]
                if kind != "v":
                    w = w1 if L.wide else w0T
                    for half in {"q": (0,), "k": (1,), "qk": (0, 1)}[kind]:
                        col = half * (INNER if L.wide else 128) + j * 128
                        last = nc.tensor.matmul(o[:, half * T:(half + 1) * T], w[:, col:col + 128], xn[par][:, :, :],
                                                start=True, stop=True)
                    last.then_inc(L.s.qk_ready, 1)
                    continue
                n = HEADS * L.hd
                for k in (range(NW // 2) if not L.wide else (j,)):
                    at_ = 0 if L.wide else k * n
                    last = nc.tensor.matmul(o[:, at_:at_ + n], xn[par][:, 2 * k:2 * k + 2, :].rearrange("c w t -> c (w t)"),
                                            w1[:, 2 * n:3 * n] if L.wide else w0T[:, 256:], start=True, stop=True)
                last.then_inc(L.s.v_ready, 1)

        def pe_scores(pe, L, s, w, half):
            if half == 0:
                if w == 0:
                    for i in range(L.qk_uses):
                        evacuated(pe, L, s, i)
                wait(pe, L.s.biased, win_count(s, w - 2))
            par = parity(s)
            keys = slice(w * WT, (w + 2) * WT)
            for g in range(half * NP, (half + 1) * NP):
                p, u = g // NU, g % NU
                if L.wide:
                    q, k = q1[par][:, p, w, :, :], k1[par][:, u, p, keys]
                else:
                    q, k = q0[par][:, w, p * NH:(p + 1) * NH, :], k0[par][:, u, keys]
                last = nc.tensor.matmul(ps_scores[w % 2][:, g * WT:(g + 2) * WT], q, k, start=True, stop=True)
            if half:
                last.then_inc(L.s.scores_ready, 1)

        def pe_transpose(pe, L, s, w):
            pe.wait_ge(L.s.scaled, win_count(s, w))
            wait(pe, L.s.probsT_sb, win_count(s, w - 2))
            for p in range(NP):
                last = nc.tensor.transpose(ps_probsT[w % 2][:, p * 128:(p + 1) * 128], probs[w][:, 2 * p:2 * p + 2, :], ident)
            last.then_inc(L.s.transposed, 1)

        def pe_values(pe, L, s, w):
            pe.wait_ge(L.s.probsT_sb, win_count(s, w))
            pT = probsT[w % 2]
            if L.wide:
                if w % 2 == 0:
                    evacuated(pe, L, s, L.qk_uses + w // 2)
                wait(pe, L.s.heads_sb, win_count(s, w - 1))
                for p in range(NP):
                    for h in range(NH):
                        last = nc.tensor.matmul(ps_heads[h * WT:(h + 1) * WT, p * WT:(p + 1) * WT],
                                                v1[parity(s)][:, w * NP + p, h, :], pT[:, p * 128 + h * WT:p * 128 + (h + 1) * WT],
                                                start=True, stop=True)
            else:
                if w == 0:
                    evacuated(pe, L, s, L.qk_uses)
                    wait(pe, L.s.heads_sb, s * 1)
                v = v0[parity(s)]
                for p in range(NP):
                    for h in range(NH):
                        last = nc.tensor.matmul(ps_heads[p * 32:(p + 1) * 32, w * WT:(w + 1) * WT],
                                                v[:, (w % 2 * 2 + w // 2) * NP + p, h, :],
                                                pT[:, p * 128 + h * WT:p * 128 + (h + 1) * WT],
                                                start=(h == 0), stop=(h == NH - 1))
            last.then_inc(L.s.pv_done, 1)

        def pe_out(pe, L, s):
            pe.wait_ge(L.s.heads_sb, win_count(s, 3) if L.wide else s + 1)
            wait(pe, L.s.y_ready, s * 1)
            half_norms = gn_count(L.n, 1) + (isinstance(s, int) and s >= B - 3)
            pe.wait_ge(gn_step, half_norms * STEPS)
            o = ps_mix[0:C, 0:T]
            if L.wide:
                for p in range(NP):
                    last = nc.tensor.matmul(o, p1[:, p, :], heads1[parity(s)][:, p, :], start=(p == 0), stop=(p == NP - 1))
            else:
                last = nc.tensor.matmul(o, p0T[:, :], heads0[parity(s)][:, :], start=True, stop=True)
            last.then_inc(L.s.out_ready, 1)

        def act_exp(act, L, s, w):
            act.wait_ge(L.s.shifted, win_count(s, w))
            nc.scalar.activation(probs[w][:, :, :], probs[w][:, :, :], ACT.Exp).then_inc(L.s.exped, 1)

        def act_probsT(act, L, s, w):
            act.wait_ge(L.s.transposed, win_count(s, w))
            wait(act, L.s.pv_done, win_count(s, w - 2))
            nc.scalar.copy(probsT[w % 2][:, :], ps_probsT[w % 2][:, 0:NP * 128]).then_inc(L.s.probsT_sb, 1)

        def act_heads(act, L, s, w):
            act.wait_ge(L.s.pv_done, win_count(s, w))
            if L.wide:
                nc.scalar.copy(heads1[parity(s)][:, :, w * WT:(w + 1) * WT],
                               ps_heads[:, 0:NP * WT].rearrange("r (p q) -> r p q", p=NP)).then_inc(L.s.heads_sb, 1)
            else:
                nc.scalar.copy(heads0[parity(s)][0:C, :], ps_heads[0:C, 0:T]).then_inc(L.s.heads_sb, 1)

        def act_out(act, L, s):
            act.wait_ge(L.s.out_ready, s + 1)
            wait(act, L.s.residual, s * L.adds)
            nc.scalar.activation(y_attn[:, :], ps_mix[0:C, 0:T], ACT.Identity,
                                 bias=(p1_b if L.wide else p0_b)[:, 0:1]).then_inc(L.s.y_ready, 1)

        def evac_q(eng, L, s, i, j, slot):
            par = parity(s)
            b, _ = bank_of(L, par, i)
            if L.wide:
                src, dst = by_window(ps_qkv[b][:, 0:T]), q1[par][:, j, :, slot, :]
                lo = CONSTS["qmask1"][0] + slot
                scale = cst[:, lo:lo + 1]
                if eng == "act":
                    return nc.scalar.activation(dst, src, ACT.Copy, scale=scale)
                return nc.vector.tensor_scalar(dst, src, scale, None, ALU.mult)
            src, dst = by_window(ps_qkv[b][:, 0:T]), q0[par][:, :, slot, :]
            lo = CONSTS["qmask0"][0] + slot
            scale, bias = cst[:, lo:lo + 1], b0_q[:, slot:slot + 1]
            if eng == "act":
                return nc.scalar.activation(dst, src, ACT.Identity, scale=scale, bias=bias)
            return nc.vector.tensor_scalar(dst, src, scale, bias, ALU.mult, ALU.add)

        def evac_k(eng, L, s, i, j, u):
            par = parity(s)
            b, _ = bank_of(L, par, i)
            rows = slice(u * 64, u * 64 + 64)
            src = ps_qkv[b][rows, T:2 * T]
            if L.wide:
                dst = k1[par][rows, u, j, 0:T]
                return nc.scalar.copy(dst, src) if eng == "act" else nc.vector.tensor_copy(dst, src)
            return nc.vector.tensor_scalar(k0[par][rows, u, 0:T], src, b0_qk[rows, 1:2], None, ALU.add)

        def evac_v(eng, L, s, i, j, odd, u):
            par = parity(s)
            b, _ = bank_of(L, par, i)
            src_rows, rows = slice(odd * WT, (odd + 1) * WT), slice(u * WT, (u + 1) * WT)
            if L.wide:
                src = ps_qkv[b][src_rows, 0:INNER].rearrange("k (p u h d) -> k u p h d", p=NP, u=NU, h=NH)[:, u]
                w = 2 * j + odd
                dst = v1[par][rows, w * NP:(w + 1) * NP, :, u * HD1:(u + 1) * HD1]
                return nc.scalar.copy(dst, src) if eng == "act" else nc.vector.tensor_copy(dst, src)
            def heads_of_u(ap):
                return ap.rearrange("k (g u h d) -> k u g h d", u=NU, h=NH, d=HD0)[:, u]
            n = 2 * NP
            dst = v0[par][rows, odd * n:(odd + 1) * n, :, :].rearrange("k g h e -> k g (h e)")[:, :, u * HD0:u * HD0 + 56] \
                .rearrange("k g (a d) -> k g a d", d=HD0)[:, :, 0:7:6, :]
            return nc.vector.tensor_tensor(dst, heads_of_u(ps_qkv[b][src_rows, 0:2 * C]), heads_of_u(b0_v[src_rows, :]), ALU.add)

        def evacuate(eng, who, L, s, i, first=0, end=99):
            kind, j, engine, _ = qkv_plan(L)[i]
            if engine != who:
                return
            if kind == "v":
                todo = [lambda o=o, u=u: evac_v(who, L, s, i, j, o, u) for o in range(2) for u in range(NU)]
            else:
                todo = []
                if kind != "k":
                    todo += [lambda h=h: evac_q(who, L, s, i, j, h) for h in range(L.slots)]
                if kind != "q":
                    todo += [lambda u=u: evac_k(who, L, s, i, j, u) for u in range(NU)]
            if first == 0 and kind == "v":
                eng.wait_ge(L.s.v_ready, s * L.v_uses + (j + 1))
                wait(eng, L.s.pv_done, s * NW - NW)
            elif first == 0:
                eng.wait_ge(L.s.qk_ready, s * L.qk_uses + (i + 1))
                wait(eng, L.s.scores_ready, s * NW - NW)
            for one in todo[first:end]:
                one().then_inc(evac_sem(L, parity(s), i), 1)

        def evacuate_step(eng, who, L, s, w, nxt, nxt2):
            for ahead, i, first, end in L.evacs_at[w]:
                if nxt2 if ahead == 2 else nxt:
                    evacuate(eng, who, L, moved(s, ahead), i, first, end)

        def dve_scores(dve, L, s, w):
            dve.wait_ge(L.s.scores_ready, win_count(s, w))
            wait(dve, L.s.transposed, win_count(s, w - 4))
            if isinstance(s, int) and s == 0 and L.n:
                dve.wait_ge(L0.s.transposed, win_count(B - 1, w))
            if L.wide:
                b = bias1[:, w, :].unsqueeze(1).broadcast_to([128, NP * NU, WT])
            else:
                b = bias0[:, :, :]
            nc.vector.tensor_tensor(probs[w][:, :, :], ps_scores[w % 2][:, 0:NP * NU * WT].rearrange("p (g k) -> p g k", k=WT),
                                    b, ALU.add).then_inc(L.s.biased, 1)
            dve.wait_ge(L.s.biased, win_count(s, w))
            nc.vector.tensor_reduce(row_max[w][:, :], probs[w][:, :, :], AX.X, ALU.max).then_inc(L.s.maxed, 1)

        def dve_sum(dve, L, s, w):
            dve.wait_ge(L.s.exped, win_count(s, w))
            nc.vector.tensor_reduce(row_sum[w][:, :], probs[w][:, :, :], AX.X, ALU.add).then_inc(L.s.summed, 1)
            dve.wait_ge(L.s.summed, win_count(s, w))
            nc.vector.reciprocal(inv_sum[w][:, :], row_sum[w][:, :]).then_inc(L.s.inverted, 1)

        def dve_new_x(dve, L, s):
            dve.wait_ge(L.s.residual, s * L.adds + L.adds)
            dve_stats(dve, L.n + 1, s)

        def dve_norm(dve, L, s):
            if isinstance(s, int) and s < 2 and L.n:
                dve.wait_ge(L0.s.v_ready, (B - 1 + s) * L0.v_uses)
            wait(dve, L.s.v_ready, s * L.v_uses - L.v_uses)
            for w in range(NW):
                for of_image, of_tokens in window_pieces(L, w):
                    tokens = xn[parity(s)][0:C, w, :].rearrange("c (y x) -> c y x", x=WIN)
                    nc.vector.tensor_scalar(of_tokens(tokens), of_image(image(x_of(s))), gn_mean[:, bass.ds(s * 1, 1)],
                                            gn_rstd[:, bass.ds(s * 1, 1)], ALU.subtract, ALU.mult).then_inc(L.s.xn_ready, 1)

        def by_row(r):
            return r[:, :].unsqueeze(2).broadcast_to([128, NP * NU, WT])

        def pool_shift(pool, L, s, w):
            pool.wait_ge(L.s.maxed, win_count(s, w))
            nc.gpsimd.tensor_tensor(probs[w][:, :, :], probs[w][:, :, :], by_row(row_max[w]),
                                    ALU.subtract).then_inc(L.s.shifted, 1)

        def pool_scale(pool, L, s, w):
            pool.wait_ge(L.s.inverted, win_count(s, w))
            nc.gpsimd.tensor_tensor(probs[w][:, :, :], probs[w][:, :, :], by_row(inv_sum[w]),
                                    ALU.mult).then_inc(L.s.scaled, 1)

        def pool_residual(pool, L, s, half):
            parts = [(w, *part) for w in range(NW) for part in window_pieces(L, w)]
            n = len(parts) // 2
            if half == 0:
                pool.wait_ge(L.s.y_ready, s + 1)
            for w, of_image, of_tokens in parts[half * n:(half + 1) * n]:
                pool.wait_ge(gn_done, 2 * gn_count(L.n, 0))
                part = of_image(image(x_of(s)))
                nc.gpsimd.tensor_tensor(part, of_tokens(y_attn[:, w * WT:(w + 1) * WT].rearrange("c (y x) -> c y x", x=WIN)),
                                        part, ALU.add).then_inc(L.s.residual, 1)

        def at(s, w):
            return moved(s, w // NW), w % NW

        def uses(L, s, w, nxt, nxt2):
            ahead, i0, i1 = L.uses_at[w]
            return (moved(s, ahead), i0, i1) if (nxt2 if ahead == 2 else nxt) else (s, 0, 0)

        def pe_sample(pe, L, s, prev, nxt, nxt2):
            for w in range(NW):
                ahead = w < 1 or nxt
                if ahead:
                    pe_scores(pe, L, *at(s, w + 3), 0)
                pe_transpose(pe, L, s, w)
                if ahead:
                    pe_scores(pe, L, *at(s, w + 3), 1)
                if w >= 1 or prev:
                    pe_values(pe, L, *at(s, w - 1))
                if w == 1 and prev:
                    pe_out(pe, L, moved(s, -1))
                q = uses(L, s, w, nxt, nxt2)
                if q[2]:
                    pe_qkv(pe, L, *q)

        def act_sample(act, L, s, prev, nxt, nxt2):
            for w in range(NW):
                evacuate_step(act, "act", L, s, w, nxt, nxt2)
                if w < 2 or nxt:
                    act_exp(act, L, *at(s, w + 2))
                act_probsT(act, L, s, w)
                if (w >= 1 or prev) and (L.wide or w == 0):
                    act_heads(act, L, *at(s, w - 1))
                if w == 1 and prev:
                    act_out(act, L, moved(s, -1))

        def dve_sample(dve, L, s, prev, nxt, nxt2):
            for w in range(NW):
                if w == 1 and nxt2:
                    dve_norm(dve, L, moved(s, 2))
                if w < 2 or nxt:
                    dve_scores(dve, L, *at(s, w + 2))
                if w < 3 or nxt:
                    dve_sum(dve, L, *at(s, w + 1))
                evacuate_step(dve, "dve", L, s, w, nxt, nxt2)
                if w == 0 and prev == 2:
                    dve_new_x(dve, L, moved(s, -2))

        def pool_sample(pool, L, s, prev, nxt, nxt2):
            for w in range(NW):
                if w < 2 or nxt:
                    pool_shift(pool, L, *at(s, w + 2))
                if w < 3 or nxt:
                    pool_scale(pool, L, *at(s, w + 1))
                if w >= 2 and prev:
                    pool_residual(pool, L, moved(s, -1), w - 2)

        def attention_loop(eng, L, body, half_norm):
            body(eng, L, 0, 0, True, True)
            if half_norm:
                half_norm(eng, L.n, 1)
            body(eng, L, 1, 1, True, True)
            if eng is nc.vector:
                gn_ready(eng, L.n, 1)
            with eng.Fori(0, B // 2 - 2) as i:
                for par in range(2):
                    body(eng, L, Sample(i + 1, par), 2, True, True)
            if half_norm:
                half_norm(eng, L.n + 1, 0)
            body(eng, L, B - 2, 2, True, False)
            body(eng, L, B - 1, 2, False, False)

        def first_uses(L):
            return [(0, 0, L.qk_uses + L.v_uses), (1, 0, L.uses_at[3][2])]

        def pe_attention_norm(pe, layer, half):
            if half == 0:
                pe.wait_ge((L0, L1)[layer - 1].s.y_ready, B - 3)
            else:
                if layer:
                    pe.wait_ge(L0.s.y_ready, B)
            pe_group_norm(pe, layer, half)


        def pe_last_values(pe, L):
            pe_values(pe, L, B - 1, 3)

        def pe_first(pe, L, before):
            if before:
                pe_last_values(pe, before)
            (_, _, n), second = first_uses(L)
            pe_qkv(pe, L, 0, 0, L.qk_uses)
            if before:
                pe_out(pe, before, B - 1)
            for w in range(2):
                for half in range(2):
                    pe_scores(pe, L, 0, w, half)
            pe_qkv(pe, L, 0, L.qk_uses, n)
            pe_qkv(pe, L, *second)
            for half in range(2):
                pe_scores(pe, L, 0, 2, half)

        def evacuate_first(eng, who, L, s, i0, i1):
            for i in range(i0, i1):
                later = [first for ahead, use, first, _ in L.evacs_at[0] if use == i]
                evacuate(eng, who, L, s, i, 0, later[0] if s == 1 and later else 99)

        def act_first(act, L, before):
            if before:
                act_heads(act, before, B - 1, 3)
            evacuate_first(act, "act", L, 0, 0, L.qk_uses)
            if before:
                act_out(act, before, B - 1)
            act_exp(act, L, 0, 0)
            evacuate_first(act, "act", L, 0, L.qk_uses, L.qk_uses + L.v_uses)
            act_exp(act, L, 0, 1)
            evacuate_first(act, "act", L, *first_uses(L)[1])

        def dve_first(dve, L, before):
            gn_ready(dve, L.n, 0)
            dve_norm(dve, L, 0)
            evacuate_first(dve, "dve", L, 0, 0, L.qk_uses)
            dve_scores(dve, L, 0, 0)
            dve_norm(dve, L, 1)
            dve_scores(dve, L, 0, 1)
            evacuate_first(dve, "dve", L, 0, L.qk_uses, L.qk_uses + L.v_uses)
            dve_sum(dve, L, 0, 0)
            if before:
                dve_new_x(dve, before, B - 2)
            evacuate_first(dve, "dve", L, *first_uses(L)[1])
            if before:
                dve_new_x(dve, before, B - 1)

        def pool_first(pool, L, before):
            pool_shift(pool, L, 0, 0)
            if before:
                for half in range(2):
                    pool_residual(pool, before, B - 1, half)
            pool_shift(pool, L, 0, 1)
            pool_scale(pool, L, 0, 0)

        PAIRS = B // 2
        N2 = 2 * T

        def pair_loop(eng, body, after_first, before_last):
            body(eng, 0, 0, True, True)
            after_first(eng)
            body(eng, 1, 1, True, True)
            pair_loop_rest(eng, body, before_last)

        def pair_loop_rest(eng, body, before_last=None):
            with eng.Fori(0, PAIRS // 2 - 2) as i:
                for par in range(2):
                    body(eng, i * 2 + (2 + par), par, True, True)
            if before_last:
                before_last(eng)
            body(eng, PAIRS - 2, 0, True, False)
            body(eng, PAIRS - 1, 1, False, False)

        def nothing(eng):
            pass

        def x_pair(j):
            return x[:, bass.ds(j * N2, N2)]

        l2_norm, l2_tap, l2_pw, l2_y, l2_res = (sem("l2_" + n) for n in ("norm", "tap", "pw", "y", "res"))

        def act_pad(act, j, par):
            for k in range(2):
                s = j * 2 + k
                act.wait_ge(gn_done, 2 * gn_count(2, 0))
                nc.scalar.activation(pad[par][:, 1:SIDE + 1, k, 1:SIDE + 1], image(x_of(s)), ACT.Identity,
                                     bias=gn_shift[:, bass.ds(s, 1)], scale=gn_rstd[:, bass.ds(s, 1)]).then_inc(l2_norm, 1)

        def tap_of(par, t):
            rows = pad[par][:, :, :, :].rearrange("c y b x -> c (y b) x")
            return rows[:, t // 3 * 2:t // 3 * 2 + 2 * SIDE, t % 3:t % 3 + SIDE]

        DVE_TAPS = 9 - PE_TAPS

        def dve_depthwise(dve, j, par):
            dve.wait_ge(l2_norm, j * 2 + 2)
            wait(dve, l2_pw, j - 1)
            y = conv[par][:, :, :]
            for t in range(DVE_TAPS):
                if t == 0:
                    ins = nc.vector.tensor_scalar(y, tap_of(par, t), dw_u[:, 0:1], None, ALU.mult)
                else:
                    dve.wait_ge(l2_tap, j * DVE_TAPS + t)
                    ins = nc.vector.scalar_tensor_tensor(y, tap_of(par, t), dw_u[:, t:t + 1], y, ALU.mult, ALU.add)
                ins.then_inc(l2_tap, 1)

        def pe_pointwise(pe, j, par):
            pe.wait_ge(l2_norm, j * 2 + 2)
            wait(pe, l2_y, j - 1)
            o = bank[par][0:C, :].rearrange("c (y x) -> c y x", x=SIDE)
            for t in range(PE_TAPS):
                nc.tensor.matmul(o, tapT[:, t, :], tap_of(par, DVE_TAPS + t), start=(t == 0), stop=False)
            pe.wait_ge(l2_tap, j * DVE_TAPS + DVE_TAPS)
            nc.tensor.matmul(bank[par][0:C, :], pwT[:, :], conv[par][:, :, :].rearrange("c y x -> c (y x)"),
                             start=False, stop=True).then_inc(l2_pw, 1)

        def act_l2_out(act, j, par):
            act.wait_ge(l2_pw, j + 1)
            wait(act, l2_res, j - 1)
            nc.scalar.copy(y_out[par][:, :].rearrange("c (b y x) -> c y b x", b=2, x=SIDE),
                           bank[par][0:C, :].rearrange("c (y b x) -> c y b x", b=2, x=SIDE)).then_inc(l2_y, 1)

        def pool_l2_residual(pool, j, par):
            pool.wait_ge(l2_y, j + 1)
            pool.wait_ge(gn_done, 2 * gn_count(2, 0))
            nc.gpsimd.tensor_tensor(x_pair(j), y_out[par][:, :], x_pair(j), ALU.add).then_inc(l2_res, 1)

        def dve_l2_stats(dve, j):
            dve.wait_ge(l2_res, j + 1)
            dve_stats(dve, 3, j * 2, 2)

        def act_l2(act, j, par, nxt, nxt2):
            act_l2_out(act, j, par)
            if nxt2:
                act_pad(act, j + 2, par)

        def dve_l2(dve, j, par, nxt, nxt2):
            if nxt:
                dve_depthwise(dve, j + 1, 1 - par)
            if not (isinstance(j, int) and j == 0):
                dve_l2_stats(dve, j - 1)
            if not nxt:
                dve_l2_stats(dve, j)

        def pool_l2(pool, j, par, nxt, nxt2):
            pool_l2_residual(pool, j, par)

        def pe_l2(pe, j, par, nxt, nxt2):
            if nxt:
                pe_pointwise(pe, j + 1, 1 - par)

        l3 = {n: sem("l3_" + n) for n in ("norm", "spike_a0", "spike", "qkv", "relu", "round_a", "round",
                                          "turned", "turned_sb", "kv", "kv_step", "attn", "relu_a", "round_b",
                                          "spike_a", "proj", "y", "out")}
        stored = [sem(f"l3_stored{i}") for i in range(2)]
        ATTN_SCALE = float(np.float32(12 ** -0.5 * 2)) / 64

        def act_l3_norm(act, j, par):
            wait(act, l3["spike_a0"], j * 1)
            for k in range(2):
                s = j * 2 + k
                act.wait_ge(gn_done, 2 * gn_count(3, 0))
                nc.scalar.activation(xn3[:, k * T:(k + 1) * T], x_of(s), ACT.Relu, bias=gn_shift[:, bass.ds(s, 1)],
                                     scale=gn_rstd[:, bass.ds(s, 1)]).then_inc(l3["norm"], 1)

        def dve_l3_spike(dve, j, par):
            dve.wait_ge(l3["norm"], j * 2 + 2)
            nc.vector.tensor_scalar(rounded[:, :], xn3[:, :], 4.0, ROUND, ALU.min, ALU.add).then_inc(l3["spike_a0"], 1)
            dve.wait_ge(l3["spike_a0"], j + 1)
            wait(dve, l3["qkv"], j * 3)
            nc.vector.tensor_scalar(spike_in[0:C, :], rounded[:, :], ROUND, None, ALU.subtract).then_inc(l3["spike"], 1)

        def pe_l3_qkv(pe, j, par):
            pe.wait_ge(l3["spike"], j + 1)
            wait(pe, l3["relu"], j * 3)
            if isinstance(j, int) and j == 0:
                pe.wait_ge(l2_y, PAIRS)
            for i in range(3):
                for part in range(3):
                    last = nc.tensor.matmul(bank[i][0:C, :], w3_parts[:, part, i * C:(i + 1) * C], spike_in[:, :],
                                            start=(part == 0), stop=(part == 2))
                last.then_inc(l3["qkv"], 1)

        def act_l3_relu(act, j, par):
            for i in range(3):
                act.wait_ge(l3["qkv"], j * 3 + (i + 1))
                if i == 0:
                    wait(act, l3["round"], j * 3 - 3)
                nc.scalar.activation(relu3[par][:, i, :], bank[i][0:C, :], ACT.Relu, bias=bn_b[:, i:i + 1],
                                     scale=bn_s4[:, i:i + 1]).then_inc(l3["relu"], 1)

        def dve_l3_round(dve, j, par):
            for i in range(3):
                dve.wait_ge(l3["relu"], j * 3 + (i + 1))
                nc.vector.tensor_scalar(relu3[par][:, i, :], relu3[par][:, i, :], 4.0, ROUND, ALU.min, ALU.add).then_inc(l3["round_a"], 1)
                dve.wait_ge(l3["round_a"], j * 3 + (i + 1))
                if i == 0:
                    wait(dve, l3["attn"], j - 1)
                nc.vector.tensor_scalar(qkv3[par][:, i, :], relu3[par][:, i, :], ROUND, None, ALU.subtract).then_inc(l3["round"], 1)

        turned = bank[3][:, :].bitcast(BF16)[:, 0:8 * C].rearrange("t (k b c) -> t k b c", k=2, c=C)

        def pe_l3_turn(pe, j, par):
            pe.wait_ge(l3["round"], j * 3 + 3)
            wait(pe, l3["turned_sb"], j)
            for k in range(2):
                for b in range(4):
                    last = nc.tensor.transpose(turned[:, k, b, :], qkv3[par][:, 1 + k, b * 128:(b + 1) * 128], ident_b[:, :])
            last.then_inc(l3["turned"], 1)

        def act_l3_turn(act, j, par):
            act.wait_ge(l3["turned"], j + 1)
            wait(act, l3["kv"], j)
            nc.scalar.copy(kvT[:, :, :, :], turned).then_inc(l3["turned_sb"], 1)

        def pe_l3_kv(pe, j, par):
            pe.wait_ge(l3["turned_sb"], j + 1)
            wait(pe, l3["kv_step"], j * 4)
            for b in range(4):
                last = nc.tensor.matmul(bank[4][0:C, b // 2 * C:(b // 2 + 1) * C], kvT[:, 0, b, :], kvT[:, 1, b, :],
                                        start=(b % 2 == 0), stop=(b % 2 == 1))
            last.then_inc(l3["kv"], 1)

        def dve_l3_kv(dve, j, par):
            dve.wait_ge(l3["kv"], j + 1)
            n = [0]

            def step(ins):
                n[0] += 1
                ins.then_inc(l3["kv_step"], 1)
                dve.wait_ge(l3["kv_step"], j * 4 + n[0])

            step(nc.vector.tensor_tensor(kv[:, :, :], bank[4][0:C, 0:2 * C].rearrange("d (b e) -> d b e", b=2),
                                         const("head_blocks", C).unsqueeze(1).broadcast_to([C, 2, C]), ALU.mult))
            wait(dve, l3["attn"], j)
            step(nc.vector.tensor_copy(kv_parts[:, 0, :, :], kv[:, :, :]))
            step(nc.vector.tensor_tensor(kv_lo[:, :, :], kv[:, :, :], kv_parts[:, 0, :, :], ALU.subtract))
            nc.vector.tensor_copy(kv_parts[:, 1, :, :], kv_lo[:, :, :]).then_inc(l3["kv_step"], 1)

        def pe_l3_attn(pe, j, par):
            pe.wait_ge(l3["kv_step"], j * 4 + 4)
            wait(pe, l3["relu_a"], j)
            for b in range(2):
                for part in range(2):
                    last = nc.tensor.matmul(bank[5][0:C, b * T:(b + 1) * T], kv_parts[:, part, b, :],
                                            qkv3[par][:, 0, b * T:(b + 1) * T], start=(part == 0), stop=(part == 1))
            last.then_inc(l3["attn"], 1)

        def act_l3_attn(act, j, par):
            act.wait_ge(l3["attn"], j + 1)
            wait(act, l3["round_b"], j)
            nc.scalar.activation(relu_a[:, :], bank[5][0:C, :], ACT.Relu, scale=ATTN_SCALE).then_inc(l3["relu_a"], 1)

        def dve_l3_attn(dve, j, par):
            dve.wait_ge(l3["relu_a"], j + 1)
            wait(dve, l3["spike_a"], j)
            nc.vector.tensor_scalar(rounded_a[:, :], relu_a[:, :], 4.0, ROUND, ALU.min, ALU.add).then_inc(l3["round_b"], 1)
            dve.wait_ge(l3["round_b"], j + 1)
            wait(dve, l3["proj"], j)
            nc.vector.tensor_scalar(spike_a[0:C, :], rounded_a[:, :], ROUND, None, ALU.subtract).then_inc(l3["spike_a"], 1)

        def pe_l3_proj(pe, j, par):
            pe.wait_ge(l3["spike_a"], j + 1)
            wait(pe, l3["y"], j)
            for part in range(3):
                last = nc.tensor.matmul(bank[6][0:C, :], w3_parts[:, part, 3 * C:4 * C], spike_a[:, :],
                                        start=(part == 0), stop=(part == 2))
            last.then_inc(l3["proj"], 1)

        def act_l3_proj(act, j, par):
            act.wait_ge(l3["proj"], j + 1)
            wait(act, l3["out"], j)
            nc.scalar.activation(y3[:, :], bank[6][0:C, :], ACT.Identity, bias=bn_b[:, 3:4],
                                 scale=bn_s4[:, 3:4]).then_inc(l3["y"], 1)

        def pool_l3_out(pool, j, par):
            pool.wait_ge(l3["y"], j + 1)
            wait(pool, stored[par], j * 8 - par * 8)
            pool.wait_ge(gn_done, 2 * gn_count(3, 0))
            nc.gpsimd.tensor_tensor(y_out[par][:, :], y3[:, :], x_pair(j), ALU.add).then_inc(l3["out"], 1)

        def sp_l3(sp, j, par, nxt, nxt2):
            sp.wait_ge(l3["out"], j + 1)
            sp.dma_start(out[bass.ds(j * 2, 2)].rearrange("b c h w -> c b (h w)"),
                         y_out[par][:, :].rearrange("c (b t) -> c b t", b=2)).then_inc(stored[par], 16)

        def pe_l3(pe, j, par, nxt, nxt2):
            pe_l3_attn(pe, j, par)
            if nxt:
                pe_l3_turn(pe, j + 1, 1 - par)
                pe_l3_kv(pe, j + 1, 1 - par)
            if nxt2:
                pe_l3_qkv(pe, j + 2, par)
            pe_l3_proj(pe, j, par)

        def act_l3(act, j, par, nxt, nxt2):
            if nxt2:
                act_l3_norm(act, j + 2, par)
            act_l3_attn(act, j, par)
            if nxt:
                act_l3_turn(act, j + 1, 1 - par)
            if nxt2:
                act_l3_relu(act, j + 2, par)
            act_l3_proj(act, j, par)

        def dve_l3(dve, j, par, nxt, nxt2):
            if nxt2:
                dve_l3_spike(dve, j + 2, par)
            dve_l3_attn(dve, j, par)
            if nxt:
                dve_l3_kv(dve, j + 1, 1 - par)
            if nxt2:
                dve_l3_round(dve, j + 2, par)

        def pool_l3(pool, j, par, nxt, nxt2):
            pool_l3_out(pool, j, par)

        @block.vector
        def _(dve):
            def norm_2(dve):
                dve_group_norm(dve, 2, 1)

            def norm_3(dve):
                dve_group_norm(dve, 3, 0)

            def norm_3b(dve):
                dve_group_norm(dve, 3, 1)

            dve_prepare(dve)
            dve_first(dve, L0, None)
            attention_loop(dve, L0, dve_sample, dve_group_norm)
            dve_first(dve, L1, L0)
            attention_loop(dve, L1, dve_sample, dve_group_norm)
            dve_depthwise(dve, 0, 0)
            dve_new_x(dve, L1, B - 2)
            dve_new_x(dve, L1, B - 1)
            pair_loop(dve, dve_l2, norm_2, norm_3)
            dve_l3_spike(dve, 0, 0)
            dve_l3_round(dve, 0, 0)
            dve_l3_spike(dve, 1, 1)
            dve_l3_kv(dve, 0, 0)
            dve_l3_round(dve, 1, 1)
            pair_loop(dve, dve_l3, norm_3b, nothing)

        @block.tensor
        def _(pe):
            def norm_2(pe):
                pe_group_norm(pe, 2, 1)

            def norm_3(pe):
                pe_group_norm(pe, 3, 0)

            def norm_3b(pe):
                pe_group_norm(pe, 3, 1)

            pe_prepare(pe)
            pe.wait_ge(dve_prep, done["all"])
            pe_first(pe, L0, None)
            attention_loop(pe, L0, pe_sample, pe_attention_norm)
            pe_first(pe, L1, L0)
            attention_loop(pe, L1, pe_sample, pe_attention_norm)
            pe_last_values(pe, L1)
            pe_out(pe, L1, B - 1)
            pe_pointwise(pe, 0, 0)
            pair_loop(pe, pe_l2, norm_2, norm_3)
            pe_l3_qkv(pe, 0, 0)
            pe_l3_turn(pe, 0, 0)
            pe_l3_kv(pe, 0, 0)
            pe_l3_qkv(pe, 1, 1)
            pair_loop(pe, pe_l3, norm_3b, nothing)

        @block.scalar
        def _(act):
            act.wait_ge(table_in, TABLE_IN)
            nc.scalar.activation(act_first_exp[:, :], cst[:, 0:1], ACT.Exp).then_inc(first_exp, 1)
            act.wait_ge(dve_prep, done["all"])
            act.wait_ge(late_in, LATE_IN)
            act_first(act, L0, None)
            attention_loop(act, L0, act_sample, None)
            act_first(act, L1, L0)
            attention_loop(act, L1, act_sample, None)
            act_heads(act, L1, B - 1, 3)
            act_out(act, L1, B - 1)
            act_pad(act, 0, 0)
            act_pad(act, 1, 1)
            act_l2(act, 0, 0, True, True)
            act_l2(act, 1, 1, True, True)
            gn_ready(act, 2, 1)
            pair_loop_rest(act, act_l2)
            act_l3_norm(act, 0, 0)
            act_l3_relu(act, 0, 0)
            act_l3_norm(act, 1, 1)
            act_l3_turn(act, 0, 0)
            act_l3_relu(act, 1, 1)
            act_l3(act, 0, 0, True, True)
            act_l3(act, 1, 1, True, True)
            gn_ready(act, 3, 1)
            pair_loop_rest(act, act_l3)

        @block.gpsimd
        def _(pool):
            def norm_2(pool):
                pool_group_norm(pool, 2, 1)

            def norm_3(pool):
                pool_group_norm(pool, 3, 0)

            def norm_3b(pool):
                pool_group_norm(pool, 3, 1)

            pool_prepare(pool)
            pool.wait_ge(table_in, TABLE_IN)
            pool_group_norm(pool, 0, 0)
            pool_prepare_late(pool)
            pool_first(pool, L0, None)
            attention_loop(pool, L0, pool_sample, pool_group_norm)
            pool_first(pool, L1, L0)
            attention_loop(pool, L1, pool_sample, pool_group_norm)
            for half in range(2):
                pool_residual(pool, L1, B - 1, half)
            pair_loop(pool, pool_l2, norm_2, norm_3)
            pair_loop(pool, pool_l3, norm_3b, nothing)

        @block.sync
        def _(sp):
            pair_loop(sp, sp_l3, nothing, nothing)
            for one in stored:
                sp.wait_ge(one, 16 * PAIRS // 2)


def kernel(**inputs):
    import concourse.bacc as bacc
    from concourse.bass_utils import run_bass_kernel_spmd

    nc = bacc.Bacc("TRN2", target_bir_lowering=False, num_devices=1)
    arrays, aps = {}, {}
    for name, value in [*inputs.items(), ("consts", constants())]:
        if name == "L1_conv_pos_emb":
            value = np.asarray(value)[::-1, ::-1]
        value = np.ascontiguousarray(value)
        arrays[f"in_{name}"] = value
        aps[name] = nc.dram_tensor(f"in_{name}", value.shape, mybir.dt.from_np(value.dtype), kind="ExternalInput").ap()
    out = nc.dram_tensor("out_0_dram", (B, C, SIDE, SIDE), F32, kind="ExternalOutput").ap()
    build(nc, aps, out)
    return run_bass_kernel_spmd(nc, [arrays], core_ids=[0]).results[0]["out_0_dram"]
```
